# Optimizing a Trainium2 kernel written in Bass

```python
import numpy as np
import jax
import jax.numpy as jnp

def _softmax(x, axis=-1):
    return jax.nn.softmax(x, axis=axis)

def _gelu(x):
    return jax.nn.gelu(x, approximate=True)

def _silu(x):
    return jax.nn.silu(x)

def _sigmoid(x):
    return jax.nn.sigmoid(x)

def _layernorm(x, axis=-1, eps=1e-05):
    m = jnp.mean(x, axis=axis, keepdims=True)
    v = jnp.var(x, axis=axis, keepdims=True)
    return (x - m) / jnp.sqrt(v + eps)

def _scatter_add(tgt, idx, src, axis=0):
    return tgt.at[idx].add(src)

def _segment_sum(src, seg, n):
    return jax.ops.segment_sum(src, seg, n)
kernel_name = 'mk_perceiver_d2_seqx_r4_443ced'

def setup_inputs(seed: int=0):
    np.random.seed(seed)
    _w = jnp.asarray

    def _rec_inputs():
        import jax
        import jax.numpy as jnp
        _rk = jax.random.key(seed)
        x = -0.0005207 + 1.001 * jax.random.normal(jax.random.fold_in(_rk, 1), (8, 64, 256), jnp.float32)
        _lenS = 64 - jax.random.randint(jax.random.fold_in(_rk, 7), (8,), 0, max(1, 64 // 4) + 1, jnp.int32)
        _lenS2 = 1024 - jax.random.randint(jax.random.fold_in(_rk, 8), (8,), 0, max(1, 1024 // 4) + 1, jnp.int32)
        _ctx_1024P = jax.random.normal(jax.random.fold_in(_rk, 11), (8, 16, 256), jnp.float32)
        _ctx_1024c = jax.random.dirichlet(jax.random.fold_in(_rk, 511), 0.3 * jnp.ones((16,), jnp.float32), (8, 1024))
        _ctx_1024t = jnp.einsum('bsk,bkd->bsd', _ctx_1024c, _ctx_1024P)
        _ctx_1024t = _ctx_1024t * jax.lax.rsqrt(jnp.mean(jnp.square(_ctx_1024t)) + 1e-12) * 0.953939
        ctx_1024 = -1.52775e-05 + 0.999936 * (_ctx_1024t + 0.3 * jax.random.normal(jax.random.fold_in(_rk, 611), (8, 1024, 256), jnp.float32))
        _validS = jnp.arange(64)[None, :] < _lenS[:, None]
        _validS2 = jnp.arange(1024)[None, :] < _lenS2[:, None]
        _causal = jnp.tril(jnp.ones((64, 64), dtype=bool))
        mask_BxS2_bf1 = jnp.ones((8, 1024), dtype=bool)
        return (x, ctx_1024, mask_BxS2_bf1)
    x, ctx_1024, mask_BxS2_bf1 = _rec_inputs()

    def _L0_xattn_setup():
        import jax, jax.numpy as jnp
        import numpy as np
        DIM = 256
        HEADS = 16
        DHEAD = 64
        INNER = HEADS * DHEAD
        EPS = 1e-05

        def layer_norm(x, g, b):
            mu = jnp.mean(x, axis=-1, keepdims=True)
            var = jnp.mean(jnp.square(x - mu), axis=-1, keepdims=True)
            return (x - mu) * jax.lax.rsqrt(var + EPS) * g + b

        def apply_rope(x, cos, sin):
            d2 = x.shape[-1] // 2
            x1, x2 = (x[..., :d2], x[..., d2:])
            return jnp.concatenate([x1 * cos - x2 * sin, x2 * cos + x1 * sin], axis=-1)
        key = jax.random.key(seed)
        ks = jax.random.split(key, 10)
        B, N, S = (8, 64, 1024)
        latents = jax.random.normal(ks[0], (B, N, DIM), dtype=jnp.float32)
        context = jax.random.normal(ks[1], (B, S, DIM), dtype=jnp.float32)
        cos = jax.random.uniform(ks[2], (S, DHEAD // 2), dtype=jnp.float32)
        sin = jax.random.uniform(ks[3], (S, DHEAD // 2), dtype=jnp.float32)
        init = lambda k, shp, fan_in: jax.random.normal(k, shp, dtype=jnp.float32) / np.sqrt(fan_in)
        return {'latents': latents, 'context': context, 'cos': cos, 'sin': sin, 'ln_lat_g': jnp.ones((DIM,), jnp.float32), 'ln_lat_b': jnp.zeros((DIM,), jnp.float32), 'ln_ctx_g': jnp.ones((DIM,), jnp.float32), 'ln_ctx_b': jnp.zeros((DIM,), jnp.float32), 'Wq': init(ks[4], (DIM, INNER), DIM), 'Wkv': init(ks[5], (DIM, 2 * INNER), DIM), 'Wo': init(ks[6], (INNER, DIM), INNER), 'bo': jnp.zeros((DIM,), jnp.float32)}
    _L0_xattn_all = _L0_xattn_setup()
    _L0_xattn_in = {k: v for k, v in _L0_xattn_all.items() if k in ('cos', 'sin', 'ln_lat_g', 'ln_lat_b', 'ln_ctx_g', 'ln_ctx_b', 'Wq', 'Wkv', 'Wo', 'bo')}
    del _L0_xattn_all

    def _L0_attn_setup():
        import jax, jax.numpy as jnp
        import numpy as np
        import math
        B, T, C = (2, 512, 256)
        H = 16
        HS = C // H
        NC = 2 * HS
        G = min(32, NC)
        LAMBDA_INIT = 0.8 - 0.6 * math.exp(-0.3 * (12 - 1))
        EPS = 1e-05

        def _heads(x, W, d):
            b, t, _ = x.shape
            return jnp.einsum('btc,oc->bto', x, W).reshape(b, t, H, d).transpose(0, 2, 1, 3)
        key = jax.random.key(seed)
        ks = jax.random.split(key, 12)
        s = 0.02
        return {'x': jax.random.normal(ks[0], (B, T, C), jnp.float32), 'Wq1': jax.random.normal(ks[1], (C, C), jnp.float32) * s, 'Wq2': jax.random.normal(ks[2], (C, C), jnp.float32) * s, 'Wk1': jax.random.normal(ks[3], (C, C), jnp.float32) * s, 'Wk2': jax.random.normal(ks[4], (C, C), jnp.float32) * s, 'Wv': jax.random.normal(ks[5], (2 * C, C), jnp.float32) * s, 'Wc': jax.random.normal(ks[6], (C, 2 * C), jnp.float32) * s, 'gn_w': jnp.ones((NC,), jnp.float32), 'gn_b': jnp.zeros((NC,), jnp.float32), 'gamma': jnp.ones((NC,), jnp.float32), 'lq1': jnp.full((H, 1, 1), 0.1, jnp.float32), 'lk1': jnp.full((H, 1, 1), 0.1, jnp.float32), 'lq2': jnp.full((H, 1, 1), 0.1, jnp.float32), 'lk2': jnp.full((H, 1, 1), 0.1, jnp.float32)}
    _L0_attn_all = _L0_attn_setup()
    _L0_attn_in = {k: v for k, v in _L0_attn_all.items() if k in ('Wq1', 'Wq2', 'Wk1', 'Wk2', 'Wv', 'Wc', 'gn_w', 'gn_b', 'gamma', 'lq1', 'lk1', 'lq2', 'lk2')}
    del _L0_attn_all

    def _L0_ffn_setup():
        import jax, jax.numpy as jnp
        import numpy as np
        D_IN, D_HID = (256, 1024)

        def _ternary(key, shape):
            return jax.random.randint(key, shape, -1, 2).astype(jnp.float32)

        def _tlin(x, w, s):
            return jnp.einsum('bsi,oi->bso', x, w) * s
        key = jax.random.key(seed)
        ks = jax.random.split(key, 12)
        inv = lambda fan: 1.0 / np.sqrt(fan).astype(np.float32)
        return {'x': jax.random.normal(ks[0], (4, 512, D_IN), dtype=jnp.float32), 'w1_w': _ternary(ks[1], (D_HID, D_IN)), 'w1_s': jax.random.uniform(ks[2], (D_HID,), dtype=jnp.float32) * inv(D_IN), 'w2_w': _ternary(ks[3], (D_HID, D_IN)), 'w2_s': jax.random.uniform(ks[4], (D_HID,), dtype=jnp.float32) * inv(D_IN), 'h1_w': _ternary(ks[5], (D_HID, D_HID)), 'h1_s': jax.random.uniform(ks[6], (D_HID,), dtype=jnp.float32) * inv(D_HID), 'h2_w': _ternary(ks[7], (D_HID, D_HID)), 'h2_s': jax.random.uniform(ks[8], (D_HID,), dtype=jnp.float32) * inv(D_HID), 'w3_w': _ternary(ks[9], (D_IN, D_HID)), 'w3_s': jax.random.uniform(ks[10], (D_IN,), dtype=jnp.float32) * inv(D_HID)}
    _L0_ffn_all = _L0_ffn_setup()
    _L0_ffn_in = {k: v for k, v in _L0_ffn_all.items() if k in ('w1_w', 'w1_s', 'w2_w', 'w2_s', 'h1_w', 'h1_s', 'h2_w', 'h2_s', 'w3_w', 'w3_s')}
    del _L0_ffn_all

    def _L1_xattn_setup():
        import jax, jax.numpy as jnp
        import numpy as np
        DIM = 256
        HEADS = 16
        DIM_HEAD = 64
        INNER = HEADS * DIM_HEAD
        EPS = 1e-05

        def layer_norm(x, gamma, beta):
            mu = jnp.mean(x, axis=-1, keepdims=True)
            var = jnp.var(x, axis=-1, keepdims=True)
            return (x - mu) * jax.lax.rsqrt(var + EPS) * gamma + beta
        key = jax.random.key(seed)
        ks = jax.random.split(key, 8)
        b, n, m = (8, 1024, 64)
        x = jax.random.normal(ks[0], (b, n, DIM), dtype=jnp.float32)
        latents = jax.random.normal(ks[1], (b, m, DIM), dtype=jnp.float32)
        mask = jnp.ones((b, n), dtype=bool)
        s = 0.02
        Wq = jax.random.normal(ks[2], (DIM, INNER), dtype=jnp.float32) * s
        Wkv = jax.random.normal(ks[3], (DIM, 2 * INNER), dtype=jnp.float32) * s
        Wout = jax.random.normal(ks[4], (INNER, DIM), dtype=jnp.float32) * s
        g_x = jnp.ones((DIM,), jnp.float32)
        b_x = jnp.zeros((DIM,), jnp.float32)
        g_l = jnp.ones((DIM,), jnp.float32)
        b_l = jnp.zeros((DIM,), jnp.float32)
        g_o = jnp.ones((DIM,), jnp.float32)
        b_o = jnp.zeros((DIM,), jnp.float32)
        return {'x': x, 'latents': latents, 'mask': mask, 'g_x': g_x, 'b_x': b_x, 'g_l': g_l, 'b_l': b_l, 'Wq': Wq, 'Wkv': Wkv, 'Wout': Wout, 'g_o': g_o, 'b_o': b_o}
    _L1_xattn_all = _L1_xattn_setup()
    _L1_xattn_in = {k: v for k, v in _L1_xattn_all.items() if k in ('g_x', 'b_x', 'g_l', 'b_l', 'Wq', 'Wkv', 'Wout', 'g_o', 'b_o')}
    del _L1_xattn_all

    def _L1_attn_setup():
        import jax, jax.numpy as jnp
        import numpy as np
        import math
        NUM_HEADS = 8
        EMB = 256
        HEAD_DIM = 128
        B, T = (1, 1024)

        def sinusoidal_pe(T, d, dtype=jnp.float32):
            pos = jnp.arange(T, dtype=dtype)[:, None]
            inv_freq = jnp.exp(-math.log(10000.0) * jnp.arange(0, d, 2, dtype=dtype) / d)
            ang = pos * inv_freq[None, :]
            pe = jnp.zeros((T, d), dtype=dtype)
            pe = pe.at[:, 0::2].set(jnp.sin(ang))
            pe = pe.at[:, 1::2].set(jnp.cos(ang))
            return pe
        key = jax.random.key(seed)
        ks = jax.random.split(key, 6)
        s = lambda fan_in: 1.0 / math.sqrt(fan_in)
        x = jax.random.normal(ks[0], (B, T, EMB), dtype=jnp.float32)
        Wq = jax.random.normal(ks[1], (EMB, NUM_HEADS * HEAD_DIM), dtype=jnp.float32) * s(EMB)
        bq = jax.random.normal(ks[2], (NUM_HEADS * HEAD_DIM,), dtype=jnp.float32) * s(EMB)
        Wkv = jax.random.normal(ks[3], (EMB, 2 * HEAD_DIM), dtype=jnp.float32) * s(EMB)
        bkv = jax.random.normal(ks[4], (2 * HEAD_DIM,), dtype=jnp.float32) * s(EMB)
        Wo = jax.random.normal(ks[5], (NUM_HEADS * HEAD_DIM, EMB), dtype=jnp.float32) * s(NUM_HEADS * HEAD_DIM)
        return {'x': x, 'Wq': Wq, 'bq': bq, 'Wkv': Wkv, 'bkv': bkv, 'Wo': Wo}
    _L1_attn_all = _L1_attn_setup()
    _L1_attn_in = {k: v for k, v in _L1_attn_all.items() if k in ('Wq', 'bq', 'Wkv', 'bkv', 'Wo')}
    del _L1_attn_all

    def _L1_ffn_setup():
        import jax, jax.numpy as jnp
        import numpy as np
        N_EXPERTS = 32
        TOP_K = 8
        N_GROUP = 4
        TOPK_GROUP = 2
        ROUTED_SCALING = 2.5

        def _gate(x, gate_w, gate_bias):
            T, E = (x.shape[0], gate_w.shape[0])
            logits = jnp.einsum('th,eh->te', x, gate_w)
            scores = jax.nn.sigmoid(logits)
            scores_choice = scores + gate_bias[None, :]
            grp = scores_choice.reshape(T, N_GROUP, E // N_GROUP)
            top2, _ = jax.lax.top_k(grp, 2)
            group_scores = top2.sum(-1)
            _, grp_idx = jax.lax.top_k(group_scores, TOPK_GROUP)
            group_mask = jax.nn.one_hot(grp_idx, N_GROUP, dtype=scores.dtype).sum(1)
            expert_mask = jnp.repeat(group_mask, E // N_GROUP, axis=1)
            masked = jnp.where(expert_mask > 0, scores_choice, 0.0)
            _, topk_idx = jax.lax.top_k(masked, TOP_K)
            topk_w = jnp.take_along_axis(scores, topk_idx, axis=1)
            topk_w = topk_w / (topk_w.sum(-1, keepdims=True) + 1e-20)
            topk_w = topk_w * ROUTED_SCALING
            return (topk_idx, topk_w)

        def _mlp(x, wg, wu, wd):
            return jnp.einsum('...i,hi->...h', jax.nn.silu(jnp.einsum('...h,ih->...i', x, wg)) * jnp.einsum('...h,ih->...i', x, wu), wd)
        key = jax.random.key(seed)
        ks = jax.random.split(key, 9)
        B, S, H, I = (2, 128, 256, 128)
        w = 0.02
        return {'hidden_states': jax.random.normal(ks[0], (B, S, H), jnp.float32), 'gate_w': jax.random.normal(ks[1], (N_EXPERTS, H), jnp.float32) * w, 'gate_bias': jax.random.normal(ks[2], (N_EXPERTS,), jnp.float32) * w, 'expert_gate': jax.random.normal(ks[3], (N_EXPERTS, I, H), jnp.float32) * w, 'expert_up': jax.random.normal(ks[4], (N_EXPERTS, I, H), jnp.float32) * w, 'expert_down': jax.random.normal(ks[5], (N_EXPERTS, H, I), jnp.float32) * w, 'shared_gate': jax.random.normal(ks[6], (2 * I, H), jnp.float32) * w, 'shared_up': jax.random.normal(ks[7], (2 * I, H), jnp.float32) * w, 'shared_down': jax.random.normal(ks[8], (H, 2 * I), jnp.float32) * w}
    _L1_ffn_all = _L1_ffn_setup()
    _L1_ffn_in = {k: v for k, v in _L1_ffn_all.items() if k in ('gate_w', 'gate_bias', 'expert_gate', 'expert_up', 'expert_down', 'shared_gate', 'shared_up', 'shared_down')}
    del _L1_ffn_all
    return {'x': x, 'ctx_1024': ctx_1024, 'mask_BxS2_bf1': mask_BxS2_bf1, 'L0_xattn_cos': _L0_xattn_in['cos'], 'L0_xattn_sin': _L0_xattn_in['sin'], 'L0_xattn_ln_lat_g': _L0_xattn_in['ln_lat_g'], 'L0_xattn_ln_lat_b': _L0_xattn_in['ln_lat_b'], 'L0_xattn_ln_ctx_g': _L0_xattn_in['ln_ctx_g'], 'L0_xattn_ln_ctx_b': _L0_xattn_in['ln_ctx_b'], 'L0_xattn_Wq': _L0_xattn_in['Wq'], 'L0_xattn_Wkv': _L0_xattn_in['Wkv'], 'L0_xattn_Wo': _L0_xattn_in['Wo'], 'L0_xattn_bo': _L0_xattn_in['bo'], 'L0_attn_Wq1': _L0_attn_in['Wq1'], 'L0_attn_Wq2': _L0_attn_in['Wq2'], 'L0_attn_Wk1': _L0_attn_in['Wk1'], 'L0_attn_Wk2': _L0_attn_in['Wk2'], 'L0_attn_Wv': _L0_attn_in['Wv'], 'L0_attn_Wc': _L0_attn_in['Wc'], 'L0_attn_gn_w': _L0_attn_in['gn_w'], 'L0_attn_gn_b': _L0_attn_in['gn_b'], 'L0_attn_gamma': _L0_attn_in['gamma'], 'L0_attn_lq1': _L0_attn_in['lq1'], 'L0_attn_lk1': _L0_attn_in['lk1'], 'L0_attn_lq2': _L0_attn_in['lq2'], 'L0_attn_lk2': _L0_attn_in['lk2'], 'L0_ffn_w1_w': _L0_ffn_in['w1_w'], 'L0_ffn_w1_s': _L0_ffn_in['w1_s'], 'L0_ffn_w2_w': _L0_ffn_in['w2_w'], 'L0_ffn_w2_s': _L0_ffn_in['w2_s'], 'L0_ffn_h1_w': _L0_ffn_in['h1_w'], 'L0_ffn_h1_s': _L0_ffn_in['h1_s'], 'L0_ffn_h2_w': _L0_ffn_in['h2_w'], 'L0_ffn_h2_s': _L0_ffn_in['h2_s'], 'L0_ffn_w3_w': _L0_ffn_in['w3_w'], 'L0_ffn_w3_s': _L0_ffn_in['w3_s'], 'L1_xattn_g_x': _L1_xattn_in['g_x'], 'L1_xattn_b_x': _L1_xattn_in['b_x'], 'L1_xattn_g_l': _L1_xattn_in['g_l'], 'L1_xattn_b_l': _L1_xattn_in['b_l'], 'L1_xattn_Wq': _L1_xattn_in['Wq'], 'L1_xattn_Wkv': _L1_xattn_in['Wkv'], 'L1_xattn_Wout': _L1_xattn_in['Wout'], 'L1_xattn_g_o': _L1_xattn_in['g_o'], 'L1_xattn_b_o': _L1_xattn_in['b_o'], 'L1_attn_Wq': _L1_attn_in['Wq'], 'L1_attn_bq': _L1_attn_in['bq'], 'L1_attn_Wkv': _L1_attn_in['Wkv'], 'L1_attn_bkv': _L1_attn_in['bkv'], 'L1_attn_Wo': _L1_attn_in['Wo'], 'L1_ffn_gate_w': _L1_ffn_in['gate_w'], 'L1_ffn_gate_bias': _L1_ffn_in['gate_bias'], 'L1_ffn_expert_gate': _L1_ffn_in['expert_gate'], 'L1_ffn_expert_up': _L1_ffn_in['expert_up'], 'L1_ffn_expert_down': _L1_ffn_in['expert_down'], 'L1_ffn_shared_gate': _L1_ffn_in['shared_gate'], 'L1_ffn_shared_up': _L1_ffn_in['shared_up'], 'L1_ffn_shared_down': _L1_ffn_in['shared_down']}

def reference(x, ctx_1024, mask_BxS2_bf1, L0_xattn_cos, L0_xattn_sin, L0_xattn_ln_lat_g, L0_xattn_ln_lat_b, L0_xattn_ln_ctx_g, L0_xattn_ln_ctx_b, L0_xattn_Wq, L0_xattn_Wkv, L0_xattn_Wo, L0_xattn_bo, L0_attn_Wq1, L0_attn_Wq2, L0_attn_Wk1, L0_attn_Wk2, L0_attn_Wv, L0_attn_Wc, L0_attn_gn_w, L0_attn_gn_b, L0_attn_gamma, L0_attn_lq1, L0_attn_lk1, L0_attn_lq2, L0_attn_lk2, L0_ffn_w1_w, L0_ffn_w1_s, L0_ffn_w2_w, L0_ffn_w2_s, L0_ffn_h1_w, L0_ffn_h1_s, L0_ffn_h2_w, L0_ffn_h2_s, L0_ffn_w3_w, L0_ffn_w3_s, L1_xattn_g_x, L1_xattn_b_x, L1_xattn_g_l, L1_xattn_b_l, L1_xattn_Wq, L1_xattn_Wkv, L1_xattn_Wout, L1_xattn_g_o, L1_xattn_b_o, L1_attn_Wq, L1_attn_bq, L1_attn_Wkv, L1_attn_bkv, L1_attn_Wo, L1_ffn_gate_w, L1_ffn_gate_bias, L1_ffn_expert_gate, L1_ffn_expert_up, L1_ffn_expert_down, L1_ffn_shared_gate, L1_ffn_shared_up, L1_ffn_shared_down):
    import jax
    import jax.numpy as jnp

    def _L0_xattn_ref(latents, context, cos, sin, ln_lat_g, ln_lat_b, ln_ctx_g, ln_ctx_b, Wq, Wkv, Wo, bo):
        import jax, jax.numpy as jnp
        import numpy as np
        DIM = 256
        HEADS = 16
        DHEAD = 64
        INNER = HEADS * DHEAD
        EPS = 1e-05

        def layer_norm(x, g, b):
            mu = jnp.mean(x, axis=-1, keepdims=True)
            var = jnp.mean(jnp.square(x - mu), axis=-1, keepdims=True)
            return (x - mu) * jax.lax.rsqrt(var + EPS) * g + b

        def apply_rope(x, cos, sin):
            d2 = x.shape[-1] // 2
            x1, x2 = (x[..., :d2], x[..., d2:])
            return jnp.concatenate([x1 * cos - x2 * sin, x2 * cos + x1 * sin], axis=-1)
        b, n, _ = latents.shape
        s = context.shape[1]
        lat = layer_norm(latents, ln_lat_g, ln_lat_b)
        ctx = layer_norm(context, ln_ctx_g, ln_ctx_b)
        q = (lat @ Wq).reshape(b, n, HEADS, DHEAD).transpose(0, 2, 1, 3)
        kv = ctx @ Wkv
        k, v = jnp.split(kv, 2, axis=-1)
        k = k.reshape(b, s, HEADS, DHEAD).transpose(0, 2, 1, 3)
        v = v.reshape(b, s, HEADS, DHEAD).transpose(0, 2, 1, 3)
        k = apply_rope(k, cos[None, None], sin[None, None])
        scale = DHEAD ** (-0.5)
        attn = jnp.einsum('bhnd,bhsd->bhns', q, k) * scale
        attn = jnp.clip(attn, -11.0, 11.0)
        attn = jax.nn.softmax(attn, axis=-1)
        out = jnp.einsum('bhns,bhsd->bhnd', attn, v)
        out = out.transpose(0, 2, 1, 3).reshape(b, n, INNER)
        return out @ Wo + bo

    def _L0_attn_ref(x, Wq1, Wq2, Wk1, Wk2, Wv, Wc, gn_w, gn_b, gamma, lq1, lk1, lq2, lk2):
        import jax, jax.numpy as jnp
        import numpy as np
        import math
        B, T, C = (2, 512, 256)
        H = 16
        HS = C // H
        NC = 2 * HS
        G = min(32, NC)
        LAMBDA_INIT = 0.8 - 0.6 * math.exp(-0.3 * (12 - 1))
        EPS = 1e-05

        def _heads(x, W, d):
            b, t, _ = x.shape
            return jnp.einsum('btc,oc->bto', x, W).reshape(b, t, H, d).transpose(0, 2, 1, 3)
        b, t, c = x.shape
        q1 = _heads(x, Wq1, HS)
        q2 = _heads(x, Wq2, HS)
        k1 = _heads(x, Wk1, HS)
        k2 = _heads(x, Wk2, HS)
        v = _heads(x, Wv, 2 * HS)
        scale = 1.0 / math.sqrt(HS)
        mask = jnp.tril(jnp.ones((t, t), bool))
        neg = jnp.float32(-jnp.inf)
        att1 = jnp.einsum('bhqd,bhkd->bhqk', q1, k1) * scale
        att2 = jnp.einsum('bhqd,bhkd->bhqk', q2, k2) * scale
        att1 = jax.nn.softmax(jnp.where(mask, att1, neg), axis=-1)
        att2 = jax.nn.softmax(jnp.where(mask, att2, neg), axis=-1)
        lam1 = jax.nn.sigmoid(lq1 * lk1)
        lam2 = jax.nn.sigmoid(lq2 * lk2)
        lam = lam1 - lam2 + LAMBDA_INIT
        att = att1 - lam[None] * att2
        y = jnp.einsum('bhqk,bhkd->bhqd', att, v)
        yr = y.reshape(b, H, t, G, NC // G)
        mean = yr.mean(axis=(2, 4), keepdims=True)
        var = ((yr - mean) ** 2).mean(axis=(2, 4), keepdims=True)
        yn = ((yr - mean) * jax.lax.rsqrt(var + EPS)).reshape(b, H, t, NC)
        yn = yn * gn_w + gn_b
        yn = yn * gamma
        yn = yn * (1.0 - LAMBDA_INIT)
        y2 = yn.transpose(0, 2, 1, 3).reshape(b, t, 2 * c)
        out = jnp.einsum('btf,of->bto', y2, Wc)
        return out

    def _L0_ffn_ref(x, w1_w, w1_s, w2_w, w2_s, h1_w, h1_s, h2_w, h2_s, w3_w, w3_s):
        import jax, jax.numpy as jnp
        import numpy as np
        D_IN, D_HID = (256, 1024)

        def _ternary(key, shape):
            return jax.random.randint(key, shape, -1, 2).astype(jnp.float32)

        def _tlin(x, w, s):
            return jnp.einsum('bsi,oi->bso', x, w) * s
        h = jax.nn.silu(_tlin(x, w1_w, w1_s)) * _tlin(x, w2_w, w2_s)
        h = jax.nn.gelu(_tlin(h, h1_w, h1_s), approximate=False)
        h = jax.nn.gelu(_tlin(h, h2_w, h2_s), approximate=False)
        return _tlin(h, w3_w, w3_s)

    def _L1_xattn_ref(x, latents, mask, g_x, b_x, g_l, b_l, Wq, Wkv, Wout, g_o, b_o):
        import jax, jax.numpy as jnp
        import numpy as np
        DIM = 256
        HEADS = 16
        DIM_HEAD = 64
        INNER = HEADS * DIM_HEAD
        EPS = 1e-05

        def layer_norm(x, gamma, beta):
            mu = jnp.mean(x, axis=-1, keepdims=True)
            var = jnp.var(x, axis=-1, keepdims=True)
            return (x - mu) * jax.lax.rsqrt(var + EPS) * gamma + beta
        scale = DIM_HEAD ** (-0.5)
        xn = layer_norm(x, g_x, b_x)
        ln = layer_norm(latents, g_l, b_l)
        b, m = (ln.shape[0], ln.shape[1])
        q = jnp.einsum('bnd,de->bne', ln, Wq)
        kv_in = jnp.concatenate([xn, ln], axis=1)
        kv = jnp.einsum('bnd,de->bne', kv_in, Wkv)
        k, v = jnp.split(kv, 2, axis=-1)

        def split_heads(t):
            return t.reshape(t.shape[0], t.shape[1], HEADS, DIM_HEAD).transpose(0, 2, 1, 3)
        q, k, v = (split_heads(q), split_heads(k), split_heads(v))
        q = q * scale
        sim = jnp.einsum('bhid,bhjd->bhij', q, k)
        full_mask = jnp.concatenate([mask, jnp.ones((b, m), dtype=bool)], axis=1)
        max_neg = -jnp.finfo(sim.dtype).max
        sim = jnp.where(full_mask[:, None, None, :], sim, max_neg)
        attn = jax.nn.softmax(sim, axis=-1)
        out = jnp.einsum('bhij,bhjd->bhid', attn, v)
        out = out.transpose(0, 2, 1, 3).reshape(b, m, INNER)
        out = jnp.einsum('bne,ed->bnd', out, Wout)
        return layer_norm(out, g_o, b_o)

    def _L1_attn_ref(x, Wq, bq, Wkv, bkv, Wo):
        import jax, jax.numpy as jnp
        import numpy as np
        import math
        NUM_HEADS = 8
        EMB = 256
        HEAD_DIM = 128
        B, T = (1, 1024)

        def sinusoidal_pe(T, d, dtype=jnp.float32):
            pos = jnp.arange(T, dtype=dtype)[:, None]
            inv_freq = jnp.exp(-math.log(10000.0) * jnp.arange(0, d, 2, dtype=dtype) / d)
            ang = pos * inv_freq[None, :]
            pe = jnp.zeros((T, d), dtype=dtype)
            pe = pe.at[:, 0::2].set(jnp.sin(ang))
            pe = pe.at[:, 1::2].set(jnp.cos(ang))
            return pe
        Bsz, Tlen, E = x.shape
        q = (x @ Wq + bq).reshape(Bsz, Tlen, NUM_HEADS, HEAD_DIM)
        kv = x @ Wkv + bkv
        k, v = (kv[..., :HEAD_DIM], kv[..., HEAD_DIM:])
        q = jnp.transpose(q, (0, 2, 1, 3))
        pe = sinusoidal_pe(Tlen, HEAD_DIM, x.dtype)
        q = q + pe[None, None, :, :]
        k = k + pe[None, :, :]
        scale = 1.0 / math.sqrt(HEAD_DIM)
        scores = jnp.einsum('bhqd,bkd->bhqk', q, k) * scale
        causal = jnp.tril(jnp.ones((Tlen, Tlen), dtype=bool))
        scores = jnp.where(causal[None, None, :, :], scores, jnp.finfo(scores.dtype).min)
        probs = jax.nn.softmax(scores, axis=-1)
        attn = jnp.einsum('bhqk,bkd->bhqd', probs, v)
        out = jnp.transpose(attn, (0, 2, 1, 3)).reshape(Bsz, Tlen, NUM_HEADS * HEAD_DIM)
        return out @ Wo

    def _L1_ffn_ref(hidden_states, gate_w, gate_bias, expert_gate, expert_up, expert_down, shared_gate, shared_up, shared_down):
        import jax, jax.numpy as jnp
        import numpy as np
        N_EXPERTS = 32
        TOP_K = 8
        N_GROUP = 4
        TOPK_GROUP = 2
        ROUTED_SCALING = 2.5

        def _gate(x, gate_w, gate_bias):
            T, E = (x.shape[0], gate_w.shape[0])
            logits = jnp.einsum('th,eh->te', x, gate_w)
            scores = jax.nn.sigmoid(logits)
            scores_choice = scores + gate_bias[None, :]
            grp = scores_choice.reshape(T, N_GROUP, E // N_GROUP)
            top2, _ = jax.lax.top_k(grp, 2)
            group_scores = top2.sum(-1)
            _, grp_idx = jax.lax.top_k(group_scores, TOPK_GROUP)
            group_mask = jax.nn.one_hot(grp_idx, N_GROUP, dtype=scores.dtype).sum(1)
            expert_mask = jnp.repeat(group_mask, E // N_GROUP, axis=1)
            masked = jnp.where(expert_mask > 0, scores_choice, 0.0)
            _, topk_idx = jax.lax.top_k(masked, TOP_K)
            topk_w = jnp.take_along_axis(scores, topk_idx, axis=1)
            topk_w = topk_w / (topk_w.sum(-1, keepdims=True) + 1e-20)
            topk_w = topk_w * ROUTED_SCALING
            return (topk_idx, topk_w)

        def _mlp(x, wg, wu, wd):
            return jnp.einsum('...i,hi->...h', jax.nn.silu(jnp.einsum('...h,ih->...i', x, wg)) * jnp.einsum('...h,ih->...i', x, wu), wd)
        orig_shape = hidden_states.shape
        H = orig_shape[-1]
        residuals = hidden_states
        x = hidden_states.reshape(-1, H)
        topk_idx, topk_w = _gate(x, gate_w, gate_bias)
        g = jnp.einsum('th,eih->eti', x, expert_gate)
        u = jnp.einsum('th,eih->eti', x, expert_up)
        outs = jnp.einsum('eti,ehi->eth', jax.nn.silu(g) * u, expert_down)
        outs_t = jnp.transpose(outs, (1, 0, 2))
        gathered = jnp.take_along_axis(outs_t, topk_idx[:, :, None], axis=1)
        final = (gathered * topk_w[:, :, None]).sum(1)
        shared = _mlp(residuals, shared_gate, shared_up, shared_down)
        return final.reshape(orig_shape) + shared
    x = x + _L0_xattn_ref(_layernorm(x, axis=-1), ctx_1024, L0_xattn_cos, L0_xattn_sin, L0_xattn_ln_lat_g, L0_xattn_ln_lat_b, L0_xattn_ln_ctx_g, L0_xattn_ln_ctx_b, L0_xattn_Wq, L0_xattn_Wkv, L0_xattn_Wo, L0_xattn_bo)
    x = x + _L0_attn_ref(_layernorm(x, axis=-1), L0_attn_Wq1, L0_attn_Wq2, L0_attn_Wk1, L0_attn_Wk2, L0_attn_Wv, L0_attn_Wc, L0_attn_gn_w, L0_attn_gn_b, L0_attn_gamma, L0_attn_lq1, L0_attn_lk1, L0_attn_lq2, L0_attn_lk2)
    x = x + _L0_ffn_ref(_layernorm(x, axis=-1), L0_ffn_w1_w, L0_ffn_w1_s, L0_ffn_w2_w, L0_ffn_w2_s, L0_ffn_h1_w, L0_ffn_h1_s, L0_ffn_h2_w, L0_ffn_h2_s, L0_ffn_w3_w, L0_ffn_w3_s)
    x = x + _L1_xattn_ref(ctx_1024, _layernorm(x, axis=-1), mask_BxS2_bf1, L1_xattn_g_x, L1_xattn_b_x, L1_xattn_g_l, L1_xattn_b_l, L1_xattn_Wq, L1_xattn_Wkv, L1_xattn_Wout, L1_xattn_g_o, L1_xattn_b_o)
    x = x + _L1_attn_ref(_layernorm(x, axis=-1), L1_attn_Wq, L1_attn_bq, L1_attn_Wkv, L1_attn_bkv, L1_attn_Wo)
    x = x + _L1_ffn_ref(_layernorm(x, axis=-1), L1_ffn_gate_w, L1_ffn_gate_bias, L1_ffn_expert_gate, L1_ffn_expert_up, L1_ffn_expert_down, L1_ffn_shared_gate, L1_ffn_shared_up, L1_ffn_shared_down)
    return x

_drawn_inputs = setup_inputs


def setup_inputs(seed=0):
    import zlib

    import numpy as np

    out = dict(_drawn_inputs(seed))
    spreads = {'L0_xattn_ln_lat_g': (1.0, 0.2),
     'L0_xattn_ln_lat_b': (0.0, 0.1),
     'L0_xattn_ln_ctx_g': (1.0, 0.2),
     'L0_xattn_ln_ctx_b': (0.0, 0.1),
     'L0_xattn_bo': (0.0, 0.1),
     'L0_attn_gn_w': (1.0, 0.2),
     'L0_attn_gn_b': (0.0, 0.1),
     'L0_attn_gamma': (1.0, 0.2),
     'L0_attn_lq1': (0.10000000149011612, 0.2),
     'L0_attn_lk1': (0.10000000149011612, 0.2),
     'L0_attn_lq2': (0.10000000149011612, 0.2),
     'L0_attn_lk2': (0.10000000149011612, 0.2),
     'L1_xattn_g_x': (1.0, 0.2),
     'L1_xattn_b_x': (0.0, 0.1),
     'L1_xattn_g_l': (1.0, 0.2),
     'L1_xattn_b_l': (0.0, 0.1),
     'L1_xattn_g_o': (1.0, 0.2),
     'L1_xattn_b_o': (0.0, 0.1)}
    factors = {}
    for name, (base, spread) in spreads.items():
        noise = np.random.default_rng([zlib.crc32(name.encode()), seed]).standard_normal(out[name].shape)
        drawn = base * np.exp(spread * noise) if base else spread * noise
        out[name] = jnp.asarray(drawn.astype(out[name].dtype))
    for name, factor in factors.items():
        out[name] = (out[name] * factor).astype(out[name].dtype)
    return out
```

```python
from contextlib import ExitStack

import numpy as np

import concourse.bass as bass
from concourse import mybir

F32 = mybir.dt.float32
U8 = mybir.dt.uint8
ALU = mybir.AluOpType
ACT = mybir.ActivationFunctionType
AX = mybir.AxisListType

P = 128
B, N, S, D = 8, 64, 1024, 256
T = B * N
TT = T // P
KD = D // P
KT = S // P
H, DH = 16, 64
PAIRS = H * DH // P
STEPS = 2 * PAIRS
ITERS = B // 2
EPS = 1e-5
MASKED = -1e30
LAMBDA_INIT = 0.8 - 0.6 * float(np.exp(-0.3 * 11))
EXPERTS = 32
ROUTED_SCALING = 2.5


def Names(**named):
    return type("Names", (), named)()


class Chain:

    def __init__(self, engine, sem):
        self.engine, self.sem, self.base, self.n = engine, sem, 0, 0

    def __call__(self, instruction):
        instruction.then_inc(self.sem, 1)
        self.n += 1
        self.engine.wait_ge(self.sem, self.base + self.n)

    def enter(self, iteration, per_iteration):
        self.base = self.base + self.n + iteration * per_iteration
        self.n = 0

    def leave(self, before, per_iteration, iterations):
        assert self.n == per_iteration, (self.n, per_iteration)
        self.base, self.n = before + per_iteration * iterations, 0


class Scope:

    def __init__(self, nc, name):
        self.nc, self.name, self.stack, self.sems = nc, name, ExitStack(), []
        self.opened = ExitStack()

    def __enter__(self):
        return self

    def __exit__(self, *e):
        self.opened.__exit__(*e)
        if self.sems and not any(e):
            numbers = sorted(x.num for x in self.sems)
            with self.nc.Block() as block:
                @block.gpsimd
                def _(pool):
                    start = last = numbers[0]
                    for x in numbers[1:] + [None]:
                        if x != last + 1:
                            pool.sem_clear(range(start, last + 1))
                            start = x
                        last = x if x is not None else last
        return self.stack.__exit__(*e)

    def sb(self, name, shape, dt=F32):
        return self.stack.enter_context(self.nc.sbuf_tensor(f"{self.name}_{name}", shape, dt))

    def ps(self, name, shape, dt=F32):
        return self.stack.enter_context(self.nc.psum_tensor(f"{self.name}_{name}", shape, dt))

    def sem(self, name):
        self.sems.append(self.stack.enter_context(self.nc.semaphore(f"{self.name}_{name}")))
        return self.sems[-1]

    def block(self):
        return self.opened.enter_context(self.nc.Block())


def norm_tensors(sc, name, tiles):
    n = Names(**{k: sc.sb(f"{name}_{k}", [P, tiles])
                           for k in "sum dif sq dif2 sqe mean var std rstd".split()})
    n.stats = sc.sb(f"{name}_stats", [P, tiles, 6])
    n.var_ready, n.std_ready = sc.sem(f"{name}_var_ready"), sc.sem(f"{name}_std_ready")
    return n


def norm_stats(v, chain, n, src, tiles):
    for t in range(tiles):
        last = v.bn_stats(n.stats[:, t, :], src[:, t, 0:D])
    chain(last)
    even, odd = n.stats[:, :, 1], n.stats[:, :, 4]
    v.tensor_tensor(n.sum[:, :], even, odd, ALU.add)
    v.tensor_tensor(n.dif[:, :], even, odd, ALU.subtract)
    chain(v.tensor_tensor(n.sq[:, :], n.stats[:, :, 2], n.stats[:, :, 5], ALU.add))
    v.tensor_scalar(n.mean[:, :], n.sum[:, :], 0.5, None, ALU.mult)
    v.scalar_tensor_tensor(out=n.dif2[:, :], in0=n.dif[:, :], scalar=0.25, in1=n.dif[:, :], op0=ALU.mult, op1=ALU.mult)
    chain(v.tensor_scalar(n.sqe[:, :], n.sq[:, :], 1.0 / D, EPS, ALU.mult, ALU.add))
    v.tensor_tensor(n.var[:, :], n.sqe[:, :], n.dif2[:, :], ALU.add).then_inc(n.var_ready, 1)


def norm_root(a, n, count):
    a.wait_ge(n.var_ready, count)
    a.activation(n.std[:, :], n.var[:, :], ACT.Sqrt).then_inc(n.std_ready, 1)


def norm_apply(v, chain, n, count, src, dst, tiles):
    v.wait_ge(n.std_ready, count)
    chain(v.reciprocal(n.rstd[:, :], n.std[:, :]))
    for t in range(tiles):
        last = v.tensor_scalar(dst[:, t, 0:D], src[:, t, 0:D], n.mean[:, t:t + 1], n.rstd[:, t:t + 1],
                               ALU.subtract, ALU.mult)
    return last


def rows(ap):
    return ap.rearrange("(k p) n -> p k n", p=P)



def phase_setup(nc, g, i):
    with Scope(nc, "setup") as sc:
        loaded, zeroed, done = sc.sem("loaded"), sc.sem("zeroed"), sc.sem("done")
        block = sc.block()

        @block.sync
        def _(sp):
            sp.dma_start(g.x_tok[:, :, :], i.x.rearrange("(t p) d -> p t d", p=P)).then_inc(loaded, 16)
            sp.wait_ge(loaded, 16)

        @block.gpsimd
        def _(pool):
            pool.memset(g.ident[:, :], 0.0).then_inc(zeroed, 1)
            pool.memset(g.ones[:, :], 1.0)
            pool.wait_ge(zeroed, 1)
            pool.affine_select(out=g.ident[:, :], in_=g.ident[:, :], compare_op=ALU.not_equal, fill=1.0,
                               base=0, pattern=[[-1, P]], channel_multiplier=1).then_inc(done, 1)
            pool.wait_ge(done, 1)


def phase_queries(nc, g, i, layer, wq, gain, shift):
    rope = layer == 0
    with Scope(nc, f"q{layer}") as sc:
        y = sc.sb("y", [P, TT, D])
        z = sc.sb("z", [P, TT, D])
        gain_sb, shift_sb = sc.sb("gain", [P, D]), sc.sb("shift", [P, D])
        w = sc.sb("w", [P, KD, H * DH])
        zT = sc.sb("zT", [P, KD, T]) if rope else g.latT
        n = norm_tensors(sc, "n", TT)
        tps = sc.ps("tps", [P, KD, T])
        qps = sc.ps("qps", [P, 2, T])
        w_loaded, g_loaded = sc.sem("w_loaded"), sc.sem("g_loaded")
        chain_sem, zeroed = sc.sem("chain"), sc.sem("zeroed")
        latents, turned, turned_copied = sc.sem("latents"), sc.sem("turned"), sc.sem("turned_copied")
        projected, taken, taken_rot = sc.sem("projected"), sc.sem("taken"), sc.sem("taken_rot")
        block = sc.block()

        @block.sync
        def _(sp):
            sp.dma_start(gain_sb[:, :], gain).then_inc(g_loaded, 16)
            sp.dma_start(shift_sb[:, :], shift).then_inc(g_loaded, 16)
            sp.dma_start(w[:, :, :], rows(wq)).then_inc(w_loaded, 16)

        if not rope:
            @block.gpsimd
            def _(pool):
                pool.memset(g.lat_rows[:, :, :], 0.0).then_inc(zeroed, 1)
                pool.wait_ge(zeroed, 1)

        @block.vector
        def _(v):
            chain = Chain(v, chain_sem)
            norm_stats(v, chain, n, g.x_tok, TT)
            chain(norm_apply(v, chain, n, 1, g.x_tok, y, TT))
            norm_stats(v, chain, n, y, TT)
            chain(norm_apply(v, chain, n, 2, y, z, TT))
            v.wait_ge(g_loaded, 32)
            for t in range(TT):
                last = v.tensor_tensor(z[:, t, :], z[:, t, :], gain_sb[:, :], ALU.mult)
            chain(last)
            for t in range(TT):
                v.tensor_tensor(z[:, t, :], z[:, t, :], shift_sb[:, :], ALU.add).then_inc(latents, 1)
            if not rope:
                v.wait_ge(latents, TT)
                v.wait_ge(zeroed, 1)
                for b in range(B):
                    half = slice(N * (b % 2), N * (b % 2) + N)
                    last = v.tensor_copy(g.lat_rows[0:N, b, 0:D], z[half, b // 2, :])
                chain(last)
                v.memset(g.lat_rows[0:N, :, D:D + 2], 1.0)
            for p in range(PAIRS):
                v.wait_ge(projected, p + 1)
                v.tensor_scalar(g.qT[:, p, :], qps[:, p % 2, :], DH ** -0.5, None, ALU.mult).then_inc(taken, 1)

        @block.scalar
        def _(a):
            norm_root(a, n, 1)
            norm_root(a, n, 2)
            for k in range(KD):
                a.wait_ge(turned, k + 1)
                a.activation(zT[:, k, :], tps[:, k, :], ACT.Copy).then_inc(turned_copied, 1)
            if rope:
                for p in range(PAIRS):
                    a.wait_ge(taken, p + 1)
                    for c in range(4):
                        to, of = 32 * c, 32 * (c ^ 1)
                        sign = 1.0 if c % 2 == 0 else -1.0
                        last = a.activation(g.qrT[to:to + 32, p, :], qps[of:of + 32, p % 2, :], ACT.Copy,
                                            scale=sign * DH ** -0.5)
                    last.then_inc(taken_rot, 1)

        @block.tensor
        def _(pe):
            for k in range(KD):
                for t in range(TT):
                    if k == 0:
                        pe.wait_ge(latents, t + 1)
                    last = pe.transpose(tps[:, k, t * P:(t + 1) * P], z[:, t, k * P:(k + 1) * P], g.ident[:, :])
                last.then_inc(turned, 1)
            pe.wait_ge(turned_copied, KD)
            pe.wait_ge(w_loaded, 16)
            for p in range(PAIRS):
                if p >= 2:
                    pe.wait_ge(taken, p - 1)
                    if rope:
                        pe.wait_ge(taken_rot, p - 1)
                for k in range(KD):
                    last = pe.matmul(qps[:, p % 2, :], w[:, k, p * P:(p + 1) * P], zT[:, k, :],
                                     start=(k == 0), stop=(k == KD - 1))
                last.then_inc(projected, 1)


def query_blocks(pool, chain, dst, src, batch):
    view = src[:, :, :].rearrange("p h (b n) -> p h b n", n=N)
    for half in range(2):
        part = slice(DH * half, DH * half + DH)
        chain(pool.tensor_copy(dst[part, :, half * N:half * N + N], view[part, :, batch, :]))


def phase_cross0(nc, g, i):
    CLIP = 11.0
    with Scope(nc, "c0") as sc:
        wk, wv = sc.sb("wk", [P, KD, H * DH]), sc.sb("wv", [P, KD, H * DH])
        wo = sc.sb("wo", [P, PAIRS, D])
        cos, sin = sc.sb("cos", [P, S]), sc.sb("sin", [P, S])
        gain, shift, bo = sc.sb("gain", [P, D]), sc.sb("shift", [P, D]), sc.sb("bo", [P, D])
        raw = sc.sb("raw", [P, KT, D])
        ctx = [sc.sb(f"ctx{u}", [P, KT, D + 2]) for u in range(2)]
        ctxT = [sc.sb(f"ctxT{u}", [P, KD, S]) for u in range(2)]
        qd = [sc.sb(f"qd{u}", [P, PAIRS, P]) for u in range(2)]
        qrd = [sc.sb(f"qrd{u}", [P, PAIRS, P]) for u in range(2)]
        kc = [sc.sb(f"kc{u}", [P, S]) for u in range(2)]
        ks = [sc.sb(f"ks{u}", [P, S]) for u in range(2)]
        pr = [sc.sb(f"pr{u}", [P, KT, P]) for u in range(2)]
        inv = sc.sb("inv", [P, 2])
        un = [sc.sb(f"un{u}", [P, D]) for u in range(2)]
        uT = [sc.sb(f"uT{u}", [P, KD, P]) for u in range(2)]
        zT = sc.sb("zT", [P, PAIRS, T])
        n = norm_tensors(sc, "n", KT)
        kps = sc.ps("kps", [P, S])
        sps = sc.ps("sps", [P, KT, P])
        ups = sc.ps("ups", [P, 512])
        uTb, zb = sc.ps("uTb", [P, 512]), sc.ps("zb", [P, 512])
        tps = sc.ps("tps", [P, 4, P])
        uTps, zps = uTb[:, 0:KD * P].rearrange("p (k q) -> p k q", k=KD), zb[:, 0:P]
        s = Names(**{name: sc.sem(name) for name in (
            "wk_loaded wv_loaded tables_loaded wo_loaded ctx_loaded chain pool_chain zeroed applied affine "
            "blocks turned turned_copied keys roped scored clipped exped summed inverted normed sumsT "
            "sumsT_copied valued valued_copied out_done added").split()})
        zTb = zT[:, :, :].rearrange("p h (b n) -> p h b n", n=N)
        block = sc.block()

        @block.sync
        def _(sp):
            def load(batch):
                sp.dma_start(raw[:, :, :], i.ctx[batch].rearrange("(p k) d -> p k d", k=KT)).then_inc(s.ctx_loaded, 16)

            load(0)
            sp.dma_start(gain[:, :], i.l0_ctx_g).then_inc(s.tables_loaded, 16)
            sp.dma_start(shift[:, :], i.l0_ctx_b).then_inc(s.tables_loaded, 16)
            sp.dma_start(wk[:, :, :], rows(i.l0_wk)).then_inc(s.wk_loaded, 16)
            sp.dma_start(cos[:, :], i.l0_cos).then_inc(s.tables_loaded, 16)
            sp.dma_start(sin[:, :], i.l0_sin).then_inc(s.tables_loaded, 16)
            sp.dma_start(wv[:, :, :], rows(i.l0_wv)).then_inc(s.wv_loaded, 16)
            sp.dma_start(wo[:, :, :], rows(i.l0_wo)).then_inc(s.wo_loaded, 16)
            sp.dma_start(bo[:, :], i.l0_bo).then_inc(s.wo_loaded, 16)
            with sp.Fori(0, ITERS) as it:
                for u in range(2):
                    batch = sp.snap((it * 2 + u + 1) % B)
                    sp.wait_ge(s.applied, it * 2 + u + 1)
                    load(batch)
            sp.wait_ge(s.ctx_loaded, 16 * (B + 1))

        @block.gpsimd
        def _(pool):
            chain = Chain(pool, s.pool_chain)
            for u in range(2):
                pool.memset(qd[u][:, :, :], 0.0)
                pool.memset(qrd[u][:, :, :], 0.0)
                last = pool.memset(ctx[u][:, :, D:D + 2], 1.0)
            chain(last)

            def prepare(nth, batch, v):
                query_blocks(pool, chain, qd[v], g.qT, batch)
                query_blocks(pool, chain, qrd[v], g.qrT, batch)
                pool.sem_inc(s.blocks, 1)
                pool.wait_ge(s.applied, nth + 1)
                wide = [P, KT, D]
                chain(pool.tensor_tensor(ctx[v][:, :, 0:D], ctx[v][:, :, 0:D],
                                         gain[:, None, :].to_broadcast(wide), ALU.mult))
                chain(pool.tensor_tensor(ctx[v][:, :, 0:D], ctx[v][:, :, 0:D],
                                         shift[:, None, :].to_broadcast(wide), ALU.add))
                pool.sem_inc(s.affine, 1)

            pool.wait_ge(s.tables_loaded, 64)
            prepare(0, 0, 0)
            before, per = chain.n, 2 * 6
            with pool.Fori(0, ITERS) as it:
                chain.enter(it, per)
                for u in range(2):
                    pool.wait_ge(s.scored, it * STEPS + u * PAIRS + 1)
                    prepare(it * 2 + u + 1, (it * 2 + u + 1) % B, 1 - u)
                chain.leave(before, per, ITERS)

        @block.vector
        def _(v):
            chain = Chain(v, s.chain)

            def stats(nth):
                v.wait_ge(s.ctx_loaded, 16 * (nth + 1))
                norm_stats(v, chain, n, raw, KT)

            def apply(nth, u, batch):
                norm_apply(v, chain, n, nth + 1, raw, ctx[u], KT).then_inc(s.applied, 1)
                v.tensor_copy(g.ctx_mean[:, batch, :], n.mean[:, :])
                chain(v.tensor_copy(g.ctx_rstd[:, batch, :], n.rstd[:, :]))

            def rope(base, j):
                v.wait_ge(s.keys, base + j + 1)
                v.tensor_tensor(kc[j % 2][:, :], kps[:, :], cos[:, :], ALU.mult)
                v.tensor_tensor(ks[j % 2][:, :], kps[:, :], sin[:, :], ALU.mult).then_inc(s.roped, 1)

            def clip(base, j):
                v.wait_ge(s.scored, base + j + 1)
                v.tensor_scalar(pr[j % 2][:, :, :], sps[:, :, :], CLIP, -CLIP, ALU.min, ALU.max).then_inc(s.clipped, 1)

            def invert(base, j):
                v.wait_ge(s.summed, base + j + 1)
                if j >= 2:
                    v.wait_ge(s.normed, base + j - 1)
                v.reciprocal(inv[:, j % 2:j % 2 + 1], ups[:, D:D + 1]).then_inc(s.inverted, 1)

            stats(0)
            apply(0, 0, 0)
            v.wait_ge(s.tables_loaded, 64)
            before, per = chain.n, 2 * 5
            with v.Fori(0, ITERS) as it:
                chain.enter(it, per)
                base = it * STEPS
                rope(base, 0)
                for j in range(STEPS):
                    u, p = j // PAIRS, j % PAIRS
                    if j + 1 < STEPS:
                        rope(base, j + 1)
                    if j >= 1:
                        invert(base, j - 1)
                    clip(base, j)
                    if p == 1:
                        stats(it * 2 + u + 1)
                    if p == 2:
                        apply(it * 2 + u + 1, 1 - u, (it * 2 + u + 1) % B)
                invert(base, STEPS - 1)
                chain.leave(before, per, ITERS)
            v.wait_ge(s.wo_loaded, 32)
            for t in range(TT):
                v.wait_ge(s.out_done, t // 2 * 2 + 2)
                chain(v.tensor_tensor(g.x_tok[:, t, :], g.x_tok[:, t, :], kps[:, t * D:(t + 1) * D], ALU.add))
                v.tensor_tensor(g.x_tok[:, t, :], g.x_tok[:, t, :], bo[:, :], ALU.add)

        @block.scalar
        def _(a):
            def turned(v, first, r):
                a.wait_ge(s.turned, first + r + 1)
                k, half = r // 2, r % 2
                a.activation(ctxT[v][:, k, half * 512:half * 512 + 512], tps[:, :, :].rearrange("p a b -> p (a b)"),
                             ACT.Copy).then_inc(s.turned_copied, 1)

            def root(nth):
                norm_root(a, n, nth + 1)

            def exp(base, j):
                a.wait_ge(s.clipped, base + j + 1)
                a.activation(pr[j % 2][:, :, :], pr[j % 2][:, :, :], ACT.Exp).then_inc(s.exped, 1)

            def normalise(base, j):
                a.wait_ge(s.inverted, base + j + 1)
                if j >= 2:
                    a.wait_ge(s.sumsT, base + j - 1)
                a.activation(un[j % 2][:, :], ups[:, 0:D], ACT.Copy, scale=inv[:, j % 2:j % 2 + 1]).then_inc(s.normed, 1)

            def copy_sumsT(base, j):
                a.wait_ge(s.sumsT, base + j + 1)
                if j >= 2:
                    a.wait_ge(s.valued, base + j - 1)
                a.activation(uT[j % 2][:, :, :], uTps, ACT.Copy).then_inc(s.sumsT_copied, 1)

            def copy_values(base, j, batch, p):
                a.wait_ge(s.valued, base + j + 1)
                for half in range(2):
                    part = slice(DH * half, DH * half + DH)
                    last = a.activation(zTb[part, p, batch, :], zps[part, half * N:half * N + N], ACT.Copy)
                last.then_inc(s.valued_copied, 1)

            root(0)
            for r in range(4):
                turned(0, 0, r)
            with a.Fori(0, ITERS) as it:
                base = it * STEPS
                for j in range(STEPS + 3):
                    u, p = j // PAIRS, j % PAIRS
                    if j < STEPS:
                        exp(base, j)
                    if 0 <= j - 3:
                        copy_values(base, j - 3, it * 2 + (j - 3) // PAIRS, (j - 3) % PAIRS)
                    if 0 <= j - 1 < STEPS:
                        normalise(base, j - 1)
                    if 0 <= j - 2 < STEPS:
                        copy_sumsT(base, j - 2)
                    if j < STEPS and p == 1:
                        root(it * 2 + u + 1)
                    if j < STEPS and 3 <= p <= 6:
                        turned(1 - u, (it * 2 + u + 1) * 4, p - 3)

        @block.tensor
        def _(pe):
            def turn(nth, v, r):
                if r == 0:
                    pe.wait_ge(s.affine, nth + 1)
                if not (isinstance(nth, int) and nth == 0 and r == 0):
                    pe.wait_ge(s.turned_copied, nth * 4 + r)
                for c in range(4):
                    kt, k = (r % 2) * 4 + c, r // 2
                    last = pe.transpose(tps[:, c, :], ctx[v][:, kt, k * P:(k + 1) * P], g.ident[:, :])
                last.then_inc(s.turned, 1)

            def keys(base, j, nth):
                u, p = j // PAIRS, j % PAIRS
                if p == 0:
                    pe.wait_ge(s.turned_copied, (nth + 1) * 4)
                if j >= 1:
                    pe.wait_ge(s.roped, base + j)
                for half in range(2):
                    for k in range(KD):
                        cols = slice(half * 512, half * 512 + 512)
                        last = pe.matmul(kps[:, cols], wk[:, k, p * P:(p + 1) * P], ctxT[u][:, k, cols],
                                         start=(k == 0), stop=(k == KD - 1))
                last.then_inc(s.keys, 1)

            def scores(base, j, nth):
                u, p = j // PAIRS, j % PAIRS
                if p == 0:
                    pe.wait_ge(s.blocks, nth + 1)
                pe.wait_ge(s.roped, base + j + 1)
                if j >= 1:
                    pe.wait_ge(s.clipped, base + j)
                for kt in range(KT):
                    cols = slice(kt * P, kt * P + P)
                    pe.matmul(sps[:, kt, :], kc[j % 2][:, cols], qd[u][:, p, :], start=True, stop=False)
                    last = pe.matmul(sps[:, kt, :], ks[j % 2][:, cols], qrd[u][:, p, :], start=False, stop=True)
                last.then_inc(s.scored, 1)

            def sums(base, j):
                pe.wait_ge(s.exped, base + j + 1)
                if j >= 1:
                    pe.wait_ge(s.normed, base + j)
                for kt in range(KT):
                    last = pe.matmul(ups[:, 0:D + 1], pr[j % 2][:, kt, :], ctx[j // PAIRS][:, kt, 0:D + 1],
                                     start=(kt == 0), stop=(kt == KT - 1))
                last.then_inc(s.summed, 1)

            def turn_sums(base, j):
                pe.wait_ge(s.normed, base + j + 1)
                if j >= 1:
                    pe.wait_ge(s.sumsT_copied, base + j)
                for k in range(KD):
                    last = pe.transpose(uTps[:, k, :], un[j % 2][:, k * P:(k + 1) * P], g.ident[:, :])
                last.then_inc(s.sumsT, 1)

            def values(base, j):
                p = j % PAIRS
                pe.wait_ge(s.sumsT_copied, base + j + 1)
                if j >= 1:
                    pe.wait_ge(s.valued_copied, base + j)
                for k in range(KD):
                    last = pe.matmul(zps, wv[:, k, p * P:(p + 1) * P], uT[j % 2][:, k, :],
                                     start=(k == 0), stop=(k == KD - 1))
                last.then_inc(s.valued, 1)

            for r in range(4):
                turn(0, 0, r)
            pe.wait_ge(s.wk_loaded, 16)
            pe.wait_ge(s.wv_loaded, 16)
            with pe.Fori(0, ITERS) as it:
                base = it * STEPS
                keys(base, 0, it * 2)
                for j in range(STEPS + 3):
                    u, p = j // PAIRS, j % PAIRS
                    if j + 1 < STEPS:
                        keys(base, j + 1, it * 2 + (j + 1) // PAIRS)
                    if j < STEPS:
                        scores(base, j, it * 2 + u)
                    if 0 <= j - 1 < STEPS:
                        sums(base, j - 1)
                    if 0 <= j - 2 < STEPS:
                        turn_sums(base, j - 2)
                    if 0 <= j - 3 < STEPS:
                        values(base, j - 3)
                    if j < STEPS and 3 <= p <= 6:
                        turn(it * 2 + u + 1, 1 - u, p - 3)
            pe.wait_ge(s.wo_loaded, 32)
            pe.wait_ge(s.valued_copied, B * PAIRS)
            for t in range(TT):
                for p in range(PAIRS):
                    last = pe.matmul(kps[:, t * D:(t + 1) * D], zT[:, p, t * P:(t + 1) * P], wo[:, p, :],
                                     start=(p == 0), stop=(p == PAIRS - 1))
                last.then_inc(s.out_done, 1)


def turned_norm(sc, name):
    m = Names(y=sc.sb(f"{name}_y", [P, TT, D]), yT=sc.sb(f"{name}_yT", [P, KD, T]))
    m.n = norm_tensors(sc, name, TT)
    m.tps = [sc.ps(f"{name}_tps{k}", [P, T]) for k in range(KD)]
    m.normed, m.turned, m.copied = (sc.sem(f"{name}_{k}") for k in ("normed", "turned", "copied"))
    return m


def turned_norm_vector(v, chain, m, x):
    norm_stats(v, chain, m.n, x, TT)
    norm_apply(v, chain, m.n, 1, x, m.y, TT).then_inc(m.normed, 1)


def turned_norm_scalar(a, m):
    norm_root(a, m.n, 1)
    for k in range(KD):
        a.wait_ge(m.turned, k + 1)
        a.activation(m.yT[:, k, :], m.tps[k][:, :], ACT.Copy).then_inc(m.copied, 1)


def turned_norm_tensor(pe, g, m):
    pe.wait_ge(m.normed, 1)
    for k in range(KD):
        for t in range(TT):
            last = pe.transpose(m.tps[k][:, t * P:(t + 1) * P], m.y[:, t, k * P:(k + 1) * P], g.ident[:, :])
        last.then_inc(m.turned, 1)


def phase_attn0(nc, g, i):
    HS, HH = 16, 8
    UNITS = TT * 2
    C4 = 2 * D // P
    G4 = HH // 2
    with Scope(nc, "a0") as sc:
        wqk = sc.sb("wqk", [P, 4, KD, D])
        wv, wc = sc.sb("wv", [P, KD, 2 * D]), sc.sb("wc", [P, C4, D])
        causal, heads = sc.sb("causal", [P, N]), sc.sb("heads", [P, HH])
        lqk, lamp, lams, lam = sc.sb("lqk", [P, 4, H]), sc.sb("lamp", [P, 2, H]), sc.sb("lams", [P, 2, H]), sc.sb("lam", [P, H])
        chan, ga, gb = sc.sb("chan", [P, 3]), sc.sb("ga", [P, 2]), sc.sb("gb", [P, 1])
        m = turned_norm(sc, "m")
        yT2 = sc.sb("yT2", [P, KD, B, 2, N])
        qkT = sc.sb("qkT", [P, 4, 2, T])
        vd = sc.sb("vd", [P, B, PAIRS, 2 * 32])
        kd = [sc.sb(f"kd{u}", [P, 2, HH, N]) for u in range(4)]
        sm = [sc.sb(f"sm{u}", [P, 2, HH, N]) for u in range(2)]
        mx, su, rs = sc.sb("mx", [P, 2, HH]), sc.sb("su", [P, 2, HH]), sc.sb("rs", [P, 2, HH])
        att = [sc.sb(f"att{u}", [P, HH, N]) for u in range(2)]
        attT = [sc.sb(f"attT{u}", [P, G4, P]) for u in range(2)]
        y4, cen, sq = sc.sb("y4", [P, C4, T]), sc.sb("cen", [P, C4, T]), sc.sb("sq", [P, C4, T])
        gm, gv, gs, gr = (sc.sb(k, [P, C4 * B]) for k in ("gm", "gv", "gs", "gr"))
        sps = [sc.ps(f"sps{u}", [P, 2, HH, N]) for u in range(2)]
        aps, yps = sc.ps("aps", [P, G4, P]), sc.ps("yps", [P, 512])
        pps = [sps[0][:, a, :, :].rearrange("p h n -> p (h n)") for a in range(2)]
        s = Names(**{name: sc.sem(name) for name in (
            "w_loaded c_loaded wc_loaded twice chain pool_chain zeroed lam_in lam_out projected taken keyed keyed_pool scored shifted "
            "exped mixed attT attT_copied valued valued_copied sq_in sq_out gvar gstd gnormed out_done").split()})
        block = sc.block()

        @block.sync
        def _(sp):
            sp.dma_start(lqk[:, :, :], i.a0_lqk).then_inc(s.c_loaded, 16)
            sp.dma_start(chan[:, :], i.a0_chan).then_inc(s.c_loaded, 16)
            sp.dma_start(causal[:, :], i.causal).then_inc(s.c_loaded, 16)
            sp.dma_start(heads[:, :], i.heads).then_inc(s.c_loaded, 16)
            sp.dma_start(wqk[:, :, :, :], i.a0_wqk.rearrange("w (k p) n -> p w k n", p=P)).then_inc(s.w_loaded, 16)
            sp.dma_start(wv[:, :, :], rows(i.a0_wv)).then_inc(s.w_loaded, 16)
            sp.dma_start(wc[:, :, :], rows(i.a0_wc)).then_inc(s.wc_loaded, 16)

        def build_keys(engine, chain, unit, a):
            t, hh = unit // 2, unit % 2
            k = qkT[:, 2 + a, hh, t * P:(t + 1) * P].rearrange("p (b n) -> p b n", n=N)
            for b in range(2):
                last = engine.tensor_tensor(kd[unit % 2 * 2 + a][:, b, :, :], k[:, b, None, :].to_broadcast([P, HH, N]),
                                            heads[:, :, None].to_broadcast([P, HH, N]), ALU.mult)
            return last

        @block.gpsimd
        def _(pool):
            chain = Chain(pool, s.pool_chain)
            pool.memset(vd[:, :, :, :], 0.0).then_inc(s.zeroed, 1)
            pool.wait_ge(s.c_loaded, 64)
            pool.wait_ge(s.taken, 8)
            for unit in range(UNITS):
                if unit >= 2:
                    pool.wait_ge(s.scored, unit - 1)
                build_keys(pool, chain, unit, 1).then_inc(s.keyed_pool, 1)

        @block.vector
        def _(v):
            chain = Chain(v, s.chain)
            turned_norm_vector(v, chain, m, g.x_tok)
            v.wait_ge(s.c_loaded, 64)
            v.tensor_tensor(lamp[:, :, :], lqk[:, 0:2, :], lqk[:, 2:4, :], ALU.mult).then_inc(s.lam_in, 1)
            v.tensor_scalar(ga[:, :], chan[:, 0:2], chan[:, 2:3], 1.0 - LAMBDA_INIT, ALU.mult, ALU.mult)
            v.wait_ge(s.lam_out, 1)
            chain(v.tensor_tensor(lam[:, :], lams[:, 0, :], lams[:, 1, :], ALU.subtract))
            chain(v.tensor_scalar(lam[:, :], lam[:, :], LAMBDA_INIT, None, ALU.add))
            v.wait_ge(s.zeroed, 1)
            for b in range(B):
                v.wait_ge(s.projected, 8 + b + 1)
                src = pps[b % 2].rearrange("p (h c e) -> p h c e", c=2, e=32)
                for c in range(2):
                    part = slice(N * c, N * c + N)
                    last = v.tensor_copy(vd[part, b, :, 32 * c:32 * c + 32], src[part, :, c, :])
                last.then_inc(s.taken, 1)

            def shift(unit):
                v.wait_ge(s.scored, unit + 1)
                if unit >= 2:
                    v.wait_ge(s.mixed, unit - 1)
                to = sm[unit % 2]
                for a in range(2):
                    last = v.scalar_tensor_tensor(out=to[:, a, :, :], in0=sps[unit % 2][:, a, :, :], scalar=HS ** -0.5,
                                                  in1=causal[:, None, :].to_broadcast([P, HH, N]), op0=ALU.mult, op1=ALU.add)
                chain(last)
                chain(v.tensor_reduce(mx[:, :, :], to[:, :, :, :], AX.X, ALU.max))
                v.tensor_tensor(to[:, :, :, :], to[:, :, :, :], mx[:, :, :, None].to_broadcast([P, 2, HH, N]),
                                ALU.subtract).then_inc(s.shifted, 1)

            def mix(unit):
                hh = unit % 2
                v.wait_ge(s.exped, unit + 1)
                of = sm[unit % 2]
                chain(v.tensor_reduce(su[:, :, :], of[:, :, :, :], AX.X, ALU.add))
                chain(v.reciprocal(rs[:, :, :], su[:, :, :]))
                chain(v.tensor_tensor(rs[:, 1, :], rs[:, 1, :], lam[:, hh * HH:hh * HH + HH], ALU.mult))
                chain(v.tensor_tensor(of[:, :, :, :], of[:, :, :, :], rs[:, :, :, None].to_broadcast([P, 2, HH, N]), ALU.mult))
                if unit >= 2:
                    v.wait_ge(s.attT, unit - 1)
                v.tensor_tensor(att[unit % 2][:, :, :], of[:, 0, :, :], of[:, 1, :, :], ALU.subtract).then_inc(s.mixed, 1)

            for unit in range(UNITS + 1):
                if unit < UNITS:
                    if unit >= 2:
                        v.wait_ge(s.scored, unit - 1)
                    build_keys(v, chain, unit, 0).then_inc(s.keyed, 1)
                    shift(unit)
                if unit >= 1:
                    mix(unit - 1)
            v.wait_ge(s.valued_copied, UNITS)
            wide = [P, C4 * B, N]
            yv, cv, qv = (t[:, :, :].rearrange("p c (b n) -> p (c b) n", n=N) for t in (y4, cen, sq))
            chain(v.tensor_reduce(gm[:, :], yv, AX.X, ALU.add))
            chain(v.tensor_scalar(gm[:, :], gm[:, :], 1.0 / N, None, ALU.mult))
            v.tensor_tensor(cv, yv, gm[:, :, None].to_broadcast(wide), ALU.subtract).then_inc(s.sq_in, 1)
            v.wait_ge(s.sq_out, 1)
            chain(v.tensor_reduce(gv[:, :], qv, AX.X, ALU.add))
            v.tensor_scalar(gv[:, :], gv[:, :], 1.0 / N, EPS, ALU.mult, ALU.add).then_inc(s.gvar, 1)
            v.wait_ge(s.gstd, 1)
            chain(v.reciprocal(gr[:, :], gs[:, :]))
            chain(v.tensor_tensor(cv, cv, gr[:, :, None].to_broadcast(wide), ALU.mult))
            v.tensor_scalar(cen[:, :, :], cen[:, :, :], ga[:, 0:1], ga[:, 1:2], ALU.mult, ALU.add).then_inc(s.gnormed, 1)
            for t in range(TT):
                v.wait_ge(s.out_done, t // 2 * 2 + 2)
                v.tensor_tensor(g.x_tok[:, t, :], g.x_tok[:, t, :], pps[t // 2][:, t % 2 * D:t % 2 * D + D], ALU.add)

        @block.scalar
        def _(a):
            turned_norm_scalar(a, m)
            for k in range(KD):
                a.activation(yT2[:, k, :, :, :], m.tps[k][:, :].rearrange("p (b n) -> p b n", n=N)[:, :, None, :]
                             .to_broadcast([P, B, 2, N]), ACT.Copy).then_inc(s.twice, 1)
            for c in range(8):
                a.wait_ge(s.projected, c + 1)
                a.activation(qkT[:, c // 2, c % 2, :], pps[c % 2], ACT.Copy).then_inc(s.taken, 1)
            a.wait_ge(s.lam_in, 1)
            a.activation(lams[:, :, :], lamp[:, :, :], ACT.Sigmoid).then_inc(s.lam_out, 1)
            for unit in range(UNITS + 3):
                if unit < UNITS:
                    a.wait_ge(s.shifted, unit + 1)
                    a.activation(sm[unit % 2][:, :, :, :], sm[unit % 2][:, :, :, :], ACT.Exp).then_inc(s.exped, 1)
                if 0 <= unit - 2 < UNITS:
                    w = unit - 2
                    a.wait_ge(s.attT, w + 1)
                    if w >= 2:
                        a.wait_ge(s.valued, w - 1)
                    a.activation(attT[w % 2][:, :, :], aps[:, :, :], ACT.Copy).then_inc(s.attT_copied, 1)
                if 0 <= unit - 3 < UNITS:
                    w = unit - 3
                    t, hh = w // 2, w % 2
                    a.wait_ge(s.valued, w + 1)
                    a.activation(y4[:, 2 * hh:2 * hh + 2, t * P:(t + 1) * P],
                                 yps[:, 0:2 * P].rearrange("p (c q) -> p c q", c=2), ACT.Copy).then_inc(s.valued_copied, 1)
            a.wait_ge(s.sq_in, 1)
            a.activation(sq[:, :, :], cen[:, :, :], ACT.Square).then_inc(s.sq_out, 1)
            a.wait_ge(s.gvar, 1)
            a.activation(gs[:, :], gv[:, :], ACT.Sqrt).then_inc(s.gstd, 1)

        @block.tensor
        def _(pe):
            turned_norm_tensor(pe, g, m)
            pe.wait_ge(m.copied, KD)
            pe.wait_ge(s.w_loaded, 32)
            for c in range(8 + B):
                if c == 8:
                    pe.wait_ge(s.twice, KD)
                if c >= 2:
                    pe.wait_ge(s.taken, c - 1)
                for k in range(KD):
                    if c < 8:
                        left, right = wqk[:, c // 2, k, c % 2 * P:c % 2 * P + P], m.yT[:, k, :]
                    else:
                        b = c - 8
                        left = yT2[:, k, b, :, :].rearrange("p c n -> p (c n)")
                        right = wv[:, k, :]
                    last = pe.matmul(pps[c % 2], left, right, start=(k == 0), stop=(k == KD - 1))
                last.then_inc(s.projected, 1)
            pe.wait_ge(s.taken, 8 + B)
            for unit in range(UNITS + 3):
                if unit < UNITS:
                    t, hh = unit // 2, unit % 2
                    pe.wait_ge(s.keyed, unit + 1)
                    pe.wait_ge(s.keyed_pool, unit + 1)
                    if unit >= 2:
                        pe.wait_ge(s.shifted, unit - 1)
                    for a in range(2):
                        for b in range(2):
                            q = qkT[:, a, hh, t * P + b * N:t * P + b * N + N]
                            last = pe.matmul(sps[unit % 2][b * N:b * N + N, a, :, :].rearrange("p h n -> p (h n)"), q,
                                             kd[unit % 2 * 2 + a][:, b, :, :].rearrange("p h n -> p (h n)"),
                                             start=True, stop=True)
                    last.then_inc(s.scored, 1)
                if 0 <= unit - 2 < UNITS:
                    w = unit - 2
                    pe.wait_ge(s.mixed, w + 1)
                    if w >= 1:
                        pe.wait_ge(s.attT_copied, w)
                    for c in range(G4):
                        last = pe.transpose(aps[:, c, :], att[w % 2][:, 2 * c:2 * c + 2, :].rearrange("p h n -> p (h n)"),
                                            g.ident[:, :])
                    last.then_inc(s.attT, 1)
                if 0 <= unit - 3 < UNITS:
                    w = unit - 3
                    t, hh = w // 2, w % 2
                    pe.wait_ge(s.attT_copied, w + 1)
                    if w >= 1:
                        pe.wait_ge(s.valued_copied, w)
                    for c in range(G4):
                        for b in range(2):
                            to = c // 2 * P + b * N
                            last = pe.matmul(yps[c % 2 * N:c % 2 * N + N, to:to + N], vd[:, 2 * t + b, hh * G4 + c, :],
                                             attT[w % 2][:, c, b * N:b * N + N], start=True, stop=True)
                    last.then_inc(s.valued, 1)
            pe.wait_ge(s.gnormed, 1)
            pe.wait_ge(s.wc_loaded, 16)
            for t in range(TT):
                for c in range(C4):
                    last = pe.matmul(pps[t // 2][:, t % 2 * D:t % 2 * D + D], cen[:, c, t * P:(t + 1) * P], wc[:, c, :],
                                     start=(c == 0), stop=(c == C4 - 1))
                last.then_inc(s.out_done, 1)


def phase_ffn0(nc, g, i):
    F = 1024
    M = F // P
    with Scope(nc, "f0") as sc:
        w1, w2 = sc.sb("w1", [P, KD, F]), sc.sb("w2", [P, KD, F])
        h1, h2 = sc.sb("h1", [P, M, F]), sc.sb("h2", [P, M, F])
        w3, w3s = sc.sb("w3", [P, M, D]), sc.sb("w3s", [P, D])
        sca = sc.sb("sca", [P, 4, M])
        m = turned_norm(sc, "m")
        gate = [sc.sb(f"gate{u}", [P, T]) for u in range(2)]
        ha, hb = sc.sb("ha", [P, M, T]), sc.sb("hb", [P, M, T])
        t3 = [sc.sb(f"t3{u}", [P, D]) for u in range(2)]
        gp = [sc.ps(f"gp{u}", [P, T]) for u in range(3)]
        up = [sc.ps(f"up{u}", [P, T]) for u in range(3)]
        s = Names(**{name: sc.sem(name) for name in (
            "w_loaded h1_loaded h2_loaded w3_loaded chain gated upped silued hidden square gelued out_done").split()})
        block = sc.block()

        @block.sync
        def _(sp):
            sp.dma_start(w1[:, :, :], rows(i.f0_w1)).then_inc(s.w_loaded, 16)
            sp.dma_start(w2[:, :, :], rows(i.f0_w2)).then_inc(s.w_loaded, 16)
            sp.dma_start(sca[:, :, :], i.f0_scales).then_inc(s.w_loaded, 16)
            sp.dma_start(h1[:, :, :], rows(i.f0_h1)).then_inc(s.h1_loaded, 16)
            sp.dma_start(h2[:, :, :], rows(i.f0_h2)).then_inc(s.h2_loaded, 16)
            sp.dma_start(w3[:, :, :], rows(i.f0_w3)).then_inc(s.w3_loaded, 16)
            sp.dma_start(w3s[:, :], i.f0_w3s).then_inc(s.w3_loaded, 16)

        @block.vector
        def _(v):
            chain = Chain(v, s.chain)
            turned_norm_vector(v, chain, m, g.x_tok)
            v.wait_ge(s.w_loaded, 48)
            for c in range(M):
                v.wait_ge(s.upped, c + 1)
                v.wait_ge(s.silued, c + 1)
                v.scalar_tensor_tensor(out=ha[:, c, :], in0=up[c % 3][:, :], scalar=sca[:, 1, c:c + 1],
                                       in1=gate[c % 2][:, :], op0=ALU.mult, op1=ALU.mult).then_inc(s.hidden, 1)
            v.wait_ge(s.w3_loaded, 32)
            for t in range(TT):
                v.wait_ge(s.out_done, t + 1)
                chain(v.tensor_tensor(t3[t % 2][:, :], up[t % 2][:, 0:D], w3s[:, :], ALU.mult))
                v.tensor_tensor(g.x_tok[:, t, :], g.x_tok[:, t, :], t3[t % 2][:, :], ALU.add)
            v.sem_inc(s.chain, 1)

        @block.scalar
        def _(a):
            turned_norm_scalar(a, m)
            a.wait_ge(s.w_loaded, 48)
            for c in range(M):
                a.wait_ge(s.gated, c + 1)
                if c >= 2:
                    a.wait_ge(s.hidden, c - 1)
                a.activation(gate[c % 2][:, :], gp[c % 3][:, :], ACT.Silu, scale=sca[:, 0, c:c + 1]).then_inc(s.silued, 1)
            for layer in range(2):
                for c in range(M):
                    nth = layer * M + c
                    a.wait_ge(s.square, nth + 1)
                    a.activation((hb, ha)[layer][:, c, :], gp[nth % 3][:, :], ACT.Gelu,
                                 scale=sca[:, 2 + layer, c:c + 1]).then_inc(s.gelued, 1)

        @block.tensor
        def _(pe):
            turned_norm_tensor(pe, g, m)
            pe.wait_ge(m.copied, KD)
            pe.wait_ge(s.w_loaded, 48)
            for c in range(M):
                for w, ps, done, free in ((w1, gp, s.gated, s.silued), (w2, up, s.upped, s.hidden)):
                    if c >= 3:
                        pe.wait_ge(free, c - 2)
                    for k in range(KD):
                        last = pe.matmul(ps[c % 3][:, :], w[:, k, c * P:(c + 1) * P], m.yT[:, k, :],
                                         start=(k == 0), stop=(k == KD - 1))
                    last.then_inc(done, 1)
            pe.wait_ge(s.silued, M)
            for layer, (w, src, loaded, ready) in enumerate(((h1, ha, s.h1_loaded, s.hidden), (h2, hb, s.h2_loaded, s.gelued))):
                pe.wait_ge(loaded, 16)
                for c in range(M):
                    nth = layer * M + c
                    if nth >= 3:
                        pe.wait_ge(s.gelued, nth - 2)
                    for k in range(M):
                        if c == 0:
                            pe.wait_ge(ready, k + 1)
                        last = pe.matmul(gp[nth % 3][:, :], w[:, k, c * P:(c + 1) * P], src[:, k, :],
                                         start=(k == 0), stop=(k == M - 1))
                    last.then_inc(s.square, 1)
            pe.wait_ge(s.w3_loaded, 32)
            for t in range(TT):
                if t >= 2:
                    pe.wait_ge(s.chain, 4 + t - 1)
                for k in range(M):
                    if t == 0:
                        pe.wait_ge(s.gelued, M + k + 1)
                    last = pe.matmul(up[t % 2][:, 0:D], ha[:, k, t * P:(t + 1) * P], w3[:, k, :],
                                     start=(k == 0), stop=(k == M - 1))
                last.then_inc(s.out_done, 1)


def phase_cross1(nc, g, i):
    K9 = KT + 1
    LAST = 4
    with Scope(nc, "c1") as sc:
        wk, wv = sc.sb("wk", [P, PAIRS, D]), sc.sb("wv", [P, KD, H * DH])
        wo = sc.sb("wo", [P, PAIRS, D])
        gain, shift, og, ob = (sc.sb(k, [P, D]) for k in ("gain", "shift", "og", "ob"))
        mask8, maskb = sc.sb("mask8", [P, B, KT], U8), sc.sb("maskb", [P, B, K9])
        raw = sc.sb("raw", [P, KT, D])
        ctx = [sc.sb(f"ctx{u}", [P, K9, D + 2]) for u in range(2)]
        ctxT = [sc.sb(f"ctxT{u}", [P, KD, K9 * P]) for u in range(2)]
        qd = [sc.sb(f"qd{u}", [P, PAIRS, P]) for u in range(2)]
        qa = [sc.sb(f"qa{u}", [P, KD, P]) for u in range(2)]
        pr = [sc.sb(f"pr{u}", [P, K9, P]) for u in range(3)]
        top = [sc.sb(f"top{u}", [P, P]) for u in range(2)]
        peak = sc.sb("peak", [P, 1])
        peaks = [sc.sb(f"peaks{u}", [P, P]) for u in range(2)]
        inv = sc.sb("inv", [P, 2])
        un = [sc.sb(f"un{u}", [P, D]) for u in range(2)]
        uT = [sc.sb(f"uT{u}", [P, KD, P]) for u in range(2)]
        zT = sc.sb("zT", [P, PAIRS, T])
        res, resn = sc.sb("res", [P, TT, D]), sc.sb("resn", [P, TT, D])
        n = norm_tensors(sc, "n", TT)
        sps = sc.ps("sps", [P, 12, P])
        ups, uTb, qb, mb = (sc.ps(k, [P, 512]) for k in ("ups", "uTb", "qb", "mb"))
        tps = sc.ps("tps", [P, 4, P])
        uTps = uTb[:, 0:KD * P].rearrange("p (k q) -> p k q", k=KD)
        qaps, zps = qb[:, 0:KD * P].rearrange("p (k q) -> p k q", k=KD), qb[:, KD * P:KD * P + P]
        topT, peakb = mb[:, 0:P], mb[:, P:2 * P]
        s = Names(**{name: sc.sem(name) for name in (
            "w_loaded tables_loaded wo_loaded ctx_loaded chain pool_chain applied affine "
            "blocks turned turned_copied absorbed absorbed_copied scored masked topped topT peaked spread "
            "shifted exped summed inverted normed sumsT sumsT_copied valued valued_copied out_done").split()})
        zTb = zT[:, :, :].rearrange("p h (b n) -> p h b n", n=N)
        block = sc.block()

        @block.sync
        def _(sp):
            def load(batch):
                sp.dma_start(raw[:, :, :], i.ctx[batch].rearrange("(p k) d -> p k d", k=KT)).then_inc(s.ctx_loaded, 16)

            load(0)
            sp.dma_start(mask8[:, :, :], i.mask).then_inc(s.tables_loaded, 16)
            sp.dma_start(gain[:, :], i.l1_ctx_g).then_inc(s.tables_loaded, 16)
            sp.dma_start(shift[:, :], i.l1_ctx_b).then_inc(s.tables_loaded, 16)
            sp.dma_start(wk[:, :, :], rows(i.l1_wkT)).then_inc(s.w_loaded, 16)
            sp.dma_start(wv[:, :, :], rows(i.l1_wv)).then_inc(s.w_loaded, 16)
            sp.dma_start(wo[:, :, :], rows(i.l1_wo)).then_inc(s.wo_loaded, 16)
            sp.dma_start(og[:, :], i.l1_out_g).then_inc(s.wo_loaded, 16)
            sp.dma_start(ob[:, :], i.l1_out_b).then_inc(s.wo_loaded, 16)
            with sp.Fori(0, ITERS) as it:
                for u in range(2):
                    batch = sp.snap((it * 2 + u + 1) % B)
                    sp.wait_ge(s.applied, it * 2 + u + 1)
                    load(batch)
            sp.wait_ge(s.ctx_loaded, 16 * (B + 1))

        @block.gpsimd
        def _(pool):
            chain = Chain(pool, s.pool_chain)
            for u in range(2):
                pool.memset(qd[u][:, :, :], 0.0)
                pool.memset(ctxT[u][:, :, KT * P:K9 * P], 0.0)
                last = pool.memset(ctx[u][:, 0:KT, D:D + 2], 1.0)
            chain(last)

            def prepare(nth, batch, v):
                query_blocks(pool, chain, qd[v], g.qT, batch)
                pool.sem_inc(s.blocks, 1)
                pool.wait_ge(s.applied, nth + 1)
                chain(pool.tensor_copy(ctx[v][:, KT, :], g.lat_rows[:, batch, :]))
                chain(pool.tensor_copy(ctxT[v][:, :, KT * P:KT * P + N], g.latT[:, :, :].rearrange(
                    "p k (b n) -> p k b n", n=N)[:, :, batch, :]))
                wide = [P, KT, D]
                chain(pool.tensor_tensor(ctx[v][:, 0:KT, 0:D], ctx[v][:, 0:KT, 0:D],
                                         gain[:, None, :].to_broadcast(wide), ALU.mult))
                chain(pool.tensor_tensor(ctx[v][:, 0:KT, 0:D], ctx[v][:, 0:KT, 0:D],
                                         shift[:, None, :].to_broadcast(wide), ALU.add))
                pool.sem_inc(s.affine, 1)

            pool.wait_ge(s.tables_loaded, 48)
            prepare(0, 0, 0)
            before, per = chain.n, 2 * 6
            with pool.Fori(0, ITERS) as it:
                chain.enter(it, per)
                for u in range(2):
                    pool.wait_ge(s.scored, it * STEPS + u * PAIRS + 1)
                    prepare(it * 2 + u + 1, (it * 2 + u + 1) % B, 1 - u)
                chain.leave(before, per, ITERS)

        @block.vector
        def _(v):
            chain = Chain(v, s.chain)

            def apply(nth, u, batch):
                v.wait_ge(s.ctx_loaded, 16 * (nth + 1))
                for t in range(KT):
                    last = v.tensor_scalar(ctx[u][:, t, 0:D], raw[:, t, :], g.ctx_mean[:, batch, t:t + 1],
                                           g.ctx_rstd[:, batch, t:t + 1], ALU.subtract, ALU.mult)
                last.then_inc(s.applied, 1)

            def masked(base, j, batch):
                v.wait_ge(s.scored, base + j + 1)
                if j >= 3:
                    v.wait_ge(s.summed, base + j - 2)
                wide = [P, K9, P]
                v.tensor_tensor(pr[j % 3][:, :, :], sps[:, 0:K9, :], maskb[:, batch, :, None].to_broadcast(wide),
                                ALU.add).then_inc(s.masked, 1)

            def peak_of(base, j):
                v.wait_ge(s.topT, base + j + 1)
                chain(v.tensor_reduce(peak[:, :], topT, AX.X, ALU.max))
                if j >= 2:
                    v.wait_ge(s.spread, base + j - 1)
                v.tensor_scalar(peaks[j % 2][:, :], g.ident[:, :], peak[:, 0:1], None, ALU.mult).then_inc(s.peaked, 1)

            def top_of(base, j):
                v.wait_ge(s.masked, base + j + 1)
                if j >= 2:
                    v.wait_ge(s.topT, base + j - 1)
                v.tensor_reduce(top[j % 2][:, :], pr[j % 3][:, :, :].rearrange("p k q -> p q k"), AX.X,
                                ALU.max).then_inc(s.topped, 1)

            def invert(base, j):
                v.wait_ge(s.summed, base + j + 1)
                if j >= 2:
                    v.wait_ge(s.normed, base + j - 1)
                v.reciprocal(inv[:, j % 2:j % 2 + 1], ups[:, D:D + 1]).then_inc(s.inverted, 1)

            def shift_by_peak(base, j):
                v.wait_ge(s.spread, base + j + 1)
                v.tensor_tensor(pr[j % 3][:, :, :], pr[j % 3][:, :, :], peakb[:, None, :].to_broadcast([P, K9, P]),
                                ALU.subtract).then_inc(s.shifted, 1)

            v.memset(maskb[0:N, :, KT], 0.0)
            v.memset(maskb[N:P, :, KT], MASKED)
            v.wait_ge(s.tables_loaded, 48)
            chain(v.tensor_scalar(maskb[:, :, 0:KT], mask8[:, :, :], -1.0, -MASKED, ALU.add, ALU.mult))
            apply(0, 0, 0)
            before, per = chain.n, STEPS
            with v.Fori(0, ITERS) as it:
                chain.enter(it, per)
                base = it * STEPS
                for j in range(STEPS + LAST):
                    u, p = j // PAIRS, j % PAIRS
                    if j < STEPS:
                        masked(base, j, it * 2 + u)
                    if 0 <= j - 1 < STEPS:
                        peak_of(base, j - 1)
                    if j < STEPS:
                        top_of(base, j)
                    if 0 <= j - 2 < STEPS:
                        invert(base, j - 2)
                    if 0 <= j - 1 < STEPS:
                        shift_by_peak(base, j - 1)
                    if j < STEPS and p == 3:
                        apply(it * 2 + u + 1, 1 - u, (it * 2 + u + 1) % B)
                chain.leave(before, per, ITERS)
            v.wait_ge(s.wo_loaded, 48)
            v.wait_ge(s.out_done, 1)
            chain(v.tensor_copy(res[:, :, :], sps[:, 0:8, :].rearrange("p (t c) d -> p t (c d)", c=2)))
            norm_stats(v, chain, n, res, TT)
            chain(norm_apply(v, chain, n, 1, res, resn, TT))
            wide = [P, TT, D]
            chain(v.tensor_tensor(resn[:, :, :], resn[:, :, :], og[:, None, :].to_broadcast(wide), ALU.mult))
            chain(v.tensor_tensor(resn[:, :, :], resn[:, :, :], ob[:, None, :].to_broadcast(wide), ALU.add))
            v.tensor_tensor(g.x_tok[:, :, :], g.x_tok[:, :, :], resn[:, :, :], ALU.add)

        @block.scalar
        def _(a):
            def turned(v, first, r):
                a.wait_ge(s.turned, first + r + 1)
                k, half = r // 2, r % 2
                a.activation(ctxT[v][:, k, half * 512:half * 512 + 512], tps[:, :, :].rearrange("p a b -> p (a b)"),
                             ACT.Copy).then_inc(s.turned_copied, 1)

            def copy_absorbed(base, j):
                a.wait_ge(s.absorbed, base + j + 1)
                if j >= 2:
                    a.wait_ge(s.scored, base + j - 1)
                a.activation(qa[j % 2][:, :, :], qaps, ACT.Copy).then_inc(s.absorbed_copied, 1)

            def exp(base, j):
                a.wait_ge(s.shifted, base + j + 1)
                a.activation(pr[j % 3][:, :, :], pr[j % 3][:, :, :], ACT.Exp).then_inc(s.exped, 1)

            def normalise(base, j):
                a.wait_ge(s.inverted, base + j + 1)
                if j >= 2:
                    a.wait_ge(s.sumsT, base + j - 1)
                a.activation(un[j % 2][:, :], ups[:, 0:D], ACT.Copy, scale=inv[:, j % 2:j % 2 + 1]).then_inc(s.normed, 1)

            def copy_sumsT(base, j):
                a.wait_ge(s.sumsT, base + j + 1)
                if j >= 2:
                    a.wait_ge(s.valued, base + j - 1)
                a.activation(uT[j % 2][:, :, :], uTps, ACT.Copy).then_inc(s.sumsT_copied, 1)

            def copy_values(base, j, batch, p):
                a.wait_ge(s.valued, base + j + 1)
                for half in range(2):
                    part = slice(DH * half, DH * half + DH)
                    last = a.activation(zTb[part, p, batch, :], zps[part, half * N:half * N + N], ACT.Copy)
                last.then_inc(s.valued_copied, 1)

            for r in range(4):
                turned(0, 0, r)
            with a.Fori(0, ITERS) as it:
                base = it * STEPS
                copy_absorbed(base, 0)
                for j in range(STEPS + LAST):
                    u, p = j // PAIRS, j % PAIRS
                    if 0 <= j - 4:
                        copy_values(base, j - 4, it * 2 + (j - 4) // PAIRS, (j - 4) % PAIRS)
                    if j + 1 < STEPS:
                        copy_absorbed(base, j + 1)
                    if 0 <= j - 2 < STEPS:
                        normalise(base, j - 2)
                    if 0 <= j - 3 < STEPS:
                        copy_sumsT(base, j - 3)
                    if 0 <= j - 1 < STEPS:
                        exp(base, j - 1)
                    if j < STEPS and 4 <= p <= 7:
                        turned(1 - u, (it * 2 + u + 1) * 4, p - 4)
            norm_root(a, n, 1)

        @block.tensor
        def _(pe):
            def turn(nth, v, r):
                if r == 0:
                    pe.wait_ge(s.affine, nth + 1)
                if not (isinstance(nth, int) and nth == 0 and r == 0):
                    pe.wait_ge(s.turned_copied, nth * 4 + r)
                for c in range(4):
                    kt, k = (r % 2) * 4 + c, r // 2
                    last = pe.transpose(tps[:, c, :], ctx[v][:, kt, k * P:(k + 1) * P], g.ident[:, :])
                last.then_inc(s.turned, 1)

            def absorb(base, j, nth):
                u, p = j // PAIRS, j % PAIRS
                if p == 0:
                    pe.wait_ge(s.blocks, nth + 1)
                if j >= 5:
                    pe.wait_ge(s.valued_copied, base + j - 4)
                if j >= 1:
                    pe.wait_ge(s.absorbed_copied, base + j)
                for k in range(KD):
                    last = pe.matmul(qaps[:, k, :], wk[:, p, k * P:(k + 1) * P], qd[u][:, p, :], start=True, stop=True)
                last.then_inc(s.absorbed, 1)

            def scores(base, j, nth):
                u, p = j // PAIRS, j % PAIRS
                if p == 0:
                    pe.wait_ge(s.turned_copied, (nth + 1) * 4)
                pe.wait_ge(s.absorbed_copied, base + j + 1)
                if j >= 1:
                    pe.wait_ge(s.masked, base + j)
                for kt in range(K9):
                    for k in range(KD):
                        last = pe.matmul(sps[:, kt, :], ctxT[u][:, k, kt * P:(kt + 1) * P], qa[j % 2][:, k, :],
                                         start=(k == 0), stop=(k == KD - 1))
                last.then_inc(s.scored, 1)

            def turn_top(base, j):
                pe.wait_ge(s.topped, base + j + 1)
                if j >= 1:
                    pe.wait_ge(s.shifted, base + j)
                pe.transpose(topT, top[j % 2][:, :], g.ident[:, :]).then_inc(s.topT, 1)

            def spread(base, j):
                pe.wait_ge(s.peaked, base + j + 1)
                pe.matmul(peakb, g.ones[:, :], peaks[j % 2][:, :], start=True, stop=True).then_inc(s.spread, 1)

            def sums(base, j):
                pe.wait_ge(s.exped, base + j + 1)
                if j >= 1:
                    pe.wait_ge(s.normed, base + j)
                for kt in range(K9):
                    last = pe.matmul(ups[:, 0:D + 1], pr[j % 3][:, kt, :], ctx[j // PAIRS][:, kt, 0:D + 1],
                                     start=(kt == 0), stop=(kt == K9 - 1))
                last.then_inc(s.summed, 1)

            def turn_sums(base, j):
                pe.wait_ge(s.normed, base + j + 1)
                if j >= 1:
                    pe.wait_ge(s.sumsT_copied, base + j)
                for k in range(KD):
                    last = pe.transpose(uTps[:, k, :], un[j % 2][:, k * P:(k + 1) * P], g.ident[:, :])
                last.then_inc(s.sumsT, 1)

            def values(base, j):
                p = j % PAIRS
                pe.wait_ge(s.sumsT_copied, base + j + 1)
                pe.wait_ge(s.absorbed_copied, base + min(j + 5, STEPS))
                if j >= 1:
                    pe.wait_ge(s.valued_copied, base + j)
                for k in range(KD):
                    last = pe.matmul(zps, wv[:, k, p * P:(p + 1) * P], uT[j % 2][:, k, :],
                                     start=(k == 0), stop=(k == KD - 1))
                last.then_inc(s.valued, 1)

            for r in range(4):
                turn(0, 0, r)
            pe.wait_ge(s.w_loaded, 32)
            with pe.Fori(0, ITERS) as it:
                base = it * STEPS
                absorb(base, 0, it * 2)
                for j in range(STEPS + LAST):
                    u, p = j // PAIRS, j % PAIRS
                    if j < STEPS:
                        scores(base, j, it * 2 + u)
                    if 0 <= j - 4 < STEPS:
                        values(base, j - 4)
                    if 0 <= j - 1 < STEPS:
                        turn_top(base, j - 1)
                    if 0 <= j - 2 < STEPS:
                        sums(base, j - 2)
                    if j + 1 < STEPS:
                        absorb(base, j + 1, it * 2 + (j + 1) // PAIRS)
                    if 0 <= j - 1 < STEPS:
                        spread(base, j - 1)
                    if 0 <= j - 3 < STEPS:
                        turn_sums(base, j - 3)
                    if j < STEPS and 4 <= p <= 7:
                        turn(it * 2 + u + 1, 1 - u, p - 4)
                pe.wait_ge(s.valued_copied, base + STEPS)
            pe.wait_ge(s.wo_loaded, 48)
            for t in range(TT):
                for p in range(PAIRS):
                    last = pe.matmul(sps[:, 2 * t:2 * t + 2, :].rearrange("p a b -> p (a b)"),
                                     zT[:, p, t * P:(t + 1) * P], wo[:, p, :], start=(p == 0), stop=(p == PAIRS - 1))
            last.then_inc(s.out_done, 1)


def phase_attn1(nc, g, i):
    HN, HD = 8, P
    UNITS = TT
    HP = HN // 2
    with Scope(nc, "a1") as sc:
        wq, wkv, wo = sc.sb("wq", [P, KD, HN * HD]), sc.sb("wkv", [P, KD, 2 * HD]), sc.sb("wo", [P, HN, D])
        bqk, bv, pos = sc.sb("bqk", [P, HN + 1]), sc.sb("bv", [P, HD]), sc.sb("pos", [P, N])
        causal = sc.sb("causal", [P, N])
        m = turned_norm(sc, "m")
        qT = sc.sb("qT", [P, B, HN, N])
        kT = sc.sb("kT", [P, B, N])
        vr = sc.sb("vr", [N, B, HD])
        sm = [sc.sb(f"sm{u}", [P, 2, HP, N]) for u in range(2)]
        mx, su, rs = sc.sb("mx", [P, 2, HP]), sc.sb("su", [P, 2, HP]), sc.sb("rs", [P, 2, HP])
        pT = [sc.sb(f"pT{u}", [N, HN * N]) for u in range(2)]
        oT = sc.sb("oT", [P, HN, T])
        pps = [sc.ps(f"pps{u}", [P, T]) for u in range(2)]
        sps = [sc.ps(f"sps{u}", [P, 2, HP, N]) for u in range(2)]
        ptps, ops = sc.ps("ptps", [N, HN * N]), sc.ps("ops", [P, HN, N])
        s = Names(**{name: sc.sem(name) for name in (
            "w_loaded t_loaded wo_loaded chain projected taken scored shifted exped probs turned turned_copied summed "
            "summed_copied out_done").split()})
        block = sc.block()

        @block.sync
        def _(sp):
            for to, of in ((bqk, i.a1_bqk), (bv, i.a1_bv), (pos, i.a1_pos), (causal, i.causal)):
                sp.dma_start(to[:, :], of).then_inc(s.t_loaded, 16)
            sp.dma_start(wq[:, :, :], rows(i.a1_wq)).then_inc(s.w_loaded, 16)
            sp.dma_start(wkv[:, :, :], rows(i.a1_wkv)).then_inc(s.w_loaded, 16)
            sp.dma_start(wo[:, :, :], rows(i.a1_wo)).then_inc(s.wo_loaded, 16)

        @block.vector
        def _(v):
            chain = Chain(v, s.chain)
            turned_norm_vector(v, chain, m, g.x_tok)
            v.wait_ge(s.t_loaded, 64)
            by_batch = lambda t: t.rearrange("p (b n) -> p b n", n=N)
            for c in range(HN + 1):
                v.wait_ge(s.projected, c + 1)
                v.scalar_tensor_tensor(out=kT[:, :, :] if c == 0 else qT[:, :, c - 1, :], in0=by_batch(pps[c % 2][:, :]),
                                       scalar=bqk[:, c:c + 1], in1=pos[:, None, :].to_broadcast([P, B, N]),
                                       op0=ALU.add, op1=ALU.add).then_inc(s.taken, 1)
            for c in range(2):
                v.wait_ge(s.projected, HN + 1 + c + 1)
                v.tensor_tensor(vr[:, 4 * c:4 * c + 4, :], pps[(HN + 1 + c) % 2][0:N, :].rearrange("p (b e) -> p b e", b=4),
                                bv[0:N, None, :].to_broadcast([N, 4, HD]), ALU.add).then_inc(s.taken, 1)

            def shift(unit):
                v.wait_ge(s.scored, unit + 1)
                if unit >= 2:
                    v.wait_ge(s.turned, 2 * (unit - 1))
                to = sm[unit % 2]
                for b in range(2):
                    last = v.scalar_tensor_tensor(out=to[:, b, :, :], in0=sps[unit % 2][:, b, :, :], scalar=HD ** -0.5,
                                                  in1=causal[:, None, :].to_broadcast([P, HP, N]), op0=ALU.mult, op1=ALU.add)
                chain(last)
                chain(v.tensor_reduce(mx[:, :, :], to[:, :, :, :], AX.X, ALU.max))
                v.tensor_tensor(to[:, :, :, :], to[:, :, :, :], mx[:, :, :, None].to_broadcast([P, 2, HP, N]),
                                ALU.subtract).then_inc(s.shifted, 1)

            def normalise(unit):
                v.wait_ge(s.exped, unit + 1)
                of = sm[unit % 2]
                chain(v.tensor_reduce(su[:, :, :], of[:, :, :, :], AX.X, ALU.add))
                chain(v.reciprocal(rs[:, :, :], su[:, :, :]))
                v.tensor_tensor(of[:, :, :, :], of[:, :, :, :], rs[:, :, :, None].to_broadcast([P, 2, HP, N]),
                                ALU.mult).then_inc(s.probs, 1)

            for unit in range(UNITS + 1):
                if unit < UNITS:
                    shift(unit)
                if unit >= 1:
                    normalise(unit - 1)
            for t in range(TT):
                v.wait_ge(s.out_done, t // 2 * 2 + 2)
                v.tensor_tensor(g.x_tok[:, t, :], g.x_tok[:, t, :], pps[t // 2][:, t % 2 * D:t % 2 * D + D], ALU.add)

        @block.scalar
        def _(a):
            turned_norm_scalar(a, m)

            def exp(unit):
                a.wait_ge(s.shifted, unit + 1)
                a.activation(sm[unit % 2][:, :, :, :], sm[unit % 2][:, :, :, :], ACT.Exp).then_inc(s.exped, 1)

            exp(0)
            for b in range(B + 1):
                if b % 2 == 0 and b // 2 + 1 < UNITS:
                    exp(b // 2 + 1)
                if b < B:
                    a.wait_ge(s.turned, b + 1)
                    if b >= 2:
                        a.wait_ge(s.summed, b - 1)
                    a.activation(pT[b % 2][:, :], ptps[:, :], ACT.Copy).then_inc(s.turned_copied, 1)
                if b >= 1:
                    w = b - 1
                    a.wait_ge(s.summed, w + 1)
                    a.activation(oT[:, :, w * N:w * N + N], ops[:, :, :], ACT.Copy).then_inc(s.summed_copied, 1)

        @block.tensor
        def _(pe):
            turned_norm_tensor(pe, g, m)
            pe.wait_ge(m.copied, KD)
            pe.wait_ge(s.w_loaded, 32)
            for c in range(HN + 1):
                if c >= 2:
                    pe.wait_ge(s.taken, c - 1)
                for k in range(KD):
                    w = wkv[:, k, 0:HD] if c == 0 else wq[:, k, (c - 1) * HD:c * HD]
                    last = pe.matmul(pps[c % 2][:, :], w, m.yT[:, k, :], start=(k == 0), stop=(k == KD - 1))
                last.then_inc(s.projected, 1)
            for c in range(2):
                nth = HN + 1 + c
                pe.wait_ge(s.taken, nth - 1)
                for b in range(4):
                    at = (4 * c + b) * N
                    for k in range(KD):
                        last = pe.matmul(pps[nth % 2][0:N, b * HD:(b + 1) * HD], m.yT[:, k, at:at + N],
                                         wkv[:, k, HD:2 * HD], start=(k == 0), stop=(k == KD - 1))
                last.then_inc(s.projected, 1)
            pe.wait_ge(s.taken, HN + 3)

            def scores(unit):
                if unit >= 2:
                    pe.wait_ge(s.shifted, unit - 1)
                for b in range(2):
                    for h in range(HP):
                        q = qT[:, 2 * unit + b, 2 * h:2 * h + 2, :].rearrange("p h n -> p (h n)")
                        last = pe.matmul(sps[unit % 2][:, b, h, :], q, kT[:, 2 * unit + b, :], start=True, stop=True)
                last.then_inc(s.scored, 1)

            scores(0)
            scores(1)
            for b in range(B + 1):
                unit = b // 2
                if b < B:
                    if b % 2 == 0:
                        pe.wait_ge(s.probs, unit + 1)
                    if b >= 1:
                        pe.wait_ge(s.turned_copied, b)
                    for h in range(HP):
                        last = pe.transpose(ptps[:, h * P:(h + 1) * P], sm[unit % 2][:, b % 2, h, :], g.ident[:, :])
                    last.then_inc(s.turned, 1)
                if b >= 1:
                    w = b - 1
                    pe.wait_ge(s.turned_copied, w + 1)
                    if w >= 1:
                        pe.wait_ge(s.summed_copied, w)
                    pe.matmul(ops[:, :, :].rearrange("p h n -> p (h n)"), vr[:, w, :], pT[w % 2][:, :],
                              start=True, stop=True).then_inc(s.summed, 1)
                if b % 2 == 1 and unit + 2 < UNITS:
                    scores(unit + 2)
            pe.wait_ge(s.summed_copied, B)
            pe.wait_ge(s.wo_loaded, 16)
            for t in range(TT):
                for h in range(HN):
                    last = pe.matmul(pps[t // 2][:, t % 2 * D:t % 2 * D + D], oT[:, h, t * P:(t + 1) * P], wo[:, h, :],
                                     start=(h == 0), stop=(h == HN - 1))
                last.then_inc(s.out_done, 1)


def phase_experts(nc, g, i):
    E, GROUPS, PER, TOP_GROUPS = EXPERTS, 4, EXPERTS // 4, 2
    ALL = E + 2
    RING = 4
    with Scope(nc, "e1") as sc:
        we = [sc.sb(f"we{u}", [P, 3 * D]) for u in range(RING)]
        gw, gbias, below = sc.sb("gw", [P, KD, E]), sc.sb("gbias", [P, E]), sc.sb("below", [P, GROUPS, GROUPS])
        m = turned_norm(sc, "m")
        score, choice, masked, left = (sc.sb(k, [P, TT, E]) for k in ("score", "choice", "masked", "left"))
        best = sc.sb("best", [P, TT, GROUPS, 8])
        gsum, rank, gmask = (sc.sb(k, [P, TT, GROUPS]) for k in ("gsum", "rank", "gmask"))
        more, same = sc.sb("more", [P, TT, GROUPS, GROUPS]), sc.sb("same", [P, TT, GROUPS, GROUPS])
        best8 = sc.sb("best8", [P, TT, 8])
        wsum = sc.sb("wsum", [P, TT])
        weight = sc.sb("weight", [P, TT, ALL])
        act = [sc.sb(f"act{u}", [P, T]) for u in range(2)]
        hid = [sc.sb(f"hid{u}", [P, T]) for u in range(2)]
        gps, ups = m.tps, [sc.ps(f"ups{u}", [P, T]) for u in range(2)]
        dps = [sc.ps(f"dps{u}", [P, TT, D]) for u in range(2)]
        s = Names(**{name: sc.sem(name) for name in (
            "t_loaded chain gated scored weighed gate_done up_done silued hidden down_done added").split()})
        loaded = [sc.sem(f"loaded{u}") for u in range(RING)]
        block = sc.block()

        @block.sync
        def _(sp):
            def load(e, u):
                sp.dma_start(we[u][:, :], i.e1_w[e]).then_inc(loaded[u], 16)

            sp.dma_start(gw[:, :, :], rows(i.e1_gw)).then_inc(s.t_loaded, 16)
            sp.dma_start(gbias[:, :], i.e1_bias).then_inc(s.t_loaded, 16)
            sp.dma_start(below[:, :, :], i.e1_below).then_inc(s.t_loaded, 16)
            for u in range(RING):
                load(u, u)
            with sp.Fori(0, E // RING - 1) as it:
                for u in range(RING):
                    e = sp.snap(it * RING + u + RING)
                    sp.wait_ge(s.down_done, it * RING + u + 1)
                    load(e, u)
            for u in range(2):
                sp.wait_ge(s.down_done, E - RING + u + 1)
                load(E + u, u)

        @block.vector
        def _(v):
            chain = Chain(v, s.chain)
            turned_norm_vector(v, chain, m, g.x_tok)
            v.memset(weight[:, :, E:ALL], 1.0)
            v.wait_ge(s.scored, 1)
            v.wait_ge(s.t_loaded, 48)
            chain(v.tensor_tensor(choice[:, :, :], score[:, :, :], gbias[:, None, :].to_broadcast([P, TT, E]), ALU.add))
            for t in range(TT):
                for q in range(GROUPS):
                    last = v.max(best[:, t, q, :], choice[:, t, q * PER:(q + 1) * PER])
            chain(last)
            chain(v.tensor_tensor(gsum[:, :, :], best[:, :, :, 0], best[:, :, :, 1], ALU.add))
            wide = [P, TT, GROUPS, GROUPS]
            other, own = gsum[:, :, None, :].to_broadcast(wide), gsum[:, :, :, None].to_broadcast(wide)
            v.tensor_tensor(more[:, :, :, :], other, own, ALU.is_gt)
            chain(v.tensor_tensor(same[:, :, :, :], other, own, ALU.is_equal))
            flat = lambda t: t[:, :, :, :].rearrange("p t a b -> p t (a b)")
            chain(v.tensor_tensor(flat(same), flat(same), below[:, :, :].rearrange("p a b -> p (a b)")[:, None, :]
                                  .to_broadcast([P, TT, GROUPS * GROUPS]), ALU.mult))
            chain(v.tensor_tensor(more[:, :, :, :], more[:, :, :, :], same[:, :, :, :], ALU.add))
            chain(v.tensor_reduce(rank[:, :, :], more[:, :, :, :], AX.X, ALU.add))
            chain(v.tensor_scalar(gmask[:, :, :], rank[:, :, :], TOP_GROUPS - 0.5, None, ALU.is_lt))
            grouped = lambda t: t[:, :, :].rearrange("p t (a b) -> p t a b", b=PER)
            chain(v.tensor_tensor(grouped(masked), grouped(choice), gmask[:, :, :, None].to_broadcast([P, TT, GROUPS, PER]),
                                  ALU.mult))
            chain(v.tensor_scalar(masked[:, :, :], masked[:, :, :], 0.0, None, ALU.add))
            for t in range(TT):
                last = v.max(best8[:, t, :], masked[:, t, :])
            chain(last)
            for t in range(TT):
                last = v.match_replace(out=left[:, t, :], in_to_replace=best8[:, t, :], in_values=masked[:, t, :],
                                       imm_value=MASKED)
            chain(last)
            chain(v.tensor_scalar(left[:, :, :], left[:, :, :], MASKED / 2, None, ALU.is_lt))
            chain(v.tensor_tensor(masked[:, :, :], left[:, :, :], score[:, :, :], ALU.mult))
            chain(v.tensor_reduce(wsum[:, :], masked[:, :, :], AX.X, ALU.add))
            chain(v.tensor_scalar(wsum[:, :], wsum[:, :], 1e-20, None, ALU.add))
            chain(v.reciprocal(wsum[:, :], wsum[:, :]))
            chain(v.tensor_scalar(wsum[:, :], wsum[:, :], ROUTED_SCALING, None, ALU.mult))
            chain(v.tensor_tensor(weight[:, :, 0:E], masked[:, :, :], wsum[:, :, None].to_broadcast([P, TT, E]), ALU.mult))

            def hide(e, u):
                v.wait_ge(s.silued, e + 1)
                v.wait_ge(s.up_done, e + 1)
                v.tensor_tensor(hid[u % 2][:, :], ups[u % 2][:, :], act[u % 2][:, :], ALU.mult).then_inc(s.hidden, 1)

            def add(e, u):
                v.wait_ge(s.down_done, e + 1)
                for t in range(TT):
                    last = v.scalar_tensor_tensor(out=g.x_tok[:, t, :], in0=dps[u % 2][:, t, :], scalar=weight[:, t, e:e + 1]
                                                  if isinstance(e, int) else weight[:, t, bass.ds(e, 1)],
                                                  in1=g.x_tok[:, t, :], op0=ALU.mult, op1=ALU.add)
                last.then_inc(s.added, 1)

            hide(0, 0)
            with v.Fori(0, E // RING) as it:
                for u in range(RING):
                    e = it * RING + u
                    hide(e + 1, u + 1)
                    add(e, u)
                    v.wait_ge(s.added, e + 1)
            hide(E + 1, E + 1)
            add(E, E)
            v.wait_ge(s.added, E + 1)
            add(E + 1, E + 1)

        @block.scalar
        def _(a):
            turned_norm_scalar(a, m)
            a.wait_ge(s.gated, 1)
            a.activation(score[:, :, :], ups[1][:, 0:TT * E].rearrange("p (t e) -> p t e", t=TT), ACT.Sigmoid).then_inc(s.scored, 1)

            def silu(e, u, free):
                a.wait_ge(s.gate_done, e + 1)
                if free is not None:
                    a.wait_ge(s.hidden, free)
                a.activation(act[u % 2][:, :], gps[u % 2][:, :], ACT.Silu).then_inc(s.silued, 1)

            silu(0, 0, None)
            silu(1, 1, None)
            with a.Fori(0, E // RING) as it:
                for u in range(RING):
                    silu(it * RING + u + 2, u, it * RING + u + 1)

        @block.tensor
        def _(pe):
            turned_norm_tensor(pe, g, m)
            pe.wait_ge(m.copied, KD)
            pe.wait_ge(s.t_loaded, 48)
            for t in range(TT):
                for k in range(KD):
                    last = pe.matmul(ups[1][:, t * E:(t + 1) * E], m.yT[:, k, t * P:(t + 1) * P], gw[:, k, :],
                                     start=(k == 0), stop=(k == KD - 1))
            last.then_inc(s.gated, 1)

            def gate_up(e, u, free, turn=0):
                pe.wait_ge(loaded[u % RING], (turn + 1 + u // RING) * 16)
                for o, ps, done, used in ((0, gps, s.gate_done, s.silued), (D, ups, s.up_done, s.hidden)):
                    if free is not None:
                        pe.wait_ge(used, free)
                    for k in range(KD):
                        last = pe.matmul(ps[u % 2][:, :], we[u % RING][:, o + k * P:o + (k + 1) * P], m.yT[:, k, :],
                                         start=(k == 0), stop=(k == KD - 1))
                    last.then_inc(done, 1)

            def down(e, u, free):
                pe.wait_ge(s.hidden, e + 1)
                if free is not None:
                    pe.wait_ge(s.added, free)
                for t in range(TT):
                    last = pe.matmul(dps[u % 2][:, t, :], hid[u % 2][:, t * P:(t + 1) * P], we[u % RING][:, 2 * D:3 * D],
                                     start=True, stop=True)
                last.then_inc(s.down_done, 1)

            gate_up(0, 0, None)
            pe.wait_ge(s.scored, 1)
            gate_up(1, 1, None)
            with pe.Fori(0, E // RING) as it:
                for u in range(RING):
                    e = it * RING + u
                    gate_up(e + 2, u + 2, e + 1, it)
                    down(e, u, None)
            down(E, E, E - 1)
            down(E + 1, E + 1, E)


def phase_store(nc, g, o):
    with Scope(nc, "store") as sc:
        stored = sc.sem("stored")
        block = sc.block()

        @block.sync
        def _(sp):
            sp.dma_start(o.rearrange("(t p) d -> p t d", p=P), g.x_tok[:, :, :]).then_inc(stored, 16)
            sp.wait_ge(stored, 16)


def build(nc, i, o, only=range(6)):
    with Scope(nc, "g") as sc:
        g = Names(
            x_tok=sc.sb("x_tok", [P, TT, D]), ident=sc.sb("ident", [P, P]), ones=sc.sb("ones", [P, P]),
            ctx_mean=sc.sb("ctx_mean", [P, B, KT]), ctx_rstd=sc.sb("ctx_rstd", [P, B, KT]))
        phase_setup(nc, g, i)
        if 0 in only:
            with Scope(nc, "x0") as sx:
                g.qT, g.qrT = sx.sb("qT", [P, PAIRS, T]), sx.sb("qrT", [P, PAIRS, T])
                phase_queries(nc, g, i, 0, i.l0_wq, i.l0_lat_g, i.l0_lat_b)
                phase_cross0(nc, g, i)
        if 1 in only:
            phase_attn0(nc, g, i)
        if 2 in only:
            phase_ffn0(nc, g, i)
        if 3 in only:
            with Scope(nc, "x1") as sx:
                g.qT, g.latT = sx.sb("qT", [P, PAIRS, T]), sx.sb("latT", [P, KD, T])
                g.lat_rows = sx.sb("lat_rows", [P, B, D + 2])
                phase_queries(nc, g, i, 1, i.l1_wq, i.l1_lat_g, i.l1_lat_b)
                phase_cross1(nc, g, i)
        if 4 in only:
            phase_attn1(nc, g, i)
        if 5 in only:
            phase_experts(nc, g, i)
        phase_store(nc, g, o)


def laid_out(a):
    wide = lambda v: np.ascontiguousarray(np.broadcast_to(v, (P, v.shape[-1])))
    keyed = lambda c: np.ascontiguousarray(
        np.tile(c.reshape(P, KT, -1).transpose(2, 1, 0).reshape(-1, S), (4, 1)))
    c = np.ascontiguousarray
    per = lambda v: c(v.reshape(-1, P).T)
    tiled = lambda v, n: np.tile(v, P // n)
    head = np.arange(P)[:, None] // 16 == np.arange(8)
    query, key = np.arange(P)[:, None] % N, np.arange(N)[None, :]
    w1, b1 = a["L1_attn_Wkv"], a["L1_attn_bkv"]
    pos = np.arange(N, dtype=np.float32)[:, None]
    ang = pos * np.exp(-np.log(np.float32(10000.0)) * np.arange(0, P, 2, dtype=np.float32) / np.float32(P))[None, :]
    pe = np.zeros((N, P), np.float32)
    pe[:, 0::2], pe[:, 1::2] = np.sin(ang), np.cos(ang)
    gates = lambda w: w.transpose(0, 2, 1).reshape(-1, KD, P, P).transpose(0, 2, 1, 3).reshape(-1, P, D)
    both = lambda k: np.concatenate([a[f"L1_ffn_expert_{k}"], a[f"L1_ffn_shared_{k}"].reshape(2, P, D)])
    down = np.concatenate([a["L1_ffn_expert_down"].transpose(0, 2, 1), a["L1_ffn_shared_down"].T.reshape(2, P, D)])
    below = np.arange(4)[None, :] < np.arange(4)[:, None]
    return {
        "e1_w": c(np.concatenate([gates(both("gate")), gates(both("up")), down], axis=2)),
        "e1_gw": c(a["L1_ffn_gate_w"].T), "e1_bias": wide(a["L1_ffn_gate_bias"]),
        "e1_below": c(np.broadcast_to(below.astype(np.float32), (P, 4, 4))),
        "a1_wq": a["L1_attn_Wq"], "a1_wkv": w1, "a1_wo": a["L1_attn_Wo"],
        "a1_bqk": c(np.concatenate([b1[None, :P], a["L1_attn_bq"].reshape(8, P)]).T), "a1_bv": wide(b1[P:]),
        "a1_pos": c(pe.T),
        "mask": c(a["mask_BxS2_bf1"].view(np.uint8).reshape(B, P, KT).transpose(1, 0, 2)),
        "l1_lat_g": wide(a["L1_xattn_g_l"]), "l1_lat_b": wide(a["L1_xattn_b_l"]),
        "l1_ctx_g": wide(a["L1_xattn_g_x"]), "l1_ctx_b": wide(a["L1_xattn_b_x"]),
        "l1_out_g": wide(a["L1_xattn_g_o"]), "l1_out_b": wide(a["L1_xattn_b_o"]),
        "l1_wq": a["L1_xattn_Wq"], "l1_wkT": c(a["L1_xattn_Wkv"][:, :H * DH].T),
        "l1_wv": c(a["L1_xattn_Wkv"][:, H * DH:]), "l1_wo": a["L1_xattn_Wout"],
        "causal": np.where(key <= query, 0.0, MASKED).astype(np.float32),
        "heads": head.astype(np.float32),
        "a0_lqk": c(np.broadcast_to(np.stack([a[f"L0_attn_{k}"].reshape(H) for k in ("lq1", "lq2", "lk1", "lk2")]), (P, 4, H))),
        "a0_chan": c(np.stack([np.tile(a[f"L0_attn_{k}"], P // 32) for k in ("gn_w", "gn_b", "gamma")], axis=1)),
        "a0_wqk": c(np.stack([a[f"L0_attn_{k}"].T for k in ("Wq1", "Wq2", "Wk1", "Wk2")])),
        "a0_wv": c(a["L0_attn_Wv"].T), "a0_wc": c(a["L0_attn_Wc"].T),
        "f0_w1": c(a["L0_ffn_w1_w"].T), "f0_w2": c(a["L0_ffn_w2_w"].T),
        "f0_h1": c(a["L0_ffn_h1_w"].T), "f0_h2": c(a["L0_ffn_h2_w"].T), "f0_w3": c(a["L0_ffn_w3_w"].T),
        "f0_scales": c(np.stack([per(a[f"L0_ffn_{k}_s"]) for k in ("w1", "w2", "h1", "h2")], axis=1)),
        "f0_w3s": wide(a["L0_ffn_w3_s"]),
        "x": a["x"].reshape(T, D),
        "ctx": a["ctx_1024"],
        "l0_lat_g": wide(a["L0_xattn_ln_lat_g"]), "l0_lat_b": wide(a["L0_xattn_ln_lat_b"]),
        "l0_ctx_g": wide(a["L0_xattn_ln_ctx_g"]), "l0_ctx_b": wide(a["L0_xattn_ln_ctx_b"]),
        "l0_cos": keyed(a["L0_xattn_cos"]), "l0_sin": keyed(a["L0_xattn_sin"]),
        "l0_wq": a["L0_xattn_Wq"],
        "l0_wk": np.ascontiguousarray(a["L0_xattn_Wkv"][:, :H * DH]),
        "l0_wv": np.ascontiguousarray(a["L0_xattn_Wkv"][:, H * DH:]),
        "l0_wo": a["L0_xattn_Wo"], "l0_bo": wide(a["L0_xattn_bo"]),
    }


def kernel(**inputs):
    import concourse.bacc as bacc
    from concourse.bass_utils import run_bass_kernel_spmd

    arrays = {f"in_{k}": np.ascontiguousarray(v) for k, v in
              laid_out({k: np.asarray(v) for k, v in inputs.items()}).items()}
    nc = bacc.Bacc("TRN2", target_bir_lowering=False, num_devices=1)
    i = Names(**{k[3:]: nc.dram_tensor(k, v.shape, mybir.dt.from_np(v.dtype), kind="ExternalInput").ap()
                           for k, v in arrays.items()})
    o = nc.dram_tensor("out_0", (T, D), F32, kind="ExternalOutput").ap()
    build(nc, i, o)
    r = run_bass_kernel_spmd(nc, [arrays], core_ids=[0])
    return r.results[0]["out_0"].reshape(B, N, D)
```

```python
from contextlib import ExitStack

import numpy as np

import concourse.bass as bass
from concourse import mybir

F32 = mybir.dt.float32
F32R = mybir.dt.float32r
U8 = mybir.dt.uint8
ALU = mybir.AluOpType
ACT = mybir.ActivationFunctionType
AX = mybir.AxisListType

P = 128
B, N, S, D = 8, 64, 1024, 256
T = B * N
TT = T // P
KD = D // P
KT = S // P
H, DH = 16, 64
PAIRS = H * DH // P
STEPS = 2 * PAIRS
ITERS = B // 2
EPS = 1e-5
MASKED = -1e30
LAMBDA_INIT = 0.8 - 0.6 * float(np.exp(-0.3 * 11))
EXPERTS = 32
ROUTED_SCALING = 2.5


def Names(**named):
    return type("Names", (), named)()


class Chain:

    def __init__(self, engine, sem):
        self.engine, self.sem, self.base, self.n = engine, sem, 0, 0

    def __call__(self, instruction):
        instruction.then_inc(self.sem, 1)
        self.n += 1
        self.engine.wait_ge(self.sem, self.base + self.n)

    def enter(self, iteration, per_iteration):
        self.base = self.base + self.n + iteration * per_iteration
        self.n = 0

    def leave(self, before, per_iteration, iterations):
        assert self.n == per_iteration, (self.n, per_iteration)
        self.base, self.n = before + per_iteration * iterations, 0


class Scope:

    def __init__(self, nc, name):
        self.nc, self.name, self.stack, self.sems = nc, name, ExitStack(), []
        self.opened = ExitStack()

    def __enter__(self):
        return self

    def __exit__(self, *e):
        self.opened.__exit__(*e)
        if self.sems and not any(e):
            numbers = sorted(x.num for x in self.sems)
            with self.nc.Block() as block:
                @block.gpsimd
                def _(pool):
                    start = last = numbers[0]
                    for x in numbers[1:] + [None]:
                        if x != last + 1:
                            pool.sem_clear(range(start, last + 1))
                            start = x
                        last = x if x is not None else last
        return self.stack.__exit__(*e)

    def sb(self, name, shape, dt=F32):
        return self.stack.enter_context(self.nc.sbuf_tensor(f"{self.name}_{name}", shape, dt))

    def ps(self, name, shape, dt=F32):
        return self.stack.enter_context(self.nc.psum_tensor(f"{self.name}_{name}", shape, dt))

    def sem(self, name):
        self.sems.append(self.stack.enter_context(self.nc.semaphore(f"{self.name}_{name}")))
        return self.sems[-1]

    def block(self):
        return self.opened.enter_context(self.nc.Block())


def norm_tensors(sc, name, tiles):
    n = Names(**{k: sc.sb(f"{name}_{k}", [P, tiles])
                           for k in "sum dif sq dif2 sqe mean var std rstd".split()})
    n.stats = sc.sb(f"{name}_stats", [P, tiles, 6])
    n.var_ready, n.std_ready = sc.sem(f"{name}_var_ready"), sc.sem(f"{name}_std_ready")
    return n


def norm_stats(v, chain, n, src, tiles):
    for t in range(tiles):
        last = v.bn_stats(n.stats[:, t, :], src[:, t, 0:D])
    chain(last)
    even, odd = n.stats[:, :, 1], n.stats[:, :, 4]
    v.tensor_tensor(n.sum[:, :], even, odd, ALU.add)
    v.tensor_tensor(n.dif[:, :], even, odd, ALU.subtract)
    chain(v.tensor_tensor(n.sq[:, :], n.stats[:, :, 2], n.stats[:, :, 5], ALU.add))
    v.tensor_scalar(n.mean[:, :], n.sum[:, :], 0.5, None, ALU.mult)
    v.scalar_tensor_tensor(out=n.dif2[:, :], in0=n.dif[:, :], scalar=0.25, in1=n.dif[:, :], op0=ALU.mult, op1=ALU.mult)
    chain(v.tensor_scalar(n.sqe[:, :], n.sq[:, :], 1.0 / D, EPS, ALU.mult, ALU.add))
    v.tensor_tensor(n.var[:, :], n.sqe[:, :], n.dif2[:, :], ALU.add).then_inc(n.var_ready, 1)


def norm_root(a, n, count):
    a.wait_ge(n.var_ready, count)
    a.activation(n.std[:, :], n.var[:, :], ACT.Sqrt).then_inc(n.std_ready, 1)


def norm_apply(v, chain, n, count, src, dst, tiles):
    v.wait_ge(n.std_ready, count)
    chain(v.reciprocal(n.rstd[:, :], n.std[:, :]))
    for t in range(tiles):
        last = v.tensor_scalar(dst[:, t, 0:D], src[:, t, 0:D], n.mean[:, t:t + 1], n.rstd[:, t:t + 1],
                               ALU.subtract, ALU.mult)
    return last


def rows(ap):
    return ap.rearrange("(k p) n -> p k n", p=P)



def phase_setup(nc, g, i):
    with Scope(nc, "setup") as sc:
        loaded, zeroed, done = sc.sem("loaded"), sc.sem("zeroed"), sc.sem("done")
        block = sc.block()

        @block.sync
        def _(sp):
            sp.dma_start(g.x_tok[:, :, :], i.x.rearrange("(t p) d -> p t d", p=P)).then_inc(loaded, 16)
            sp.wait_ge(loaded, 16)

        @block.gpsimd
        def _(pool):
            pool.memset(g.ident[:, :], 0.0).then_inc(zeroed, 1)
            pool.memset(g.ones[:, :], 1.0)
            pool.wait_ge(zeroed, 1)
            pool.affine_select(out=g.ident[:, :], in_=g.ident[:, :], compare_op=ALU.not_equal, fill=1.0,
                               base=0, pattern=[[-1, P]], channel_multiplier=1).then_inc(done, 1)
            pool.wait_ge(done, 1)


def phase_queries(nc, g, i, layer, wq, gain, shift, ctx, wk):
    with Scope(nc, f"q{layer}") as sc:
        y = sc.sb("y", [P, TT, D])
        z = sc.sb("z", [P, TT, D])
        gain_sb, shift_sb = sc.sb("gain", [P, D]), sc.sb("shift", [P, D])
        w = sc.sb("w", [P, KD, H * DH])
        zT = sc.sb("zT", [P, KD, T])
        qT = sc.sb("qT", [P, PAIRS, T])
        n = norm_tensors(sc, "n", TT)
        tps = sc.ps("tps", [P, KD, T])
        qps = sc.ps("qps", [P, 2, T])
        w_loaded, g_loaded, wk_loaded, wk_hi = (sc.sem(k) for k in ("w_loaded", "g_loaded", "wk_loaded", "wk_hi"))
        chain_sem, stored = sc.sem("chain"), sc.sem("stored")
        latents, turned, turned_copied = sc.sem("latents"), sc.sem("turned"), sc.sem("turned_copied")
        projected, taken, lat_stored = sc.sem("projected"), sc.sem("taken"), sc.sem("lat_stored")
        block = sc.block()

        @block.sync
        def _(sp):
            sp.dma_start(gain_sb[:, :], gain).then_inc(g_loaded, 16)
            sp.dma_start(shift_sb[:, :], shift).then_inc(g_loaded, 16)
            ctx.load(sp, 0, latents=False)
            sp.dma_start(w[:, :, :], rows(wq)).then_inc(w_loaded, 16)
            for to, of in ctx.table_loads:
                sp.dma_start(to, of).then_inc(ctx.tables, 16)
            if layer == 0:
                sp.dma_start(wk.staged, rows(wk.source)).then_inc(wk_loaded, 16)
            else:
                sp.wait_ge(ctx.empty, 2)
                sp.wait_ge(latents, TT)
                sp.dma_start(g.lat.rearrange("b n d -> (b n) d").rearrange("(t p) d -> p t d", p=P),
                             z[:, :, :]).then_inc(lat_stored, 16)
                sp.wait_ge(lat_stored, 16)
                ctx.load_latents(sp, 0)
            for p in range(0, PAIRS, 2):
                sp.wait_ge(taken, p + 2)
                sp.dma_start(g.q[:, p:p + 2, :], qT[:, p:p + 2, :]).then_inc(stored, 16)
            sp.wait_ge(stored, 16 * (PAIRS // 2))

        @block.gpsimd
        def _(pool):
            ctx.constants(pool)
            pool.wait_ge(ctx.tables, 16 * len(ctx.table_loads))
            for r in range(KT // 2):
                ctx.shifts(pool, 0, r)
            ctx.rest_rows(pool, 0, 0)

        @block.vector
        def _(v):
            chain = Chain(v, chain_sem)

            def take(p):
                v.wait_ge(projected, p + 1)
                v.tensor_scalar(qT[:, p, :], qps[:, p % 2, :], DH ** -0.5, None, ALU.mult).then_inc(taken, 1)

            norm_stats(v, chain, n, g.x_tok, TT)
            chain(norm_apply(v, chain, n, 1, g.x_tok, y, TT))
            norm_stats(v, chain, n, y, TT)
            chain(norm_apply(v, chain, n, 2, y, z, TT))
            v.wait_ge(g_loaded, 32)
            for t in range(TT):
                last = v.tensor_tensor(z[:, t, :], z[:, t, :], gain_sb[:, :], ALU.mult)
            chain(last)
            for t in range(TT):
                v.tensor_tensor(z[:, t, :], z[:, t, :], shift_sb[:, :], ALU.add).then_inc(latents, 1)
            if layer == 0:
                ctx.statistics(v, chain, 0)
                ctx.scales(v, chain, 0)
            else:
                ctx.apply_vector(v, 0)
            for p in range(PAIRS - 3):
                take(p)
            if layer == 0:
                v.wait_ge(wk_hi, 1)
                v.tensor_tensor(wk.lo[:, :, :], wk.staged, wk.hi[:, :, :].bitcast(F32), ALU.subtract)
            for r in range(ctx.rounds):
                ctx.rest_turned(v, 0, 0, r)
                if r < 3:
                    take(PAIRS - 3 + r)

        @block.scalar
        def _(a):
            norm_root(a, n, 1)
            norm_root(a, n, 2)
            if layer == 0:
                norm_root(a, ctx.n, 1)
            for k in range(KD):
                a.wait_ge(turned, k + 1)
                a.activation(zT[:, k, :], tps[:, k, :], ACT.Copy).then_inc(turned_copied, 1)
            if layer == 0:
                ctx.apply_scalar(a, 0)
                a.wait_ge(wk_loaded, 16)
                a.activation(wk.hi[:, :, :], wk.staged, ACT.Copy).then_inc(wk_hi, 1)
            for r in range(ctx.rounds):
                ctx.leading_turned(a, 0, 0, r)
                if r == layer + 1:
                    ctx.leading_rows(a, 0, 0)

        @block.tensor
        def _(pe):
            for k in range(KD):
                for t in range(TT):
                    if k == 0:
                        pe.wait_ge(latents, t + 1)
                    last = pe.transpose(tps[:, k, t * P:(t + 1) * P], z[:, t, k * P:(k + 1) * P], g.ident[:, :])
                last.then_inc(turned, 1)
            pe.wait_ge(turned_copied, KD)
            pe.wait_ge(w_loaded, 16)
            for p in range(PAIRS):
                if p >= 2:
                    pe.wait_ge(taken, p - 1)
                for k in range(KD):
                    last = pe.matmul(qps[:, p % 2, :], w[:, k, p * P:(p + 1) * P], zT[:, k, :],
                                     start=(k == 0), stop=(k == KD - 1))
                last.then_inc(projected, 1)
                if p >= PAIRS - 4:
                    ctx.turn(pe, 0, p - (PAIRS - 4))
            for r in range(4, ctx.rounds):
                ctx.turn(pe, 0, r)


def pipelined(engine, step, lead, steps, chain=None, per_iteration=0):
    for j in range(lead):
        step(0, j)
    before = chain.n if chain else 0
    with engine.Fori(0, ITERS - 1) as it:
        if chain:
            chain.enter(it, per_iteration)
        for j in range(lead, lead + steps):
            step(it, j)
        if chain:
            chain.leave(before, per_iteration, ITERS - 1)
    for j in range(lead, lead + steps):
        step(ITERS - 1, j)


def there(it, j):
    return not isinstance(it, int) or 0 <= STEPS * it + j < B * PAIRS


def need(engine, sem, value):
    if not isinstance(value, int) or value > 0:
        engine.wait_ge(sem, value)


def three(pe, out, left, right, start, stop):
    (lh, ll), (rh, rl) = left, right
    pe.matmul(out, lh, rh, start=start, stop=False)
    pe.matmul(out, lh, rl, start=False, stop=False)
    return pe.matmul(out, ll, rh, start=False, stop=stop)


def settled(sp, value):
    return value if isinstance(value, int) else sp.snap(value)


class Context:

    def __init__(self, g, i, layer, sc):
        self.g, self.i, self.layer = g, i, layer
        self.tiles = tiles = KT + layer
        self.first = layer
        self.rounds = KT // 2 + layer
        self.raw = sc.sb("raw", [P, tiles, D])
        self.gain, self.shift = sc.sb("gain", [P, D]), sc.sb("shift", [P, D])
        self.table_loads = [(self.gain[:, :], i.l0_ctx_g if layer == 0 else i.l1_ctx_g),
                            (self.shift[:, :], i.l0_ctx_b if layer == 0 else i.l1_ctx_b)]
        self.hi, self.lo = ([sc.sb(f"ctx_{k}{u}", [P, tiles, D + 2], F32R) for u in range(2)] for k in ("hi", "lo"))
        self.hiT, self.loT = ([sc.sb(f"ctxT_{k}{u}", [P, KD, tiles * P], F32R) for u in range(2)] for k in ("hi", "lo"))
        self.tps = sc.ps("tps", [P, KD, 2 * P])
        if layer == 0:
            self.n, self.offset, self.scaled = norm_tensors(sc, "n", KT), sc.sb("offset", [P, KT]), sc.sem("scaled")
        self.loaded, self.tables = sc.sem("ctx_loaded"), sc.sem("tables_loaded")
        self.lat_loaded = sc.sem("lat_loaded")
        self.empty, self.applied, self.affine = sc.sem("empty"), sc.sem("applied"), sc.sem("affine")
        self.turned, self.turned_hi, self.turned_lo = sc.sem("turned"), sc.sem("turned_hi"), sc.sem("turned_lo")
        self.gained = sc.sem("gained")
        self.rows_hi, self.rows_lo = sc.sem("rows_hi"), sc.sem("rows_lo")

    def load(self, sp, nth, latents=True):
        need(sp, self.turned, self.rounds * nth)
        need(sp, self.rows_lo, nth)
        sp.dma_start(self.raw[:, self.first:, :], self.i.ctx[nth].rearrange("(p k) d -> p k d", k=KT)).then_inc(self.loaded, 16)
        if self.layer and latents:
            self.load_latents(sp, nth)

    def load_latents(self, sp, nth):
        sp.dma_start(self.raw[0:N, 0, :], self.g.lat[nth]).then_inc(self.lat_loaded, 16)

    def wait_loaded(self, engine, nth):
        engine.wait_ge(self.loaded, 16 * (nth + 1))

    def constants(self, pool):
        for u in range(2):
            pool.memset(self.hi[u][:, :, D:D + 2].bitcast(F32), 1.0)
            last = pool.memset(self.lo[u][:, :, D:D + 2].bitcast(F32), 0.0)
        last.then_inc(self.empty, 1)
        pool.wait_ge(self.empty, 1)
        if self.layer:
            pool.memset(self.raw[N:P, 0, :], 0.0).then_inc(self.empty, 1)
            pool.wait_ge(self.empty, 2)

    def statistics(self, v, chain, nth):
        self.wait_loaded(v, nth)
        norm_stats(v, chain, self.n, self.raw, KT)

    def scales(self, v, chain, nth):
        n = self.n
        v.wait_ge(n.std_ready, nth + 1)
        chain(v.reciprocal(n.rstd[:, :], n.std[:, :]))
        v.tensor_copy(self.g.ctx_mean[:, nth, :], n.mean[:, :])
        v.tensor_copy(self.g.ctx_rstd[:, nth, :], n.rstd[:, :])
        v.scalar_tensor_tensor(out=self.offset[:, :], in0=n.mean[:, :], scalar=-1.0, in1=n.rstd[:, :],
                               op0=ALU.mult, op1=ALU.mult).then_inc(self.scaled, 1)

    def apply_scalar(self, a, nth):
        a.wait_ge(self.scaled, nth + 1)
        for t in range(KT):
            last = a.activation(self.raw[:, t, :], self.raw[:, t, :], ACT.Identity, scale=self.n.rstd[:, t:t + 1],
                                bias=self.offset[:, t:t + 1])
        last.then_inc(self.applied, 1)

    def apply_vector(self, v, nth):
        self.wait_loaded(v, nth)
        mean, rstd = self.g.ctx_mean[:, nth, :], self.g.ctx_rstd[:, nth, :]
        for t in range(KT):
            tile = self.raw[:, self.first + t, :]
            last = v.tensor_scalar(tile, tile, mean[:, t:t + 1], rstd[:, t:t + 1], ALU.subtract, ALU.mult)
        last.then_inc(self.applied, 1)

    def shifts(self, pool, nth, r):
        wide, tiles = [P, 2, D], self.raw[:, self.first + 2 * r:self.first + 2 * r + 2, :]
        pool.wait_ge(self.applied, nth + 1)
        pool.tensor_tensor(tiles, tiles, self.gain[:, None, :].to_broadcast(wide), ALU.mult).then_inc(self.gained, 1)
        pool.wait_ge(self.gained, (KT // 2) * nth + r + 1)
        pool.tensor_tensor(tiles, tiles, self.shift[:, None, :].to_broadcast(wide), ALU.add).then_inc(self.affine, 1)

    def leading_rows(self, a, nth, u):
        a.wait_ge(self.affine, (KT // 2) * (nth + 1))
        if self.layer:
            a.wait_ge(self.lat_loaded, 16 * (nth + 1))
        a.activation(self.hi[u][:, :, 0:D], self.raw[:, :, :], ACT.Copy).then_inc(self.rows_hi, 1)

    def rest_rows(self, pool, nth, u):
        pool.wait_ge(self.rows_hi, nth + 1)
        pool.tensor_tensor(self.lo[u][:, :, 0:D], self.raw[:, :, :], self.hi[u][:, :, 0:D].bitcast(F32),
                           ALU.subtract).then_inc(self.rows_lo, 1)

    def turned_tiles(self, r):
        start = self.first + 2 * (r - self.first)
        return range(max(start, 0), start + 2)

    def turn(self, pe, nth, r):
        if r < self.first:
            pe.wait_ge(self.lat_loaded, 16 * (nth + 1))
        else:
            pe.wait_ge(self.affine, (KT // 2) * nth + r - self.first + 1)
        need(pe, self.turned_lo, self.rounds * nth + r)
        for k in range(KD):
            for c, t in enumerate(self.turned_tiles(r)):
                last = pe.transpose(self.tps[:, k, c * P:c * P + P], self.raw[:, t, k * P:(k + 1) * P],
                                    self.g.ident[:, :])
        last.then_inc(self.turned, 1)

    def turned_cols(self, r):
        tiles = self.turned_tiles(r)
        return slice(tiles[0] * P, (tiles[-1] + 1) * P), self.tps[:, :, 0:len(tiles) * P]

    def leading_turned(self, a, nth, u, r):
        cols, of = self.turned_cols(r)
        a.wait_ge(self.turned, self.rounds * nth + r + 1)
        a.activation(self.hiT[u][:, :, cols], of, ACT.Copy).then_inc(self.turned_hi, 1)

    def rest_turned(self, v, nth, u, r):
        cols, of = self.turned_cols(r)
        v.wait_ge(self.turned_hi, self.rounds * nth + r + 1)
        v.tensor_tensor(self.loT[u][:, :, cols], of, self.hiT[u][:, :, cols].bitcast(F32),
                        ALU.subtract).then_inc(self.turned_lo, 1)


class Weighted:

    def __init__(self, g, sc, ctx, wv, uT, uTps, zps):
        self.g, self.ctx, self.wv, self.uT, self.uTps, self.zps = g, ctx, wv, uT, uTps, zps
        self.zT = g.zT
        tiles = ctx.tiles
        self.ph, self.pl = ([sc.sb(f"p{k}{u}", [P, tiles, P], F32R) for u in range(2)] for k in "hl")
        self.inv = sc.sb("inv", [P, 2])
        self.un = [sc.sb(f"un{u}", [P, D]) for u in range(2)]
        self.ups = sc.ps("ups", [P, 512])
        self.exped, self.led, self.rested = sc.sem("exped"), sc.sem("led"), sc.sem("rested")
        self.summed, self.inverted, self.normed = sc.sem("summed"), sc.sem("inverted"), sc.sem("normed")
        self.sumsT, self.sumsT_copied = sc.sem("sumsT"), sc.sem("sumsT_copied")
        self.valued, self.valued_copied = sc.sem("valued"), sc.sem("valued_copied")

    def exp(self, a, pr, ready, it, j):
        e = it * STEPS + j
        a.wait_ge(ready, e + 1)
        a.activation(pr[:, :, :], pr[:, :, :], ACT.Exp).then_inc(self.exped, 1)
        need(a, self.summed, e - 1)
        a.wait_ge(self.exped, e + 1)
        a.activation(self.ph[j % 2][:, :, :], pr[:, :, :], ACT.Copy).then_inc(self.led, 1)

    def rest(self, engine, pr, it, j):
        engine.wait_ge(self.led, it * STEPS + j + 1)
        engine.tensor_tensor(self.pl[j % 2][:, :, :], pr[:, :, :], self.ph[j % 2][:, :, :].bitcast(F32),
                             ALU.subtract).then_inc(self.rested, 1)

    def sums(self, pe, it, j):
        e, u, ctx = it * STEPS + j, j // PAIRS % 2, self.ctx
        pe.wait_ge(self.rested, e + 1)
        need(pe, self.normed, e)
        if j % PAIRS == 0:
            pe.wait_ge(ctx.rows_lo, it * 2 + j // PAIRS + 1)
        for kt in range(ctx.tiles):
            last = three(pe, self.ups[:, 0:D + 2], (self.ph[j % 2][:, kt, :], self.pl[j % 2][:, kt, :]),
                         (ctx.hi[u][:, kt, :], ctx.lo[u][:, kt, :]), kt == 0, kt == ctx.tiles - 1)
        last.then_inc(self.summed, 1)

    def invert(self, v, it, j):
        e = it * STEPS + j
        v.wait_ge(self.summed, e + 1)
        need(v, self.normed, e - 1)
        v.reciprocal(self.inv[:, j % 2:j % 2 + 1], self.ups[:, D:D + 1]).then_inc(self.inverted, 1)

    def normalise(self, a, it, j):
        e = it * STEPS + j
        a.wait_ge(self.inverted, e + 1)
        need(a, self.sumsT, e - 1)
        a.activation(self.un[j % 2][:, :], self.ups[:, 0:D], ACT.Copy, scale=self.inv[:, j % 2:j % 2 + 1]).then_inc(self.normed, 1)

    def turn_sums(self, pe, it, first, count):
        e = it * STEPS + first
        pe.wait_ge(self.normed, e + count)
        need(pe, self.sumsT_copied, e)
        for c in range(count):
            for k in range(KD):
                last = pe.transpose(self.uTps[:, c, k, :], self.un[(first + c) % 2][:, k * P:(k + 1) * P], self.g.ident[:, :])
        last.then_inc(self.sumsT, count)

    def copy_sumsT(self, a, it, first, count):
        e = it * STEPS + first
        a.wait_ge(self.sumsT, e + count)
        need(a, self.valued, e - count * (len(self.uT) - 1))
        a.activation(self.uT[first // count % len(self.uT)][:, :, :, :], self.uTps, ACT.Copy).then_inc(self.sumsT_copied, count)

    def values(self, pe, it, first, count):
        e = it * STEPS + first
        pe.wait_ge(self.sumsT_copied, e + count)
        need(pe, self.valued_copied, e)
        for c in range(count):
            p = (first + c) % PAIRS
            for k in range(KD):
                last = pe.matmul(self.zps[:, c, :], self.wv[:, k, p * P:(p + 1) * P],
                                 self.uT[first // count % len(self.uT)][:, c, k, :], start=(k == 0), stop=(k == KD - 1))
        last.then_inc(self.valued, count)

    def copy_values(self, a, it, first, count):
        zTb, p = self.zT[:, :, :].rearrange("p h (b n) -> p h b n", n=N), first % PAIRS
        a.wait_ge(self.valued, it * STEPS + first + count)
        for half in range(2):
            part = slice(DH * half, DH * half + DH)
            last = a.activation(zTb[part, p:p + count, it * 2 + first // PAIRS, :],
                                self.zps[part, :, half * N:half * N + N], ACT.Copy)
        last.then_inc(self.valued_copied, count)


def load_blocks(sp, g, qd, loaded, scored, nth):
    need(sp, scored, PAIRS * (nth - 1))
    of = g.q.rearrange("p h (b n) -> p h b n", n=N)
    for half in range(2):
        part = slice(DH * half, DH * half + DH)
        sp.dma_start(qd[part, :, half * N:half * N + N], of[part, :, nth, :]).then_inc(loaded, 16)


def phase_cross0(nc, g, i, ctx, wk):
    CLIP, LAST = 11.0, 3
    with Scope(nc, "c0") as sc:
        wv = sc.sb("wv", [P, KD, H * DH])
        cos, sin = sc.sb("cos", [P, S]), sc.sb("sin", [P, S])
        qd = [sc.sb(f"qd{u}", [P, PAIRS, P]) for u in range(2)]
        kc, ks, kr = ([sc.sb(f"{k}{u}", [P, S]) for u in range(2)] for k in ("kc", "ks", "kr"))
        pr = sc.sb("pr", [P, KT, P])
        kps = sc.ps("kps", [P, S])
        sps = sc.ps("sps", [P, KT, P])
        uTb, zb = sc.ps("uTb", [P, 512]), sc.ps("zb", [P, 512])
        uT = [sc.sb(f"uT{u}", [P, 1, KD, P]) for u in range(2)]
        w = Weighted(g, sc, ctx, wv, uT, uTb[:, 0:KD * P].rearrange("p (c k q) -> p c k q", c=1, k=KD),
                     zb[:, 0:P].rearrange("p (c q) -> p c q", c=1))
        s = Names(**{name: sc.sem(name) for name in (
            "wv_loaded rope_loaded chain zeroed keys multiplied roped scored clipped").split()})
        swapped = [sc.sem(f"swapped{u}") for u in range(2)]
        blocks_loaded = [sc.sem(f"blocks_loaded{u}") for u in range(2)]
        block = sc.block()

        @block.sync
        def _(sp):
            def blocks(nth, u):
                load_blocks(sp, g, qd[u], blocks_loaded[u], s.scored, nth)

            def swap(it, j):
                sp.wait_ge(s.multiplied, it * STEPS + j + 1)
                for c in range(4):
                    to, of = 32 * c, 32 * (c ^ 1)
                    sp.dma_start(kr[j % 2][to:to + 32, :], ks[j % 2][of:of + 32, :]).then_inc(swapped[j % 2], 16)

            def step(it, j):
                batch, p = j // PAIRS, j % PAIRS
                if p == 1 and there(it, j + PAIRS):
                    blocks(settled(sp, it * 2 + batch + 1), (batch + 1) % 2)
                if p == 6 and there(it, j + 2 * PAIRS):
                    ctx.load(sp, settled(sp, it * 2 + batch + 2))
                if there(it, j + 2):
                    swap(it, j + 2)

            sp.dma_start(cos[:, :], i.l0_cos).then_inc(s.rope_loaded, 16)
            sp.dma_start(sin[:, :], i.l0_sin).then_inc(s.rope_loaded, 16)
            sp.wait_ge(s.zeroed, 1)
            blocks(0, 0)
            sp.dma_start(wv[:, :, :], rows(i.l0_wv)).then_inc(s.wv_loaded, 16)
            ctx.load(sp, 1)
            swap(0, 0)
            swap(0, 1)
            pipelined(sp, step, LAST, STEPS)

        @block.gpsimd
        def _(pool):
            for u in range(2):
                last = pool.memset(qd[u][:, :, :], 0.0)
            last.then_inc(s.zeroed, 1)

            def prepare(nth, u):
                for r in range(KT // 2):
                    ctx.shifts(pool, nth, r)
                ctx.rest_rows(pool, nth, u)

            prepare(1, 1)
            with pool.Fori(0, ITERS - 1) as it:
                for u in range(2):
                    prepare(it * 2 + 2 + u, u)

        @block.vector
        def _(v):
            chain = Chain(v, s.chain)

            def multiply(it, j):
                v.wait_ge(s.keys, it * STEPS + j + 1)
                need(v, s.scored, it * STEPS + j - 1)
                v.tensor_tensor(kc[j % 2][:, :], kps[:, :], cos[:, :], ALU.mult)
                v.tensor_tensor(ks[j % 2][:, :], kps[:, :], sin[:, :], ALU.mult).then_inc(s.multiplied, 1)

            def rope(it, j):
                v.wait_ge(swapped[j % 2], (it * (STEPS // 2) + j // 2 + 1) * 64)
                v.tensor_tensor(kc[j % 2][:, :], kc[j % 2][:, :], kr[j % 2][:, :], ALU.add).then_inc(s.roped, 1)

            def clip(it, j):
                v.wait_ge(s.scored, it * STEPS + j + 1)
                need(v, w.rested, it * STEPS + j)
                v.tensor_scalar(pr[:, :, :], sps[:, :, :], CLIP, -CLIP, ALU.min, ALU.max).then_inc(s.clipped, 1)

            def step(it, j):
                nth, u, p = it * 2 + j // PAIRS + 1, (j // PAIRS + 1) % 2, j % PAIRS
                more = there(it, j + PAIRS)
                if there(it, j - 2):
                    w.invert(v, it, j - 2)
                if there(it, j):
                    clip(it, j)
                if there(it, j + 1):
                    rope(it, j + 1)
                if p == 0 and more:
                    ctx.statistics(v, chain, nth)
                if there(it, j + 2):
                    multiply(it, j + 2)
                if p == 0 and more:
                    ctx.scales(v, chain, nth)
                if there(it, j):
                    w.rest(v, pr, it, j)
                if 2 <= p <= 5 and more:
                    ctx.rest_turned(v, nth, u, p - 2)

            v.wait_ge(s.rope_loaded, 32)
            for c in (1, 3):
                part = slice(32 * c, 32 * c + 32)
                last = v.tensor_scalar(sin[part, :], sin[part, :], -1.0, None, ALU.mult)
            chain(last)
            multiply(0, 0)
            multiply(0, 1)
            rope(0, 0)
            pipelined(v, step, LAST, STEPS, chain, 2 * 4)

        @block.scalar
        def _(a):
            def step(it, j):
                nth, u, p = it * 2 + j // PAIRS + 1, (j // PAIRS + 1) % 2, j % PAIRS
                more = there(it, j + PAIRS)
                if there(it, j - 2):
                    w.normalise(a, it, j - 2)
                if there(it, j):
                    w.exp(a, pr, s.clipped, it, j)
                if p == 0 and more:
                    norm_root(a, ctx.n, nth + 1)
                if p == 1 and more:
                    ctx.apply_scalar(a, nth)
                if there(it, j - 2):
                    w.copy_sumsT(a, it, j - 2, 1)
                if there(it, j - 3):
                    w.copy_values(a, it, j - 3, 1)
                if 2 <= p <= 5 and more:
                    ctx.leading_turned(a, nth, u, p - 2)
                if p == 4 and more:
                    ctx.leading_rows(a, nth, u)

            pipelined(a, step, LAST, STEPS)

        @block.tensor
        def _(pe):
            def keys(it, j):
                e, u, p = it * STEPS + j, j // PAIRS % 2, j % PAIRS
                if p == 0:
                    pe.wait_ge(ctx.turned_lo, (it * 2 + j // PAIRS + 1) * ctx.rounds)
                need(pe, s.multiplied, e)
                cols = slice(p * P, (p + 1) * P)
                for half in range(2):
                    part = slice(half * 512, half * 512 + 512)
                    for k in range(KD):
                        last = three(pe, kps[:, part], (wk.hi[:, k, cols], wk.lo[:, k, cols]),
                                     (ctx.hiT[u][:, k, part], ctx.loT[u][:, k, part]), k == 0, k == KD - 1)
                last.then_inc(s.keys, 1)

            def scores(it, j):
                e, u, p = it * STEPS + j, j // PAIRS % 2, j % PAIRS
                if p == 0:
                    pe.wait_ge(blocks_loaded[u], (it + j // STEPS + 1) * 32)
                pe.wait_ge(s.roped, e + 1)
                need(pe, s.clipped, e)
                for kt in range(KT):
                    last = pe.matmul(sps[:, kt, :], kc[j % 2][:, kt * P:kt * P + P], qd[u][:, p, :], start=True, stop=True)
                last.then_inc(s.scored, 1)

            def step(it, j):
                nth, p = it * 2 + j // PAIRS + 1, j % PAIRS
                if there(it, j):
                    scores(it, j)
                if there(it, j + 2):
                    keys(it, j + 2)
                if there(it, j - 2):
                    w.turn_sums(pe, it, j - 2, 1)
                if there(it, j - 3):
                    w.values(pe, it, j - 3, 1)
                if 2 <= p <= 5 and there(it, j + PAIRS):
                    ctx.turn(pe, nth, p - 2)
                if there(it, j - 1):
                    w.sums(pe, it, j - 1)

            keys(0, 0)
            keys(0, 1)
            pe.wait_ge(s.wv_loaded, 16)
            pipelined(pe, step, LAST, STEPS)


def phase_out0(nc, g, i):
    with Scope(nc, "o0") as sc:
        wo, bo = sc.sb("wo", [P, PAIRS, D]), sc.sb("bo", [P, D])
        ops = sc.ps("ops", [P, TT, 512])
        loaded, biased, out_done = sc.sem("loaded"), sc.sem("biased"), sc.sem("out_done")
        block = sc.block()

        @block.sync
        def _(sp):
            sp.dma_start(wo[:, :, :], rows(i.l0_wo)).then_inc(loaded, 16)
            sp.dma_start(bo[:, :], i.l0_bo).then_inc(loaded, 16)

        @block.vector
        def _(v):
            v.wait_ge(loaded, 32)
            v.tensor_tensor(g.x_tok[:, :, :], g.x_tok[:, :, :], bo[:, None, :].to_broadcast([P, TT, D]),
                            ALU.add).then_inc(biased, 1)
            v.wait_ge(biased, 1)
            for t in range(TT):
                v.wait_ge(out_done, t + 1)
                v.tensor_tensor(g.x_tok[:, t, :], g.x_tok[:, t, :], ops[:, t, 0:D], ALU.add)

        @block.tensor
        def _(pe):
            pe.wait_ge(loaded, 32)
            for t in range(TT):
                for p in range(PAIRS):
                    last = pe.matmul(ops[:, t, 0:D], g.zT[:, p, t * P:(t + 1) * P], wo[:, p, :],
                                     start=(p == 0), stop=(p == PAIRS - 1))
                last.then_inc(out_done, 1)


def turned_norm(sc, name):
    m = Names(y=sc.sb(f"{name}_y", [P, TT, D]), yT=sc.sb(f"{name}_yT", [P, KD, T]))
    m.n = norm_tensors(sc, name, TT)
    m.tps = [sc.ps(f"{name}_tps{k}", [P, T]) for k in range(KD)]
    m.normed, m.turned, m.copied = (sc.sem(f"{name}_{k}") for k in ("normed", "turned", "copied"))
    return m


def turned_norm_vector(v, chain, m, x):
    norm_stats(v, chain, m.n, x, TT)
    norm_apply(v, chain, m.n, 1, x, m.y, TT).then_inc(m.normed, 1)


def turned_norm_scalar(a, m):
    norm_root(a, m.n, 1)
    for k in range(KD):
        a.wait_ge(m.turned, k + 1)
        a.activation(m.yT[:, k, :], m.tps[k][:, :], ACT.Copy).then_inc(m.copied, 1)


def turned_norm_tensor(pe, g, m):
    pe.wait_ge(m.normed, 1)
    for k in range(KD):
        for t in range(TT):
            last = pe.transpose(m.tps[k][:, t * P:(t + 1) * P], m.y[:, t, k * P:(k + 1) * P], g.ident[:, :])
        last.then_inc(m.turned, 1)


def phase_attn0(nc, g, i):
    HS, HH = 16, 8
    UNITS = TT * 2
    C4 = 2 * D // P
    G4 = HH // 2
    with Scope(nc, "a0") as sc:
        wqk = sc.sb("wqk", [P, 4, KD, D])
        wv, wc = sc.sb("wv", [P, KD, 2 * D]), sc.sb("wc", [P, C4, D])
        causal, heads = sc.sb("causal", [P, N]), sc.sb("heads", [P, HH])
        lqk, lamp, lams, lam = sc.sb("lqk", [P, 4, H]), sc.sb("lamp", [P, 2, H]), sc.sb("lams", [P, 2, H]), sc.sb("lam", [P, H])
        chan, ga, gb = sc.sb("chan", [P, 3]), sc.sb("ga", [P, 2]), sc.sb("gb", [P, 1])
        m = turned_norm(sc, "m")
        yT2 = sc.sb("yT2", [P, KD, B, 2, N])
        qkT = sc.sb("qkT", [P, 4, 2, T])
        vd = sc.sb("vd", [P, B, PAIRS, 2 * 32])
        kd = [sc.sb(f"kd{u}", [P, 2, HH, N]) for u in range(4)]
        sm = [sc.sb(f"sm{u}", [P, 2, HH, N]) for u in range(2)]
        mx, su, rs = sc.sb("mx", [P, 2, HH]), sc.sb("su", [P, 2, HH]), sc.sb("rs", [P, 2, HH])
        att = [sc.sb(f"att{u}", [P, HH, N]) for u in range(2)]
        attT = [sc.sb(f"attT{u}", [P, G4, P]) for u in range(2)]
        y4, cen, sq = sc.sb("y4", [P, C4, T]), sc.sb("cen", [P, C4, T]), sc.sb("sq", [P, C4, T])
        gm, gv, gs, gr = (sc.sb(k, [P, C4 * B]) for k in ("gm", "gv", "gs", "gr"))
        sps = [sc.ps(f"sps{u}", [P, 2, HH, N]) for u in range(2)]
        aps, yps = sc.ps("aps", [P, G4, P]), sc.ps("yps", [P, 512])
        pps = [sps[0][:, a, :, :].rearrange("p h n -> p (h n)") for a in range(2)]
        s = Names(**{name: sc.sem(name) for name in (
            "w_loaded c_loaded wc_loaded twice chain pool_chain zeroed lam_in lam_out projected taken keyed keyed_pool scored shifted "
            "exped mixed attT attT_copied valued valued_copied sq_in sq_out gvar gstd gnormed out_done").split()})
        block = sc.block()

        @block.sync
        def _(sp):
            sp.dma_start(lqk[:, :, :], i.a0_lqk).then_inc(s.c_loaded, 16)
            sp.dma_start(chan[:, :], i.a0_chan).then_inc(s.c_loaded, 16)
            sp.dma_start(causal[:, :], i.causal).then_inc(s.c_loaded, 16)
            sp.dma_start(heads[:, :], i.heads).then_inc(s.c_loaded, 16)
            sp.dma_start(wqk[:, :, :, :], i.a0_wqk.rearrange("w (k p) n -> p w k n", p=P)).then_inc(s.w_loaded, 16)
            sp.dma_start(wv[:, :, :], rows(i.a0_wv)).then_inc(s.w_loaded, 16)
            sp.dma_start(wc[:, :, :], rows(i.a0_wc)).then_inc(s.wc_loaded, 16)

        def build_keys(engine, chain, unit, a):
            t, hh = unit // 2, unit % 2
            k = qkT[:, 2 + a, hh, t * P:(t + 1) * P].rearrange("p (b n) -> p b n", n=N)
            for b in range(2):
                last = engine.tensor_tensor(kd[unit % 2 * 2 + a][:, b, :, :], k[:, b, None, :].to_broadcast([P, HH, N]),
                                            heads[:, :, None].to_broadcast([P, HH, N]), ALU.mult)
            return last

        @block.gpsimd
        def _(pool):
            chain = Chain(pool, s.pool_chain)
            pool.memset(vd[:, :, :, :], 0.0).then_inc(s.zeroed, 1)
            pool.wait_ge(s.c_loaded, 64)
            pool.wait_ge(s.taken, 8)
            for unit in range(UNITS):
                if unit >= 2:
                    pool.wait_ge(s.scored, unit - 1)
                build_keys(pool, chain, unit, 1).then_inc(s.keyed_pool, 1)

        @block.vector
        def _(v):
            chain = Chain(v, s.chain)
            turned_norm_vector(v, chain, m, g.x_tok)
            v.wait_ge(s.c_loaded, 64)
            v.tensor_tensor(lamp[:, :, :], lqk[:, 0:2, :], lqk[:, 2:4, :], ALU.mult).then_inc(s.lam_in, 1)
            v.tensor_scalar(ga[:, :], chan[:, 0:2], chan[:, 2:3], 1.0 - LAMBDA_INIT, ALU.mult, ALU.mult)
            v.wait_ge(s.lam_out, 1)
            chain(v.tensor_tensor(lam[:, :], lams[:, 0, :], lams[:, 1, :], ALU.subtract))
            chain(v.tensor_scalar(lam[:, :], lam[:, :], LAMBDA_INIT, None, ALU.add))
            v.wait_ge(s.zeroed, 1)
            for b in range(B):
                v.wait_ge(s.projected, 8 + b + 1)
                src = pps[b % 2].rearrange("p (h c e) -> p h c e", c=2, e=32)
                for c in range(2):
                    part = slice(N * c, N * c + N)
                    last = v.tensor_copy(vd[part, b, :, 32 * c:32 * c + 32], src[part, :, c, :])
                last.then_inc(s.taken, 1)

            def shift(unit):
                v.wait_ge(s.scored, unit + 1)
                if unit >= 2:
                    v.wait_ge(s.mixed, unit - 1)
                to = sm[unit % 2]
                for a in range(2):
                    last = v.scalar_tensor_tensor(out=to[:, a, :, :], in0=sps[unit % 2][:, a, :, :], scalar=HS ** -0.5,
                                                  in1=causal[:, None, :].to_broadcast([P, HH, N]), op0=ALU.mult, op1=ALU.add)
                chain(last)
                chain(v.tensor_reduce(mx[:, :, :], to[:, :, :, :], AX.X, ALU.max))
                v.tensor_tensor(to[:, :, :, :], to[:, :, :, :], mx[:, :, :, None].to_broadcast([P, 2, HH, N]),
                                ALU.subtract).then_inc(s.shifted, 1)

            def mix(unit):
                hh = unit % 2
                v.wait_ge(s.exped, unit + 1)
                of = sm[unit % 2]
                chain(v.tensor_reduce(su[:, :, :], of[:, :, :, :], AX.X, ALU.add))
                chain(v.reciprocal(rs[:, :, :], su[:, :, :]))
                chain(v.tensor_tensor(rs[:, 1, :], rs[:, 1, :], lam[:, hh * HH:hh * HH + HH], ALU.mult))
                chain(v.tensor_tensor(of[:, :, :, :], of[:, :, :, :], rs[:, :, :, None].to_broadcast([P, 2, HH, N]), ALU.mult))
                if unit >= 2:
                    v.wait_ge(s.attT, unit - 1)
                v.tensor_tensor(att[unit % 2][:, :, :], of[:, 0, :, :], of[:, 1, :, :], ALU.subtract).then_inc(s.mixed, 1)

            for unit in range(UNITS + 1):
                if unit < UNITS:
                    if unit >= 2:
                        v.wait_ge(s.scored, unit - 1)
                    build_keys(v, chain, unit, 0).then_inc(s.keyed, 1)
                    shift(unit)
                if unit >= 1:
                    mix(unit - 1)
            v.wait_ge(s.valued_copied, UNITS)
            wide = [P, C4 * B, N]
            yv, cv, qv = (t[:, :, :].rearrange("p c (b n) -> p (c b) n", n=N) for t in (y4, cen, sq))
            chain(v.tensor_reduce(gm[:, :], yv, AX.X, ALU.add))
            chain(v.tensor_scalar(gm[:, :], gm[:, :], 1.0 / N, None, ALU.mult))
            v.tensor_tensor(cv, yv, gm[:, :, None].to_broadcast(wide), ALU.subtract).then_inc(s.sq_in, 1)
            v.wait_ge(s.sq_out, 1)
            chain(v.tensor_reduce(gv[:, :], qv, AX.X, ALU.add))
            v.tensor_scalar(gv[:, :], gv[:, :], 1.0 / N, EPS, ALU.mult, ALU.add).then_inc(s.gvar, 1)
            v.wait_ge(s.gstd, 1)
            chain(v.reciprocal(gr[:, :], gs[:, :]))
            chain(v.tensor_tensor(cv, cv, gr[:, :, None].to_broadcast(wide), ALU.mult))
            v.tensor_scalar(cen[:, :, :], cen[:, :, :], ga[:, 0:1], ga[:, 1:2], ALU.mult, ALU.add).then_inc(s.gnormed, 1)
            for t in range(TT):
                v.wait_ge(s.out_done, t // 2 * 2 + 2)
                v.tensor_tensor(g.x_tok[:, t, :], g.x_tok[:, t, :], pps[t // 2][:, t % 2 * D:t % 2 * D + D], ALU.add)

        @block.scalar
        def _(a):
            turned_norm_scalar(a, m)
            for k in range(KD):
                a.activation(yT2[:, k, :, :, :], m.tps[k][:, :].rearrange("p (b n) -> p b n", n=N)[:, :, None, :]
                             .to_broadcast([P, B, 2, N]), ACT.Copy).then_inc(s.twice, 1)
            for c in range(8):
                a.wait_ge(s.projected, c + 1)
                a.activation(qkT[:, c // 2, c % 2, :], pps[c % 2], ACT.Copy).then_inc(s.taken, 1)
            a.wait_ge(s.lam_in, 1)
            a.activation(lams[:, :, :], lamp[:, :, :], ACT.Sigmoid).then_inc(s.lam_out, 1)
            for unit in range(UNITS + 3):
                if unit < UNITS:
                    a.wait_ge(s.shifted, unit + 1)
                    a.activation(sm[unit % 2][:, :, :, :], sm[unit % 2][:, :, :, :], ACT.Exp).then_inc(s.exped, 1)
                if 0 <= unit - 2 < UNITS:
                    w = unit - 2
                    a.wait_ge(s.attT, w + 1)
                    if w >= 2:
                        a.wait_ge(s.valued, w - 1)
                    a.activation(attT[w % 2][:, :, :], aps[:, :, :], ACT.Copy).then_inc(s.attT_copied, 1)
                if 0 <= unit - 3 < UNITS:
                    w = unit - 3
                    t, hh = w // 2, w % 2
                    a.wait_ge(s.valued, w + 1)
                    a.activation(y4[:, 2 * hh:2 * hh + 2, t * P:(t + 1) * P],
                                 yps[:, 0:2 * P].rearrange("p (c q) -> p c q", c=2), ACT.Copy).then_inc(s.valued_copied, 1)
            a.wait_ge(s.sq_in, 1)
            a.activation(sq[:, :, :], cen[:, :, :], ACT.Square).then_inc(s.sq_out, 1)
            a.wait_ge(s.gvar, 1)
            a.activation(gs[:, :], gv[:, :], ACT.Sqrt).then_inc(s.gstd, 1)

        @block.tensor
        def _(pe):
            turned_norm_tensor(pe, g, m)
            pe.wait_ge(m.copied, KD)
            pe.wait_ge(s.w_loaded, 32)
            for c in range(8 + B):
                if c == 8:
                    pe.wait_ge(s.twice, KD)
                if c >= 2:
                    pe.wait_ge(s.taken, c - 1)
                for k in range(KD):
                    if c < 8:
                        left, right = wqk[:, c // 2, k, c % 2 * P:c % 2 * P + P], m.yT[:, k, :]
                    else:
                        b = c - 8
                        left = yT2[:, k, b, :, :].rearrange("p c n -> p (c n)")
                        right = wv[:, k, :]
                    last = pe.matmul(pps[c % 2], left, right, start=(k == 0), stop=(k == KD - 1))
                last.then_inc(s.projected, 1)
            pe.wait_ge(s.taken, 8 + B)
            for unit in range(UNITS + 3):
                if unit < UNITS:
                    t, hh = unit // 2, unit % 2
                    pe.wait_ge(s.keyed, unit + 1)
                    pe.wait_ge(s.keyed_pool, unit + 1)
                    if unit >= 2:
                        pe.wait_ge(s.shifted, unit - 1)
                    for a in range(2):
                        for b in range(2):
                            q = qkT[:, a, hh, t * P + b * N:t * P + b * N + N]
                            last = pe.matmul(sps[unit % 2][b * N:b * N + N, a, :, :].rearrange("p h n -> p (h n)"), q,
                                             kd[unit % 2 * 2 + a][:, b, :, :].rearrange("p h n -> p (h n)"),
                                             start=True, stop=True)
                    last.then_inc(s.scored, 1)
                if 0 <= unit - 2 < UNITS:
                    w = unit - 2
                    pe.wait_ge(s.mixed, w + 1)
                    if w >= 1:
                        pe.wait_ge(s.attT_copied, w)
                    for c in range(G4):
                        last = pe.transpose(aps[:, c, :], att[w % 2][:, 2 * c:2 * c + 2, :].rearrange("p h n -> p (h n)"),
                                            g.ident[:, :])
                    last.then_inc(s.attT, 1)
                if 0 <= unit - 3 < UNITS:
                    w = unit - 3
                    t, hh = w // 2, w % 2
                    pe.wait_ge(s.attT_copied, w + 1)
                    if w >= 1:
                        pe.wait_ge(s.valued_copied, w)
                    for c in range(G4):
                        for b in range(2):
                            to = c // 2 * P + b * N
                            last = pe.matmul(yps[c % 2 * N:c % 2 * N + N, to:to + N], vd[:, 2 * t + b, hh * G4 + c, :],
                                             attT[w % 2][:, c, b * N:b * N + N], start=True, stop=True)
                    last.then_inc(s.valued, 1)
            pe.wait_ge(s.gnormed, 1)
            pe.wait_ge(s.wc_loaded, 16)
            for t in range(TT):
                for c in range(C4):
                    last = pe.matmul(pps[t // 2][:, t % 2 * D:t % 2 * D + D], cen[:, c, t * P:(t + 1) * P], wc[:, c, :],
                                     start=(c == 0), stop=(c == C4 - 1))
                last.then_inc(s.out_done, 1)


def phase_ffn0(nc, g, i):
    F = 1024
    M = F // P
    with Scope(nc, "f0") as sc:
        w1, w2 = sc.sb("w1", [P, KD, F]), sc.sb("w2", [P, KD, F])
        h1, h2 = sc.sb("h1", [P, M, F]), sc.sb("h2", [P, M, F])
        w3, w3s = sc.sb("w3", [P, M, D]), sc.sb("w3s", [P, D])
        sca = sc.sb("sca", [P, 4, M])
        m = turned_norm(sc, "m")
        gate = [sc.sb(f"gate{u}", [P, T]) for u in range(2)]
        ha, hb = sc.sb("ha", [P, M, T]), sc.sb("hb", [P, M, T])
        t3 = [sc.sb(f"t3{u}", [P, D]) for u in range(2)]
        gp = [sc.ps(f"gp{u}", [P, T]) for u in range(3)]
        up = [sc.ps(f"up{u}", [P, T]) for u in range(3)]
        s = Names(**{name: sc.sem(name) for name in (
            "w_loaded h1_loaded h2_loaded w3_loaded chain gated upped silued hidden square gelued out_done").split()})
        block = sc.block()

        @block.sync
        def _(sp):
            sp.dma_start(w1[:, :, :], rows(i.f0_w1)).then_inc(s.w_loaded, 16)
            sp.dma_start(w2[:, :, :], rows(i.f0_w2)).then_inc(s.w_loaded, 16)
            sp.dma_start(sca[:, :, :], i.f0_scales).then_inc(s.w_loaded, 16)
            sp.dma_start(h1[:, :, :], rows(i.f0_h1)).then_inc(s.h1_loaded, 16)
            sp.dma_start(h2[:, :, :], rows(i.f0_h2)).then_inc(s.h2_loaded, 16)
            sp.dma_start(w3[:, :, :], rows(i.f0_w3)).then_inc(s.w3_loaded, 16)
            sp.dma_start(w3s[:, :], i.f0_w3s).then_inc(s.w3_loaded, 16)

        @block.vector
        def _(v):
            chain = Chain(v, s.chain)
            turned_norm_vector(v, chain, m, g.x_tok)
            v.wait_ge(s.w_loaded, 48)
            for c in range(M):
                v.wait_ge(s.upped, c + 1)
                v.wait_ge(s.silued, c + 1)
                v.scalar_tensor_tensor(out=ha[:, c, :], in0=up[c % 3][:, :], scalar=sca[:, 1, c:c + 1],
                                       in1=gate[c % 2][:, :], op0=ALU.mult, op1=ALU.mult).then_inc(s.hidden, 1)
            v.wait_ge(s.w3_loaded, 32)
            for t in range(TT):
                v.wait_ge(s.out_done, t + 1)
                chain(v.tensor_tensor(t3[t % 2][:, :], up[t % 2][:, 0:D], w3s[:, :], ALU.mult))
                v.tensor_tensor(g.x_tok[:, t, :], g.x_tok[:, t, :], t3[t % 2][:, :], ALU.add)
            v.sem_inc(s.chain, 1)

        @block.scalar
        def _(a):
            turned_norm_scalar(a, m)
            a.wait_ge(s.w_loaded, 48)
            for c in range(M):
                a.wait_ge(s.gated, c + 1)
                if c >= 2:
                    a.wait_ge(s.hidden, c - 1)
                a.activation(gate[c % 2][:, :], gp[c % 3][:, :], ACT.Silu, scale=sca[:, 0, c:c + 1]).then_inc(s.silued, 1)
            for layer in range(2):
                for c in range(M):
                    nth = layer * M + c
                    a.wait_ge(s.square, nth + 1)
                    a.activation((hb, ha)[layer][:, c, :], gp[nth % 3][:, :], ACT.Gelu,
                                 scale=sca[:, 2 + layer, c:c + 1]).then_inc(s.gelued, 1)

        @block.tensor
        def _(pe):
            turned_norm_tensor(pe, g, m)
            pe.wait_ge(m.copied, KD)
            pe.wait_ge(s.w_loaded, 48)
            for c in range(M):
                for w, ps, done, free in ((w1, gp, s.gated, s.silued), (w2, up, s.upped, s.hidden)):
                    if c >= 3:
                        pe.wait_ge(free, c - 2)
                    for k in range(KD):
                        last = pe.matmul(ps[c % 3][:, :], w[:, k, c * P:(c + 1) * P], m.yT[:, k, :],
                                         start=(k == 0), stop=(k == KD - 1))
                    last.then_inc(done, 1)
            pe.wait_ge(s.silued, M)
            for layer, (w, src, loaded, ready) in enumerate(((h1, ha, s.h1_loaded, s.hidden), (h2, hb, s.h2_loaded, s.gelued))):
                pe.wait_ge(loaded, 16)
                for c in range(M):
                    nth = layer * M + c
                    if nth >= 3:
                        pe.wait_ge(s.gelued, nth - 2)
                    for k in range(M):
                        if c == 0:
                            pe.wait_ge(ready, k + 1)
                        last = pe.matmul(gp[nth % 3][:, :], w[:, k, c * P:(c + 1) * P], src[:, k, :],
                                         start=(k == 0), stop=(k == M - 1))
                    last.then_inc(s.square, 1)
            pe.wait_ge(s.w3_loaded, 32)
            for t in range(TT):
                if t >= 2:
                    pe.wait_ge(s.chain, 4 + t - 1)
                for k in range(M):
                    if t == 0:
                        pe.wait_ge(s.gelued, M + k + 1)
                    last = pe.matmul(up[t % 2][:, 0:D], ha[:, k, t * P:(t + 1) * P], w3[:, k, :],
                                     start=(k == 0), stop=(k == M - 1))
                last.then_inc(s.out_done, 1)


def phase_cross1(nc, g, i, ctx):
    K9 = KT + 1
    QQ = 2 * P
    CHUNKS = (K9 + 1) // 2
    BANKS = 3
    PER_BATCH = PAIRS // 2
    PER_ITER = 2 * PER_BATCH
    LAST = 2
    with Scope(nc, "c1") as sc:
        wk, wv = sc.sb("wk", [P, PAIRS, D]), sc.sb("wv", [P, KD, H * DH])
        mask8, maskb = sc.sb("mask8", [P, B, KT], U8), sc.sb("maskb", [P, B, K9])
        qd = [sc.sb(f"qd{u}", [P, PAIRS, P]) for u in range(2)]
        qh, ql = ([sc.sb(f"q{k}{u}", [P, KD, QQ], F32R) for u in range(2)] for k in "hl")
        pr = [sc.sb(f"pr{u}", [P, K9, QQ]) for u in range(2)]
        top, peak, peaks = sc.sb("top", [P, QQ]), sc.sb("peak", [P, 2]), sc.sb("peaks", [P, 2, P])
        sps = sc.ps("sps", [P, BANKS, 2, QQ])
        qb, mb, uTb = (sc.ps(k, [P, 512]) for k in ("qb", "mb", "uTb"))
        qaps = qb[:, :].rearrange("p (k q) -> p k q", k=KD)
        topT, peakb = mb[:, 0:QQ].rearrange("p (c q) -> p c q", c=2), mb[:, QQ:2 * QQ].rearrange("p (c q) -> p c q", c=2)
        w = Weighted(g, sc, ctx, wv, [sc.sb("uT", [P, 2, KD, P])],
                     uTb[:, :].rearrange("p (c k q) -> p c k q", c=2, k=KD), topT)
        s = Names(**{name: sc.sem(name) for name in (
            "w_loaded mask_loaded chain zeroed absorbed absorbed_hi absorbed_lo scored masked topped topT peaked "
            "spread shifted").split()})
        blocks_loaded = [sc.sem(f"blocks_loaded{u}") for u in range(2)]
        block = sc.block()

        def when(j):
            return j // PER_BATCH + 1, (j // PER_BATCH + 1) % 2, j % PER_BATCH

        def part(j, c):
            return pr[j % 2][:, :, c * P:(c + 1) * P]

        @block.sync
        def _(sp):
            def blocks(nth, u):
                load_blocks(sp, g, qd[u], blocks_loaded[u], s.absorbed, nth)

            sp.dma_start(mask8[:, :, :], i.mask).then_inc(s.mask_loaded, 16)
            sp.wait_ge(s.zeroed, 1)
            blocks(0, 0)
            sp.dma_start(wk[:, :, :], rows(i.l1_wkT)).then_inc(s.w_loaded, 16)
            sp.dma_start(wv[:, :, :], rows(i.l1_wv)).then_inc(s.w_loaded, 16)

            def load(nth, u):
                ctx.load(sp, nth)
                blocks(nth, u)

            load(1, 1)
            with sp.Fori(0, ITERS - 1) as it:
                for u in range(2):
                    load(sp.snap(it * 2 + 2 + u), u)

        @block.gpsimd
        def _(pool):
            pool.memset(qd[0][:, :, :], 0.0)
            pool.memset(qd[1][:, :, :], 0.0).then_inc(s.zeroed, 1)

            def step(it, j):
                nth, u, q = when(j)
                more = there(it, 2 * j + PAIRS)
                for c in range(2):
                    if there(it, 2 * j - 2):
                        w.rest(pool, part(j - 1, c), it, 2 * j - 2 + c)
                    if 1 <= q <= 2 and more:
                        ctx.shifts(pool, it * 2 + nth, 2 * (q - 1) + c)
                if q == 3 and more:
                    ctx.rest_rows(pool, it * 2 + nth, u)

            pipelined(pool, step, LAST, PER_ITER)

        @block.vector
        def _(v):
            chain = Chain(v, s.chain)

            def rest_absorbed(it, j):
                v.wait_ge(s.absorbed_hi, it * PER_ITER + j + 1)
                v.tensor_tensor(ql[j % 2][:, :, :], qaps, qh[j % 2][:, :, :].bitcast(F32),
                                ALU.subtract).then_inc(s.absorbed_lo, 1)

            def masked(it, j):
                e = it * PER_ITER + j
                need(v, w.rested, (e - 1) * 2)
                for c in range(CHUNKS):
                    tiles = slice(2 * c, min(2 * c + 2, K9))
                    count = tiles.stop - tiles.start
                    v.wait_ge(s.scored, e * CHUNKS + c + 1)
                    v.tensor_tensor(pr[j % 2][:, tiles, :], sps[:, c % BANKS, 0:count, :],
                                    maskb[:, it * 2 + j // PER_BATCH, tiles, None].to_broadcast([P, count, QQ]),
                                    ALU.add).then_inc(s.masked, 1)

            def top_of(it, j):
                e = it * PER_ITER + j
                v.wait_ge(s.masked, (e + 1) * CHUNKS)
                need(v, s.topT, e)
                v.tensor_reduce(top[:, :], pr[j % 2][:, :, :].rearrange("p k q -> p q k"), AX.X,
                                ALU.max).then_inc(s.topped, 1)

            def peak_of(it, j):
                e = it * PER_ITER + j
                v.wait_ge(s.topT, e + 1)
                chain(v.tensor_reduce(peak[:, :], topT, AX.X, ALU.max))
                need(v, s.spread, e)
                v.tensor_tensor(peaks[:, :, :], g.ident[:, None, :].to_broadcast([P, 2, P]),
                                peak[:, :, None].to_broadcast([P, 2, P]), ALU.mult).then_inc(s.peaked, 1)

            def shift_by_peak(it, j):
                v.wait_ge(s.spread, it * PER_ITER + j + 1)
                for c in range(2):
                    v.tensor_tensor(part(j, c), part(j, c), peakb[:, None, c, :].to_broadcast([P, K9, P]),
                                    ALU.subtract).then_inc(s.shifted, 1)

            def step(it, j):
                nth, u, q = when(j)
                more = there(it, 2 * j + PAIRS)
                if there(it, 2 * j):
                    masked(it, j)
                if q == 3 and more:
                    ctx.rest_turned(v, it * 2 + nth, u, 3)
                if there(it, 2 * j):
                    top_of(it, j)
                if there(it, 2 * j - 2):
                    w.invert(v, it, 2 * j - 2)
                if there(it, 2 * j):
                    peak_of(it, j)
                if 1 <= q and more:
                    ctx.rest_turned(v, it * 2 + nth, u, (0, 1, 4)[q - 1])
                if there(it, 2 * j + 2):
                    rest_absorbed(it, j + 1)
                if there(it, 2 * j - 2):
                    w.invert(v, it, 2 * j - 1)
                if there(it, 2 * j):
                    shift_by_peak(it, j)
                if q == 2 and more:
                    ctx.rest_turned(v, it * 2 + nth, u, 2)
                if q == 0 and more:
                    ctx.apply_vector(v, it * 2 + nth)

            v.memset(maskb[0:N, :, 0], 0.0)
            v.memset(maskb[N:P, :, 0], MASKED)
            v.wait_ge(s.mask_loaded, 16)
            chain(v.tensor_scalar(maskb[:, :, 1:K9], mask8[:, :, :], -1.0, -MASKED, ALU.add, ALU.mult))
            rest_absorbed(0, 0)
            pipelined(v, step, LAST, PER_ITER, chain, PER_ITER)

        @block.scalar
        def _(a):
            def lead_absorbed(it, j):
                e = it * PER_ITER + j
                a.wait_ge(s.absorbed, 2 * (e + 1))
                need(a, s.scored, (e - 1) * CHUNKS)
                a.activation(qh[j % 2][:, :, :], qaps, ACT.Copy).then_inc(s.absorbed_hi, 1)

            def step(it, j):
                nth, u, q = when(j)
                more = there(it, 2 * j + PAIRS)
                if there(it, 2 * j - 2):
                    w.exp(a, part(j - 1, 0), s.shifted, it, 2 * j - 2)
                if there(it, 2 * j - 4):
                    w.copy_sumsT(a, it, 2 * j - 4, 2)
                if q == 3 and more:
                    ctx.leading_turned(a, it * 2 + nth, u, 3)
                if there(it, 2 * j - 2):
                    w.exp(a, part(j - 1, 1), s.shifted, it, 2 * j - 1)
                if there(it, 2 * j - 4):
                    w.copy_values(a, it, 2 * j - 4, 2)
                if q == 3 and more:
                    ctx.leading_rows(a, it * 2 + nth, u)
                if there(it, 2 * j - 2):
                    w.normalise(a, it, 2 * j - 2)
                if 1 <= q and more:
                    ctx.leading_turned(a, it * 2 + nth, u, (0, 1, 4)[q - 1])
                if there(it, 2 * j + 2):
                    lead_absorbed(it, j + 1)
                if there(it, 2 * j - 2):
                    w.normalise(a, it, 2 * j - 1)
                if q == 2 and more:
                    ctx.leading_turned(a, it * 2 + nth, u, 2)

            lead_absorbed(0, 0)
            pipelined(a, step, LAST, PER_ITER)

        @block.tensor
        def _(pe):
            def absorb(it, j):
                e, u = it * PER_ITER + j, j // PER_BATCH % 2
                if j % PER_BATCH == 0:
                    pe.wait_ge(blocks_loaded[u], (it + j // PER_ITER + 1) * 32)
                need(pe, s.absorbed_lo, e)
                for c in range(2):
                    p = (2 * j + c) % PAIRS
                    for k in range(KD):
                        last = pe.matmul(qaps[:, k, c * P:(c + 1) * P], wk[:, p, k * P:(k + 1) * P], qd[u][:, p, :],
                                         start=True, stop=True)
                last.then_inc(s.absorbed, 2)

            def scores(it, j, chunks):
                e, u = it * PER_ITER + j, j // PER_BATCH % 2
                if j % PER_BATCH == 0 and chunks[0] == 0:
                    pe.wait_ge(ctx.turned_lo, (it * 2 + j // PER_BATCH + 1) * ctx.rounds)
                if chunks[0] == 0:
                    pe.wait_ge(s.absorbed_lo, e + 1)
                for c in chunks:
                    need(pe, s.masked, e * CHUNKS + (c - BANKS + 1 if c >= BANKS else (-1, 0, -2)[c]))
                    for t in range(2 * c, min(2 * c + 2, K9)):
                        cols = slice(t * P, (t + 1) * P)
                        for k in range(KD):
                            last = three(pe, sps[:, c % BANKS, t % 2, :], (ctx.hiT[u][:, k, cols], ctx.loT[u][:, k, cols]),
                                         (qh[j % 2][:, k, :], ql[j % 2][:, k, :]), k == 0, k == KD - 1)
                    last.then_inc(s.scored, 1)

            def turn_top(it, j):
                e = it * PER_ITER + j
                pe.wait_ge(s.topped, e + 1)
                need(pe, s.shifted, 2 * e)
                need(pe, w.valued_copied, 2 * (e - 1))
                for c in range(2):
                    last = pe.transpose(topT[:, c, :], top[:, c * P:(c + 1) * P], g.ident[:, :])
                last.then_inc(s.topT, 1)

            def spread(it, j):
                pe.wait_ge(s.peaked, it * PER_ITER + j + 1)
                pe.matmul(peakb, g.ones[:, :], peaks[:, :, :], start=True, stop=True).then_inc(s.spread, 1)

            def step(it, j):
                nth, u, q = when(j)
                more = there(it, 2 * j + PAIRS)
                if there(it, 2 * j):
                    scores(it, j, range(2))
                if there(it, 2 * j - 4):
                    w.turn_sums(pe, it, 2 * j - 4, 2)
                if q == 3 and more:
                    ctx.turn(pe, it * 2 + nth, 3)
                if there(it, 2 * j):
                    scores(it, j, range(2, CHUNKS))
                if there(it, 2 * j - 4):
                    if there(it, 2 * j - 2):
                        pe.wait_ge(s.shifted, 2 * (it * PER_ITER + j))
                    w.values(pe, it, 2 * j - 4, 2)
                if there(it, 2 * j - 2):
                    w.sums(pe, it, 2 * j - 2)
                if there(it, 2 * j):
                    turn_top(it, j)
                if 1 <= q and more:
                    ctx.turn(pe, it * 2 + nth, (0, 1, 4)[q - 1])
                if there(it, 2 * j + 2):
                    absorb(it, j + 1)
                if there(it, 2 * j - 2):
                    w.sums(pe, it, 2 * j - 1)
                if there(it, 2 * j):
                    spread(it, j)
                if q == 2 and more:
                    ctx.turn(pe, it * 2 + nth, 2)

            pe.wait_ge(s.w_loaded, 32)
            absorb(0, 0)
            pipelined(pe, step, LAST, PER_ITER)


def phase_out1(nc, g, i):
    with Scope(nc, "o1") as sc:
        wo, og, ob = sc.sb("wo", [P, PAIRS, D]), sc.sb("og", [P, D]), sc.sb("ob", [P, D])
        res, resn = sc.sb("res", [P, TT, D]), sc.sb("resn", [P, TT, D])
        n = norm_tensors(sc, "n", TT)
        ops = sc.ps("ops", [P, TT, 512])
        loaded, chain_sem, out_done = sc.sem("loaded"), sc.sem("chain"), sc.sem("out_done")
        block = sc.block()

        @block.sync
        def _(sp):
            sp.dma_start(wo[:, :, :], rows(i.l1_wo)).then_inc(loaded, 16)
            sp.dma_start(og[:, :], i.l1_out_g).then_inc(loaded, 16)
            sp.dma_start(ob[:, :], i.l1_out_b).then_inc(loaded, 16)

        @block.vector
        def _(v):
            chain = Chain(v, chain_sem)
            for t in range(TT):
                v.wait_ge(out_done, t + 1)
                last = v.tensor_copy(res[:, t, :], ops[:, t, 0:D])
            chain(last)
            norm_stats(v, chain, n, res, TT)
            chain(norm_apply(v, chain, n, 1, res, resn, TT))
            wide = [P, TT, D]
            v.wait_ge(loaded, 48)
            chain(v.tensor_tensor(resn[:, :, :], resn[:, :, :], og[:, None, :].to_broadcast(wide), ALU.mult))
            chain(v.tensor_tensor(resn[:, :, :], resn[:, :, :], ob[:, None, :].to_broadcast(wide), ALU.add))
            v.tensor_tensor(g.x_tok[:, :, :], g.x_tok[:, :, :], resn[:, :, :], ALU.add)

        @block.scalar
        def _(a):
            norm_root(a, n, 1)

        @block.tensor
        def _(pe):
            pe.wait_ge(loaded, 48)
            for t in range(TT):
                for p in range(PAIRS):
                    last = pe.matmul(ops[:, t, 0:D], g.zT[:, p, t * P:(t + 1) * P], wo[:, p, :],
                                     start=(p == 0), stop=(p == PAIRS - 1))
                last.then_inc(out_done, 1)


def phase_attn1(nc, g, i):
    HN, HD = 8, P
    UNITS = TT
    HP = HN // 2
    with Scope(nc, "a1") as sc:
        wq, wkv, wo = sc.sb("wq", [P, KD, HN * HD]), sc.sb("wkv", [P, KD, 2 * HD]), sc.sb("wo", [P, HN, D])
        bqk, bv, pos = sc.sb("bqk", [P, HN + 1]), sc.sb("bv", [P, HD]), sc.sb("pos", [P, N])
        causal = sc.sb("causal", [P, N])
        m = turned_norm(sc, "m")
        qT = sc.sb("qT", [P, B, HN, N])
        kT = sc.sb("kT", [P, B, N])
        vr = sc.sb("vr", [N, B, HD])
        sm = [sc.sb(f"sm{u}", [P, 2, HP, N]) for u in range(2)]
        mx, su, rs = sc.sb("mx", [P, 2, HP]), sc.sb("su", [P, 2, HP]), sc.sb("rs", [P, 2, HP])
        pT = [sc.sb(f"pT{u}", [N, HN * N]) for u in range(2)]
        oT = sc.sb("oT", [P, HN, T])
        pps = [sc.ps(f"pps{u}", [P, T]) for u in range(2)]
        sps = [sc.ps(f"sps{u}", [P, 2, HP, N]) for u in range(2)]
        ptps, ops = sc.ps("ptps", [N, HN * N]), sc.ps("ops", [P, HN, N])
        s = Names(**{name: sc.sem(name) for name in (
            "w_loaded t_loaded wo_loaded chain projected taken scored shifted exped probs turned turned_copied summed "
            "summed_copied out_done").split()})
        block = sc.block()

        @block.sync
        def _(sp):
            for to, of in ((bqk, i.a1_bqk), (bv, i.a1_bv), (pos, i.a1_pos), (causal, i.causal)):
                sp.dma_start(to[:, :], of).then_inc(s.t_loaded, 16)
            sp.dma_start(wq[:, :, :], rows(i.a1_wq)).then_inc(s.w_loaded, 16)
            sp.dma_start(wkv[:, :, :], rows(i.a1_wkv)).then_inc(s.w_loaded, 16)
            sp.dma_start(wo[:, :, :], rows(i.a1_wo)).then_inc(s.wo_loaded, 16)

        @block.vector
        def _(v):
            chain = Chain(v, s.chain)
            turned_norm_vector(v, chain, m, g.x_tok)
            v.wait_ge(s.t_loaded, 64)
            by_batch = lambda t: t.rearrange("p (b n) -> p b n", n=N)
            for c in range(HN + 1):
                v.wait_ge(s.projected, c + 1)
                v.scalar_tensor_tensor(out=kT[:, :, :] if c == 0 else qT[:, :, c - 1, :], in0=by_batch(pps[c % 2][:, :]),
                                       scalar=bqk[:, c:c + 1], in1=pos[:, None, :].to_broadcast([P, B, N]),
                                       op0=ALU.add, op1=ALU.add).then_inc(s.taken, 1)
            for c in range(2):
                v.wait_ge(s.projected, HN + 1 + c + 1)
                v.tensor_tensor(vr[:, 4 * c:4 * c + 4, :], pps[(HN + 1 + c) % 2][0:N, :].rearrange("p (b e) -> p b e", b=4),
                                bv[0:N, None, :].to_broadcast([N, 4, HD]), ALU.add).then_inc(s.taken, 1)

            def shift(unit):
                v.wait_ge(s.scored, unit + 1)
                if unit >= 2:
                    v.wait_ge(s.turned, 2 * (unit - 1))
                to = sm[unit % 2]
                for b in range(2):
                    last = v.scalar_tensor_tensor(out=to[:, b, :, :], in0=sps[unit % 2][:, b, :, :], scalar=HD ** -0.5,
                                                  in1=causal[:, None, :].to_broadcast([P, HP, N]), op0=ALU.mult, op1=ALU.add)
                chain(last)
                chain(v.tensor_reduce(mx[:, :, :], to[:, :, :, :], AX.X, ALU.max))
                v.tensor_tensor(to[:, :, :, :], to[:, :, :, :], mx[:, :, :, None].to_broadcast([P, 2, HP, N]),
                                ALU.subtract).then_inc(s.shifted, 1)

            def normalise(unit):
                v.wait_ge(s.exped, unit + 1)
                of = sm[unit % 2]
                chain(v.tensor_reduce(su[:, :, :], of[:, :, :, :], AX.X, ALU.add))
                chain(v.reciprocal(rs[:, :, :], su[:, :, :]))
                v.tensor_tensor(of[:, :, :, :], of[:, :, :, :], rs[:, :, :, None].to_broadcast([P, 2, HP, N]),
                                ALU.mult).then_inc(s.probs, 1)

            for unit in range(UNITS + 1):
                if unit < UNITS:
                    shift(unit)
                if unit >= 1:
                    normalise(unit - 1)
            for t in range(TT):
                v.wait_ge(s.out_done, t // 2 * 2 + 2)
                v.tensor_tensor(g.x_tok[:, t, :], g.x_tok[:, t, :], pps[t // 2][:, t % 2 * D:t % 2 * D + D], ALU.add)

        @block.scalar
        def _(a):
            turned_norm_scalar(a, m)

            def exp(unit):
                a.wait_ge(s.shifted, unit + 1)
                a.activation(sm[unit % 2][:, :, :, :], sm[unit % 2][:, :, :, :], ACT.Exp).then_inc(s.exped, 1)

            exp(0)
            for b in range(B + 1):
                if b % 2 == 0 and b // 2 + 1 < UNITS:
                    exp(b // 2 + 1)
                if b < B:
                    a.wait_ge(s.turned, b + 1)
                    if b >= 2:
                        a.wait_ge(s.summed, b - 1)
                    a.activation(pT[b % 2][:, :], ptps[:, :], ACT.Copy).then_inc(s.turned_copied, 1)
                if b >= 1:
                    w = b - 1
                    a.wait_ge(s.summed, w + 1)
                    a.activation(oT[:, :, w * N:w * N + N], ops[:, :, :], ACT.Copy).then_inc(s.summed_copied, 1)

        @block.tensor
        def _(pe):
            turned_norm_tensor(pe, g, m)
            pe.wait_ge(m.copied, KD)
            pe.wait_ge(s.w_loaded, 32)
            for c in range(HN + 1):
                if c >= 2:
                    pe.wait_ge(s.taken, c - 1)
                for k in range(KD):
                    w = wkv[:, k, 0:HD] if c == 0 else wq[:, k, (c - 1) * HD:c * HD]
                    last = pe.matmul(pps[c % 2][:, :], w, m.yT[:, k, :], start=(k == 0), stop=(k == KD - 1))
                last.then_inc(s.projected, 1)
            for c in range(2):
                nth = HN + 1 + c
                pe.wait_ge(s.taken, nth - 1)
                for b in range(4):
                    at = (4 * c + b) * N
                    for k in range(KD):
                        last = pe.matmul(pps[nth % 2][0:N, b * HD:(b + 1) * HD], m.yT[:, k, at:at + N],
                                         wkv[:, k, HD:2 * HD], start=(k == 0), stop=(k == KD - 1))
                last.then_inc(s.projected, 1)
            pe.wait_ge(s.taken, HN + 3)

            def scores(unit):
                if unit >= 2:
                    pe.wait_ge(s.shifted, unit - 1)
                for b in range(2):
                    for h in range(HP):
                        q = qT[:, 2 * unit + b, 2 * h:2 * h + 2, :].rearrange("p h n -> p (h n)")
                        last = pe.matmul(sps[unit % 2][:, b, h, :], q, kT[:, 2 * unit + b, :], start=True, stop=True)
                last.then_inc(s.scored, 1)

            scores(0)
            scores(1)
            for b in range(B + 1):
                unit = b // 2
                if b < B:
                    if b % 2 == 0:
                        pe.wait_ge(s.probs, unit + 1)
                    if b >= 1:
                        pe.wait_ge(s.turned_copied, b)
                    for h in range(HP):
                        last = pe.transpose(ptps[:, h * P:(h + 1) * P], sm[unit % 2][:, b % 2, h, :], g.ident[:, :])
                    last.then_inc(s.turned, 1)
                if b >= 1:
                    w = b - 1
                    pe.wait_ge(s.turned_copied, w + 1)
                    if w >= 1:
                        pe.wait_ge(s.summed_copied, w)
                    pe.matmul(ops[:, :, :].rearrange("p h n -> p (h n)"), vr[:, w, :], pT[w % 2][:, :],
                              start=True, stop=True).then_inc(s.summed, 1)
                if b % 2 == 1 and unit + 2 < UNITS:
                    scores(unit + 2)
            pe.wait_ge(s.summed_copied, B)
            pe.wait_ge(s.wo_loaded, 16)
            for t in range(TT):
                for h in range(HN):
                    last = pe.matmul(pps[t // 2][:, t % 2 * D:t % 2 * D + D], oT[:, h, t * P:(t + 1) * P], wo[:, h, :],
                                     start=(h == 0), stop=(h == HN - 1))
                last.then_inc(s.out_done, 1)


def phase_experts(nc, g, i):
    E, GROUPS, PER, TOP_GROUPS = EXPERTS, 4, EXPERTS // 4, 2
    ALL = E + 2
    RING = 4
    with Scope(nc, "e1") as sc:
        we = [sc.sb(f"we{u}", [P, 3 * D]) for u in range(RING)]
        gw, gbias, below = sc.sb("gw", [P, KD, E]), sc.sb("gbias", [P, E]), sc.sb("below", [P, GROUPS, GROUPS])
        m = turned_norm(sc, "m")
        score, choice, masked, left = (sc.sb(k, [P, TT, E]) for k in ("score", "choice", "masked", "left"))
        best = sc.sb("best", [P, TT, GROUPS, 8])
        gsum, rank, gmask = (sc.sb(k, [P, TT, GROUPS]) for k in ("gsum", "rank", "gmask"))
        more, same = sc.sb("more", [P, TT, GROUPS, GROUPS]), sc.sb("same", [P, TT, GROUPS, GROUPS])
        best8 = sc.sb("best8", [P, TT, 8])
        wsum = sc.sb("wsum", [P, TT])
        weight = sc.sb("weight", [P, TT, ALL])
        act = [sc.sb(f"act{u}", [P, T]) for u in range(2)]
        hid = [sc.sb(f"hid{u}", [P, T]) for u in range(2)]
        gps, ups = m.tps, [sc.ps(f"ups{u}", [P, T]) for u in range(2)]
        dps = [sc.ps(f"dps{u}", [P, TT, D]) for u in range(2)]
        s = Names(**{name: sc.sem(name) for name in (
            "t_loaded chain gated scored weighed gate_done up_done silued hidden down_done added").split()})
        loaded = [sc.sem(f"loaded{u}") for u in range(RING)]
        block = sc.block()

        @block.sync
        def _(sp):
            def load(e, u):
                sp.dma_start(we[u][:, :], i.e1_w[e]).then_inc(loaded[u], 16)

            sp.dma_start(gw[:, :, :], rows(i.e1_gw)).then_inc(s.t_loaded, 16)
            sp.dma_start(gbias[:, :], i.e1_bias).then_inc(s.t_loaded, 16)
            sp.dma_start(below[:, :, :], i.e1_below).then_inc(s.t_loaded, 16)
            for u in range(RING):
                load(u, u)
            with sp.Fori(0, E // RING - 1) as it:
                for u in range(RING):
                    e = sp.snap(it * RING + u + RING)
                    sp.wait_ge(s.down_done, it * RING + u + 1)
                    load(e, u)
            for u in range(2):
                sp.wait_ge(s.down_done, E - RING + u + 1)
                load(E + u, u)

        @block.vector
        def _(v):
            chain = Chain(v, s.chain)
            turned_norm_vector(v, chain, m, g.x_tok)
            v.memset(weight[:, :, E:ALL], 1.0)
            v.wait_ge(s.scored, 1)
            v.wait_ge(s.t_loaded, 48)
            chain(v.tensor_tensor(choice[:, :, :], score[:, :, :], gbias[:, None, :].to_broadcast([P, TT, E]), ALU.add))
            for t in range(TT):
                for q in range(GROUPS):
                    last = v.max(best[:, t, q, :], choice[:, t, q * PER:(q + 1) * PER])
            chain(last)
            chain(v.tensor_tensor(gsum[:, :, :], best[:, :, :, 0], best[:, :, :, 1], ALU.add))
            wide = [P, TT, GROUPS, GROUPS]
            other, own = gsum[:, :, None, :].to_broadcast(wide), gsum[:, :, :, None].to_broadcast(wide)
            v.tensor_tensor(more[:, :, :, :], other, own, ALU.is_gt)
            chain(v.tensor_tensor(same[:, :, :, :], other, own, ALU.is_equal))
            flat = lambda t: t[:, :, :, :].rearrange("p t a b -> p t (a b)")
            chain(v.tensor_tensor(flat(same), flat(same), below[:, :, :].rearrange("p a b -> p (a b)")[:, None, :]
                                  .to_broadcast([P, TT, GROUPS * GROUPS]), ALU.mult))
            chain(v.tensor_tensor(more[:, :, :, :], more[:, :, :, :], same[:, :, :, :], ALU.add))
            chain(v.tensor_reduce(rank[:, :, :], more[:, :, :, :], AX.X, ALU.add))
            chain(v.tensor_scalar(gmask[:, :, :], rank[:, :, :], TOP_GROUPS - 0.5, None, ALU.is_lt))
            grouped = lambda t: t[:, :, :].rearrange("p t (a b) -> p t a b", b=PER)
            chain(v.tensor_tensor(grouped(masked), grouped(choice), gmask[:, :, :, None].to_broadcast([P, TT, GROUPS, PER]),
                                  ALU.mult))
            chain(v.tensor_scalar(masked[:, :, :], masked[:, :, :], 0.0, None, ALU.add))
            for t in range(TT):
                last = v.max(best8[:, t, :], masked[:, t, :])
            chain(last)
            for t in range(TT):
                last = v.match_replace(out=left[:, t, :], in_to_replace=best8[:, t, :], in_values=masked[:, t, :],
                                       imm_value=MASKED)
            chain(last)
            chain(v.tensor_scalar(left[:, :, :], left[:, :, :], MASKED / 2, None, ALU.is_lt))
            chain(v.tensor_tensor(masked[:, :, :], left[:, :, :], score[:, :, :], ALU.mult))
            chain(v.tensor_reduce(wsum[:, :], masked[:, :, :], AX.X, ALU.add))
            chain(v.tensor_scalar(wsum[:, :], wsum[:, :], 1e-20, None, ALU.add))
            chain(v.reciprocal(wsum[:, :], wsum[:, :]))
            chain(v.tensor_scalar(wsum[:, :], wsum[:, :], ROUTED_SCALING, None, ALU.mult))
            chain(v.tensor_tensor(weight[:, :, 0:E], masked[:, :, :], wsum[:, :, None].to_broadcast([P, TT, E]), ALU.mult))

            def hide(e, u):
                v.wait_ge(s.silued, e + 1)
                v.wait_ge(s.up_done, e + 1)
                v.tensor_tensor(hid[u % 2][:, :], ups[u % 2][:, :], act[u % 2][:, :], ALU.mult).then_inc(s.hidden, 1)

            def add(e, u):
                v.wait_ge(s.down_done, e + 1)
                for t in range(TT):
                    last = v.scalar_tensor_tensor(out=g.x_tok[:, t, :], in0=dps[u % 2][:, t, :], scalar=weight[:, t, e:e + 1]
                                                  if isinstance(e, int) else weight[:, t, bass.ds(e, 1)],
                                                  in1=g.x_tok[:, t, :], op0=ALU.mult, op1=ALU.add)
                last.then_inc(s.added, 1)

            hide(0, 0)
            with v.Fori(0, E // RING) as it:
                for u in range(RING):
                    e = it * RING + u
                    hide(e + 1, u + 1)
                    add(e, u)
                    v.wait_ge(s.added, e + 1)
            hide(E + 1, E + 1)
            add(E, E)
            v.wait_ge(s.added, E + 1)
            add(E + 1, E + 1)

        @block.scalar
        def _(a):
            turned_norm_scalar(a, m)
            a.wait_ge(s.gated, 1)
            a.activation(score[:, :, :], ups[1][:, 0:TT * E].rearrange("p (t e) -> p t e", t=TT), ACT.Sigmoid).then_inc(s.scored, 1)

            def silu(e, u, free):
                a.wait_ge(s.gate_done, e + 1)
                if free is not None:
                    a.wait_ge(s.hidden, free)
                a.activation(act[u % 2][:, :], gps[u % 2][:, :], ACT.Silu).then_inc(s.silued, 1)

            silu(0, 0, None)
            silu(1, 1, None)
            with a.Fori(0, E // RING) as it:
                for u in range(RING):
                    silu(it * RING + u + 2, u, it * RING + u + 1)

        @block.tensor
        def _(pe):
            turned_norm_tensor(pe, g, m)
            pe.wait_ge(m.copied, KD)
            pe.wait_ge(s.t_loaded, 48)
            for t in range(TT):
                for k in range(KD):
                    last = pe.matmul(ups[1][:, t * E:(t + 1) * E], m.yT[:, k, t * P:(t + 1) * P], gw[:, k, :],
                                     start=(k == 0), stop=(k == KD - 1))
            last.then_inc(s.gated, 1)

            def gate_up(e, u, free, turn=0):
                pe.wait_ge(loaded[u % RING], (turn + 1 + u // RING) * 16)
                for o, ps, done, used in ((0, gps, s.gate_done, s.silued), (D, ups, s.up_done, s.hidden)):
                    if free is not None:
                        pe.wait_ge(used, free)
                    for k in range(KD):
                        last = pe.matmul(ps[u % 2][:, :], we[u % RING][:, o + k * P:o + (k + 1) * P], m.yT[:, k, :],
                                         start=(k == 0), stop=(k == KD - 1))
                    last.then_inc(done, 1)

            def down(e, u, free):
                pe.wait_ge(s.hidden, e + 1)
                if free is not None:
                    pe.wait_ge(s.added, free)
                for t in range(TT):
                    last = pe.matmul(dps[u % 2][:, t, :], hid[u % 2][:, t * P:(t + 1) * P], we[u % RING][:, 2 * D:3 * D],
                                     start=True, stop=True)
                last.then_inc(s.down_done, 1)

            gate_up(0, 0, None)
            pe.wait_ge(s.scored, 1)
            gate_up(1, 1, None)
            with pe.Fori(0, E // RING) as it:
                for u in range(RING):
                    e = it * RING + u
                    gate_up(e + 2, u + 2, e + 1, it)
                    down(e, u, None)
            down(E, E, E - 1)
            down(E + 1, E + 1, E)


def phase_store(nc, g, o):
    with Scope(nc, "store") as sc:
        stored = sc.sem("stored")
        block = sc.block()

        @block.sync
        def _(sp):
            sp.dma_start(o.rearrange("(t p) d -> p t d", p=P), g.x_tok[:, :, :]).then_inc(stored, 16)
            sp.wait_ge(stored, 16)


def build(nc, i, o, only=range(6)):
    with Scope(nc, "g") as sc:
        g = Names(
            x_tok=sc.sb("x_tok", [P, TT, D]), ident=sc.sb("ident", [P, P]), ones=sc.sb("ones", [P, P]),
            ctx_mean=sc.sb("ctx_mean", [P, B, KT]), ctx_rstd=sc.sb("ctx_rstd", [P, B, KT]))
        phase_setup(nc, g, i)
        g.q = nc.dram_tensor("q", (P, PAIRS, T), F32, kind="Internal").ap()
        g.lat = nc.dram_tensor("lat", (B, N, D), F32, kind="Internal").ap()
        if 0 in only:
            with Scope(nc, "x0") as sx:
                g.zT = sx.sb("zT", [P, PAIRS, T])
                ctx = Context(g, i, 0, sx)
                wk = Names(source=i.l0_wk, staged=g.zT[:, 0:4, :].rearrange("p (k a) t -> p k (a t)", k=KD),
                           hi=sx.sb("wk_hi", [P, KD, H * DH], F32R), lo=sx.sb("wk_lo", [P, KD, H * DH], F32R))
                phase_queries(nc, g, i, 0, i.l0_wq, i.l0_lat_g, i.l0_lat_b, ctx, wk)
                phase_cross0(nc, g, i, ctx, wk)
                phase_out0(nc, g, i)
        if 1 in only:
            phase_attn0(nc, g, i)
        if 2 in only:
            phase_ffn0(nc, g, i)
        if 3 in only:
            with Scope(nc, "x1") as sx:
                g.zT = sx.sb("zT", [P, PAIRS, T])
                ctx = Context(g, i, 1, sx)
                phase_queries(nc, g, i, 1, i.l1_wq, i.l1_lat_g, i.l1_lat_b, ctx, None)
                phase_cross1(nc, g, i, ctx)
                phase_out1(nc, g, i)
        if 4 in only:
            phase_attn1(nc, g, i)
        if 5 in only:
            phase_experts(nc, g, i)
        phase_store(nc, g, o)


def laid_out(a):
    wide = lambda v: np.ascontiguousarray(np.broadcast_to(v, (P, v.shape[-1])))
    keyed = lambda c: np.ascontiguousarray(
        np.tile(c.reshape(P, KT, -1).transpose(2, 1, 0).reshape(-1, S), (4, 1)))
    c = np.ascontiguousarray
    per = lambda v: c(v.reshape(-1, P).T)
    tiled = lambda v, n: np.tile(v, P // n)
    head = np.arange(P)[:, None] // 16 == np.arange(8)
    query, key = np.arange(P)[:, None] % N, np.arange(N)[None, :]
    w1, b1 = a["L1_attn_Wkv"], a["L1_attn_bkv"]
    pos = np.arange(N, dtype=np.float32)[:, None]
    ang = pos * np.exp(-np.log(np.float32(10000.0)) * np.arange(0, P, 2, dtype=np.float32) / np.float32(P))[None, :]
    pe = np.zeros((N, P), np.float32)
    pe[:, 0::2], pe[:, 1::2] = np.sin(ang), np.cos(ang)
    gates = lambda w: w.transpose(0, 2, 1).reshape(-1, KD, P, P).transpose(0, 2, 1, 3).reshape(-1, P, D)
    both = lambda k: np.concatenate([a[f"L1_ffn_expert_{k}"], a[f"L1_ffn_shared_{k}"].reshape(2, P, D)])
    down = np.concatenate([a["L1_ffn_expert_down"].transpose(0, 2, 1), a["L1_ffn_shared_down"].T.reshape(2, P, D)])
    below = np.arange(4)[None, :] < np.arange(4)[:, None]
    return {
        "e1_w": c(np.concatenate([gates(both("gate")), gates(both("up")), down], axis=2)),
        "e1_gw": c(a["L1_ffn_gate_w"].T), "e1_bias": wide(a["L1_ffn_gate_bias"]),
        "e1_below": c(np.broadcast_to(below.astype(np.float32), (P, 4, 4))),
        "a1_wq": a["L1_attn_Wq"], "a1_wkv": w1, "a1_wo": a["L1_attn_Wo"],
        "a1_bqk": c(np.concatenate([b1[None, :P], a["L1_attn_bq"].reshape(8, P)]).T), "a1_bv": wide(b1[P:]),
        "a1_pos": c(pe.T),
        "mask": c(a["mask_BxS2_bf1"].view(np.uint8).reshape(B, P, KT).transpose(1, 0, 2)),
        "l1_lat_g": wide(a["L1_xattn_g_l"]), "l1_lat_b": wide(a["L1_xattn_b_l"]),
        "l1_ctx_g": wide(a["L1_xattn_g_x"]), "l1_ctx_b": wide(a["L1_xattn_b_x"]),
        "l1_out_g": wide(a["L1_xattn_g_o"]), "l1_out_b": wide(a["L1_xattn_b_o"]),
        "l1_wq": a["L1_xattn_Wq"], "l1_wkT": c(a["L1_xattn_Wkv"][:, :H * DH].T),
        "l1_wv": c(a["L1_xattn_Wkv"][:, H * DH:]), "l1_wo": a["L1_xattn_Wout"],
        "causal": np.where(key <= query, 0.0, MASKED).astype(np.float32),
        "heads": head.astype(np.float32),
        "a0_lqk": c(np.broadcast_to(np.stack([a[f"L0_attn_{k}"].reshape(H) for k in ("lq1", "lq2", "lk1", "lk2")]), (P, 4, H))),
        "a0_chan": c(np.stack([np.tile(a[f"L0_attn_{k}"], P // 32) for k in ("gn_w", "gn_b", "gamma")], axis=1)),
        "a0_wqk": c(np.stack([a[f"L0_attn_{k}"].T for k in ("Wq1", "Wq2", "Wk1", "Wk2")])),
        "a0_wv": c(a["L0_attn_Wv"].T), "a0_wc": c(a["L0_attn_Wc"].T),
        "f0_w1": c(a["L0_ffn_w1_w"].T), "f0_w2": c(a["L0_ffn_w2_w"].T),
        "f0_h1": c(a["L0_ffn_h1_w"].T), "f0_h2": c(a["L0_ffn_h2_w"].T), "f0_w3": c(a["L0_ffn_w3_w"].T),
        "f0_scales": c(np.stack([per(a[f"L0_ffn_{k}_s"]) for k in ("w1", "w2", "h1", "h2")], axis=1)),
        "f0_w3s": wide(a["L0_ffn_w3_s"]),
        "x": a["x"].reshape(T, D),
        "ctx": a["ctx_1024"],
        "l0_lat_g": wide(a["L0_xattn_ln_lat_g"]), "l0_lat_b": wide(a["L0_xattn_ln_lat_b"]),
        "l0_ctx_g": wide(a["L0_xattn_ln_ctx_g"]), "l0_ctx_b": wide(a["L0_xattn_ln_ctx_b"]),
        "l0_cos": keyed(a["L0_xattn_cos"]), "l0_sin": keyed(a["L0_xattn_sin"]),
        "l0_wq": a["L0_xattn_Wq"],
        "l0_wk": np.ascontiguousarray(a["L0_xattn_Wkv"][:, :H * DH]),
        "l0_wv": np.ascontiguousarray(a["L0_xattn_Wkv"][:, H * DH:]),
        "l0_wo": a["L0_xattn_Wo"], "l0_bo": wide(a["L0_xattn_bo"]),
    }


def kernel(**inputs):
    import concourse.bacc as bacc
    from concourse.bass_utils import run_bass_kernel_spmd

    arrays = {f"in_{k}": np.ascontiguousarray(v) for k, v in
              laid_out({k: np.asarray(v) for k, v in inputs.items()}).items()}
    nc = bacc.Bacc("TRN2", target_bir_lowering=False, num_devices=1)
    i = Names(**{k[3:]: nc.dram_tensor(k, v.shape, mybir.dt.from_np(v.dtype), kind="ExternalInput").ap()
                           for k, v in arrays.items()})
    o = nc.dram_tensor("out_0", (T, D), F32, kind="ExternalOutput").ap()
    build(nc, i, o)
    r = run_bass_kernel_spmd(nc, [arrays], core_ids=[0])
    return r.results[0]["out_0"].reshape(B, N, D)
```

```python
from contextlib import ExitStack

import numpy as np

import concourse.bass as bass
from concourse import mybir

F32 = mybir.dt.float32
BF16 = mybir.dt.bfloat16
F32R = mybir.dt.float32r
U8 = mybir.dt.uint8
ALU = mybir.AluOpType
ACT = mybir.ActivationFunctionType
AX = mybir.AxisListType

P = 128
B, N, S, D = 8, 64, 1024, 256
T = B * N
TT = T // P
KD = D // P
KT = S // P
H, DH = 16, 64
PAIRS = H * DH // P
STEPS = 2 * PAIRS
ITERS = B // 2
EPS = 1e-5
MASKED = -1e30
LAMBDA_INIT = 0.8 - 0.6 * float(np.exp(-0.3 * 11))
EXPERTS = 32
ROUTED_SCALING = 2.5


def Names(**named):
    return type("Names", (), named)()


class Chain:

    def __init__(self, engine, sem):
        self.engine, self.sem, self.base, self.n = engine, sem, 0, 0

    def __call__(self, instruction):
        instruction.then_inc(self.sem, 1)
        self.n += 1
        self.engine.wait_ge(self.sem, self.base + self.n)

    def enter(self, iteration, per_iteration):
        self.base = self.base + self.n + iteration * per_iteration
        self.n = 0

    def leave(self, before, per_iteration, iterations):
        assert self.n == per_iteration, (self.n, per_iteration)
        self.base, self.n = before + per_iteration * iterations, 0


class Scope:

    def __init__(self, nc, name):
        self.nc, self.name, self.stack, self.sems = nc, name, ExitStack(), []
        self.opened = ExitStack()

    def __enter__(self):
        return self

    def __exit__(self, *e):
        self.opened.__exit__(*e)
        if self.sems and not any(e):
            numbers = sorted(x.num for x in self.sems)
            with self.nc.Block() as block:
                @block.gpsimd
                def _(pool):
                    start = last = numbers[0]
                    for x in numbers[1:] + [None]:
                        if x != last + 1:
                            pool.sem_clear(range(start, last + 1))
                            start = x
                        last = x if x is not None else last
        return self.stack.__exit__(*e)

    def sb(self, name, shape, dt=F32):
        return self.stack.enter_context(self.nc.sbuf_tensor(f"{self.name}_{name}", shape, dt))

    def ps(self, name, shape, dt=F32):
        return self.stack.enter_context(self.nc.psum_tensor(f"{self.name}_{name}", shape, dt))

    def sem(self, name):
        self.sems.append(self.stack.enter_context(self.nc.semaphore(f"{self.name}_{name}")))
        return self.sems[-1]

    def block(self):
        return self.opened.enter_context(self.nc.Block())


def norm_tensors(sc, name, tiles):
    n = Names(**{k: sc.sb(f"{name}_{k}", [P, tiles])
                           for k in "sum dif sq dif2 sqe mean var std rstd".split()})
    n.stats = sc.sb(f"{name}_stats", [P, tiles, 6])
    n.var_ready, n.std_ready = sc.sem(f"{name}_var_ready"), sc.sem(f"{name}_std_ready")
    return n


def norm_stats(v, chain, n, src, tiles, scale=1.0, eps=EPS):
    for t in range(tiles):
        last = v.bn_stats(n.stats[:, t, :], src[:, t, 0:D])
    chain(last)
    even, odd = n.stats[:, :, 1], n.stats[:, :, 4]
    v.tensor_tensor(n.sum[:, :], even, odd, ALU.add)
    v.tensor_tensor(n.dif[:, :], even, odd, ALU.subtract)
    chain(v.tensor_tensor(n.sq[:, :], n.stats[:, :, 2], n.stats[:, :, 5], ALU.add))
    v.tensor_scalar(n.mean[:, :], n.sum[:, :], 0.5, None, ALU.mult)
    v.scalar_tensor_tensor(out=n.dif2[:, :], in0=n.dif[:, :], scalar=0.25 * scale, in1=n.dif[:, :], op0=ALU.mult, op1=ALU.mult)
    chain(v.tensor_scalar(n.sqe[:, :], n.sq[:, :], scale / D, eps, ALU.mult, ALU.add))
    v.tensor_tensor(n.var[:, :], n.sqe[:, :], n.dif2[:, :], ALU.add).then_inc(n.var_ready, 1)


def norm_root(a, n, count):
    a.wait_ge(n.var_ready, count)
    a.activation(n.std[:, :], n.var[:, :], ACT.Sqrt).then_inc(n.std_ready, 1)


def norm_apply(v, chain, n, count, src, dst, tiles, normed=None):
    v.wait_ge(n.std_ready, count)
    chain(v.reciprocal(n.rstd[:, :], n.std[:, :]))
    for t in range(tiles):
        last = v.tensor_scalar(dst[:, t, 0:D], src[:, t, 0:D], n.mean[:, t:t + 1], n.rstd[:, t:t + 1],
                               ALU.subtract, ALU.mult)
        if normed:
            last.then_inc(normed, 1)
    return last


def norm_gained(v, chain, n, count, src, dst, gain, shift, tiles, done):
    for t in range(tiles):
        v.scalar_tensor_tensor(out=dst[:, t, 0:D], in0=src[:, t, 0:D], scalar=n.mean[:, t:t + 1], in1=gain,
                                      op0=ALU.subtract, op1=ALU.mult)
    v.wait_ge(n.std_ready, count)
    chain(v.reciprocal(n.rstd[:, :], n.std[:, :]))
    for t in range(tiles):
        v.scalar_tensor_tensor(out=dst[:, t, 0:D], in0=dst[:, t, 0:D], scalar=n.rstd[:, t:t + 1], in1=shift,
                               op0=ALU.mult, op1=ALU.add).then_inc(done, 1)


def rows(ap):
    return ap.rearrange("(k p) n -> p k n", p=P)



def phase_setup(nc, g, i, wait):
    with Scope(nc, "setup") as sc:
        zeroed, done = sc.sem("zeroed"), sc.sem("done")
        block = sc.block()

        @block.sync
        def _(sp):
            sp.dma_start(g.x_tok[:, :, :], i.x.rearrange("(t p) d -> p t d", p=P)).then_inc(g.x_loaded, 16)
            if wait:
                sp.wait_ge(g.x_loaded, 16)

        @block.gpsimd
        def _(pool):
            pool.memset(g.ident[:, :], 0.0).then_inc(zeroed, 1)
            pool.memset(g.ones[:, :], 1.0)
            pool.wait_ge(zeroed, 1)
            pool.affine_select(out=g.ident[:, :], in_=g.ident[:, :], compare_op=ALU.not_equal, fill=1.0,
                               base=0, pattern=[[-1, P]], channel_multiplier=1).then_inc(done, 1)
            pool.wait_ge(done, 1)


class Ahead:

    def __init__(self, g, sc, loads):
        self.g, self.loads = g, loads
        self.qd = [sc.sb(f"qd{u}", [P, PAIRS, P]) for u in range(2)]
        self.loaded, self.zeroed = sc.sem("loaded"), sc.sem("zeroed")
        self.blocks_loaded = [sc.sem(f"blocks_loaded{u}") for u in range(2)]

    def load(self, sp):
        for to, of in self.loads:
            sp.dma_start(to, of).then_inc(self.loaded, 16)

    def wait_loaded(self, engine):
        engine.wait_ge(self.loaded, 16 * len(self.loads))

    def zero(self, pool):
        for qd in self.qd:
            pool.memset(qd[:, :, :], 0.0).then_inc(self.zeroed, 1)

    def load_blocks(self, sp, multiplied, nth, u):
        need(sp, multiplied, PAIRS * (nth - 1))
        of = self.g.q.rearrange("p h (b n) -> p h b n", n=N)
        for half in range(2):
            part = slice(DH * half, DH * half + DH)
            sp.dma_start(self.qd[u][part, :, half * N:half * N + N], of[part, :, nth, :]).then_inc(self.blocks_loaded[u], 16)


def phase_queries(nc, g, i, layer, wq, gain, shift, ctx, wk, ahead):
    with Scope(nc, f"q{layer}") as sc:
        z = sc.sb("z", [P, TT, D])
        gain_sb, shift_sb = sc.sb("gain", [P, D]), sc.sb("shift", [P, D])
        w = sc.sb("w", [P, KD, H * DH])
        zT = sc.sb("zT", [P, KD, T])
        qT = sc.sb("qT", [P, PAIRS, T])
        n = norm_tensors(sc, "n", TT)
        tps = sc.ps("tps", [P, KD, T])
        qps = sc.ps("qps", [P, 2, T])
        w_loaded, g_loaded, wk_loaded, wk_hi = (sc.sem(k) for k in ("w_loaded", "g_loaded", "wk_loaded", "wk_hi"))
        chain_sem, stored = sc.sem("chain"), sc.sem("stored")
        latents, turned, turned_copied = sc.sem("latents"), sc.sem("turned"), sc.sem("turned_copied")
        projected, taken, lat_stored = sc.sem("projected"), sc.sem("taken"), sc.sem("lat_stored")
        block = sc.block()

        @block.sync
        def _(sp):
            sp.dma_start(gain_sb[:, :], gain).then_inc(g_loaded, 16)
            sp.dma_start(shift_sb[:, :], shift).then_inc(g_loaded, 16)
            ctx.load(sp, 0, latents=False)
            sp.dma_start(w[:, :, :], rows(wq)).then_inc(w_loaded, 16)
            for to, of in ctx.table_loads:
                sp.dma_start(to, of).then_inc(ctx.tables, 16)
            if layer == 0:
                sp.dma_start(wk.staged, rows(wk.source)).then_inc(wk_loaded, 16)
            else:
                sp.wait_ge(ctx.empty, 2)
                sp.wait_ge(latents, TT)
                sp.dma_start(g.lat.rearrange("b n d -> (b n) d").rearrange("(t p) d -> p t d", p=P),
                             z[:, :, :]).then_inc(lat_stored, 16)
                sp.wait_ge(lat_stored, 16)
                ctx.load_latents(sp, 0)
            for p in range(0, PAIRS, 2):
                sp.wait_ge(taken, p + 2)
                sp.dma_start(g.q[:, p:p + 2, :], qT[:, p:p + 2, :]).then_inc(stored, 16)
                if p == 0:
                    ahead.load(sp)
            sp.wait_ge(stored, 16 * (PAIRS // 2))
            sp.wait_ge(ahead.zeroed, 2)
            ahead.load_blocks(sp, None, 0, 0)

        @block.gpsimd
        def _(pool):
            ctx.constants(pool)
            ahead.zero(pool)
            pool.wait_ge(ctx.tables, 16 * len(ctx.table_loads))
            for r in range(KT // 2):
                ctx.shifts(pool, 0, r)
            ctx.rest_rows(pool, 0, 0)

        @block.vector
        def _(v):
            chain = Chain(v, chain_sem)

            def take(p):
                v.wait_ge(projected, p + 1)
                v.tensor_scalar(qT[:, p, :], qps[:, p % 2, :], DH ** -0.5, None, ALU.mult).then_inc(taken, 1)

            if layer == 0:
                v.wait_ge(g.x_loaded, 16)
            norm_stats(v, chain, n, g.x_tok, TT, 1.0 + EPS, EPS * EPS)
            v.wait_ge(g_loaded, 32)
            norm_gained(v, chain, n, 1, g.x_tok, z, gain_sb[:, :], shift_sb[:, :], TT, latents)
            if layer == 0:
                ctx.statistics(v, chain, 0)
                ctx.scales(v, chain, 0)
            else:
                ctx.apply_vector(v, 0)
            for p in range(PAIRS - 3):
                take(p)
            if layer == 0:
                v.wait_ge(wk_hi, 1)
                v.tensor_tensor(wk.lo[:, :, :], wk.staged, wk.hi[:, :, :].bitcast(F32), ALU.subtract)
            for r in range(ctx.rounds):
                ctx.rest_turned(v, 0, 0, r)
                if r < 3:
                    take(PAIRS - 3 + r)

        @block.scalar
        def _(a):
            norm_root(a, n, 1)
            if layer == 0:
                norm_root(a, ctx.n, 1)
            for k in range(KD):
                a.wait_ge(turned, k + 1)
                a.activation(zT[:, k, :], tps[:, k, :], ACT.Copy).then_inc(turned_copied, 1)
            if layer == 0:
                ctx.apply_scalar(a, 0)
                a.wait_ge(wk_loaded, 16)
                a.activation(wk.hi[:, :, :], wk.staged, ACT.Copy).then_inc(wk_hi, 1)
            for r in range(ctx.rounds):
                ctx.leading_turned(a, 0, 0, r)
                if r == layer + 1:
                    ctx.leading_rows(a, 0, 0)

        @block.tensor
        def _(pe):
            for k in range(KD):
                for t in range(TT):
                    if k == 0:
                        pe.wait_ge(latents, t + 1)
                    last = pe.transpose(tps[:, k, t * P:(t + 1) * P], z[:, t, k * P:(k + 1) * P], g.ident[:, :])
                last.then_inc(turned, 1)
            pe.wait_ge(turned_copied, KD)
            pe.wait_ge(w_loaded, 16)
            for p in range(PAIRS):
                if p >= 2:
                    pe.wait_ge(taken, p - 1)
                for k in range(KD):
                    last = pe.matmul(qps[:, p % 2, :], w[:, k, p * P:(p + 1) * P], zT[:, k, :],
                                     start=(k == 0), stop=(k == KD - 1))
                last.then_inc(projected, 1)
                if p >= PAIRS - 4:
                    ctx.turn(pe, 0, p - (PAIRS - 4))
            for r in range(4, ctx.rounds):
                ctx.turn(pe, 0, r)


def pipelined(engine, step, lead, steps, chain=None, per_iteration=0):
    for j in range(lead):
        step(0, j)
    before = chain.n if chain else 0
    with engine.Fori(0, ITERS - 1) as it:
        if chain:
            chain.enter(it, per_iteration)
        for j in range(lead, lead + steps):
            step(it, j)
        if chain:
            chain.leave(before, per_iteration, ITERS - 1)
    for j in range(lead, lead + steps):
        step(ITERS - 1, j)


def there(it, j):
    return not isinstance(it, int) or 0 <= STEPS * it + j < B * PAIRS


def need(engine, sem, value):
    if not isinstance(value, int) or value > 0:
        engine.wait_ge(sem, value)


def three(pe, out, left, right, start, stop):
    (lh, ll), (rh, rl) = left, right
    pe.matmul(out, lh, rh, start=start, stop=False)
    pe.matmul(out, lh, rl, start=False, stop=False)
    return pe.matmul(out, ll, rh, start=False, stop=stop)


def settled(sp, value):
    return value if isinstance(value, int) else sp.snap(value)


class Context:

    def __init__(self, g, i, layer, sc):
        self.g, self.i, self.layer = g, i, layer
        self.tiles = tiles = KT + layer
        self.first = layer
        self.rounds = KT // 2 + layer
        self.raw = sc.sb("raw", [P, tiles, D])
        self.gain, self.shift = sc.sb("gain", [P, D]), sc.sb("shift", [P, D])
        self.table_loads = [(self.gain[:, :], i.l0_ctx_g if layer == 0 else i.l1_ctx_g),
                            (self.shift[:, :], i.l0_ctx_b if layer == 0 else i.l1_ctx_b)]
        self.hi, self.lo = ([sc.sb(f"ctx_{k}{u}", [P, tiles, D + 2], F32R) for u in range(2)] for k in ("hi", "lo"))
        self.hiT, self.loT = ([sc.sb(f"ctxT_{k}{u}", [P, KD, tiles * P], F32R) for u in range(2)] for k in ("hi", "lo"))
        self.tps = sc.ps("tps", [P, KD, 2 * P])
        if layer == 0:
            self.n, self.offset, self.scaled = norm_tensors(sc, "n", KT), sc.sb("offset", [P, KT]), sc.sem("scaled")
        self.loaded, self.tables = sc.sem("ctx_loaded"), sc.sem("tables_loaded")
        self.lat_loaded, self.output_loaded = sc.sem("lat_loaded"), sc.sem("output_loaded")
        self.empty, self.applied, self.affine = sc.sem("empty"), sc.sem("applied"), sc.sem("affine")
        self.turned, self.turned_hi, self.turned_lo = sc.sem("turned"), sc.sem("turned_hi"), sc.sem("turned_lo")
        self.gained = sc.sem("gained")
        self.rows_hi, self.rows_lo = sc.sem("rows_hi"), sc.sem("rows_lo")

    def load(self, sp, nth, latents=True):
        need(sp, self.turned, self.rounds * nth)
        need(sp, self.rows_lo, nth)
        sp.dma_start(self.raw[:, self.first:, :], self.i.ctx[nth].rearrange("(p k) d -> p k d", k=KT)).then_inc(self.loaded, 16)
        if self.layer and latents:
            self.load_latents(sp, nth)

    def load_output(self, sp, wo):
        sp.wait_ge(self.turned, self.rounds * B)
        sp.wait_ge(self.rows_lo, B)
        sp.dma_start(self.raw[:, 0:PAIRS, :], rows(wo)).then_inc(self.output_loaded, 16)

    def load_latents(self, sp, nth):
        sp.dma_start(self.raw[0:N, 0, :], self.g.lat[nth]).then_inc(self.lat_loaded, 16)

    def wait_loaded(self, engine, nth):
        engine.wait_ge(self.loaded, 16 * (nth + 1))

    def constants(self, pool):
        for u in range(2):
            pool.memset(self.hi[u][:, :, D:D + 2].bitcast(F32), 1.0)
            last = pool.memset(self.lo[u][:, :, D:D + 2].bitcast(F32), 0.0)
        last.then_inc(self.empty, 1)
        pool.wait_ge(self.empty, 1)
        if self.layer:
            pool.memset(self.raw[N:P, 0, :], 0.0).then_inc(self.empty, 1)
            pool.wait_ge(self.empty, 2)

    def statistics(self, v, chain, nth):
        self.wait_loaded(v, nth)
        norm_stats(v, chain, self.n, self.raw, KT)

    def scales(self, v, chain, nth):
        n = self.n
        v.wait_ge(n.std_ready, nth + 1)
        chain(v.reciprocal(n.rstd[:, :], n.std[:, :]))
        v.tensor_copy(self.g.ctx_mean[:, nth, :], n.mean[:, :])
        v.tensor_copy(self.g.ctx_rstd[:, nth, :], n.rstd[:, :])
        v.scalar_tensor_tensor(out=self.offset[:, :], in0=n.mean[:, :], scalar=-1.0, in1=n.rstd[:, :],
                               op0=ALU.mult, op1=ALU.mult).then_inc(self.scaled, 1)

    def apply_scalar(self, a, nth):
        a.wait_ge(self.scaled, nth + 1)
        for t in range(KT):
            last = a.activation(self.raw[:, t, :], self.raw[:, t, :], ACT.Identity, scale=self.n.rstd[:, t:t + 1],
                                bias=self.offset[:, t:t + 1])
        last.then_inc(self.applied, 1)

    def apply_vector(self, v, nth):
        self.wait_loaded(v, nth)
        mean, rstd = self.g.ctx_mean[:, nth, :], self.g.ctx_rstd[:, nth, :]
        for t in range(KT):
            tile = self.raw[:, self.first + t, :]
            last = v.tensor_scalar(tile, tile, mean[:, t:t + 1], rstd[:, t:t + 1], ALU.subtract, ALU.mult)
        last.then_inc(self.applied, 1)

    def shifts(self, pool, nth, r):
        wide, tiles = [P, 2, D], self.raw[:, self.first + 2 * r:self.first + 2 * r + 2, :]
        pool.wait_ge(self.applied, nth + 1)
        pool.tensor_tensor(tiles, tiles, self.gain[:, None, :].to_broadcast(wide), ALU.mult).then_inc(self.gained, 1)
        pool.wait_ge(self.gained, (KT // 2) * nth + r + 1)
        pool.tensor_tensor(tiles, tiles, self.shift[:, None, :].to_broadcast(wide), ALU.add).then_inc(self.affine, 1)

    def leading_rows(self, a, nth, u):
        a.wait_ge(self.affine, (KT // 2) * (nth + 1))
        if self.layer:
            a.wait_ge(self.lat_loaded, 16 * (nth + 1))
        a.activation(self.hi[u][:, :, 0:D], self.raw[:, :, :], ACT.Copy).then_inc(self.rows_hi, 1)

    def rest_rows(self, pool, nth, u):
        pool.wait_ge(self.rows_hi, nth + 1)
        pool.tensor_tensor(self.lo[u][:, :, 0:D], self.raw[:, :, :], self.hi[u][:, :, 0:D].bitcast(F32),
                           ALU.subtract).then_inc(self.rows_lo, 1)

    def turned_tiles(self, r):
        start = self.first + 2 * (r - self.first)
        return range(max(start, 0), start + 2)

    def turn(self, pe, nth, r):
        if r < self.first:
            pe.wait_ge(self.lat_loaded, 16 * (nth + 1))
        else:
            pe.wait_ge(self.affine, (KT // 2) * nth + r - self.first + 1)
        need(pe, self.turned_lo, self.rounds * nth + r)
        for k in range(KD):
            for c, t in enumerate(self.turned_tiles(r)):
                last = pe.transpose(self.tps[:, k, c * P:c * P + P], self.raw[:, t, k * P:(k + 1) * P],
                                    self.g.ident[:, :])
        last.then_inc(self.turned, 1)

    def turned_cols(self, r):
        tiles = self.turned_tiles(r)
        return slice(tiles[0] * P, (tiles[-1] + 1) * P), self.tps[:, :, 0:len(tiles) * P]

    def leading_turned(self, a, nth, u, r):
        cols, of = self.turned_cols(r)
        a.wait_ge(self.turned, self.rounds * nth + r + 1)
        a.activation(self.hiT[u][:, :, cols], of, ACT.Copy).then_inc(self.turned_hi, 1)

    def rest_turned(self, v, nth, u, r):
        cols, of = self.turned_cols(r)
        v.wait_ge(self.turned_hi, self.rounds * nth + r + 1)
        v.tensor_tensor(self.loT[u][:, :, cols], of, self.hiT[u][:, :, cols].bitcast(F32),
                        ALU.subtract).then_inc(self.turned_lo, 1)


class Weighted:

    def __init__(self, g, sc, ctx, wv, uT, uTps, zps):
        self.g, self.ctx, self.wv, self.uT, self.uTps, self.zps = g, ctx, wv, uT, uTps, zps
        self.zT = g.zT
        tiles = ctx.tiles
        self.ph, self.pl = ([sc.sb(f"p{k}{u}", [P, tiles, P], F32R) for u in range(2)] for k in "hl")
        self.inv = sc.sb("inv", [P, 2])
        self.un = [sc.sb(f"un{u}", [P, D]) for u in range(2)]
        self.ups = sc.ps("ups", [P, 512])
        self.exped, self.led, self.rested = sc.sem("exped"), sc.sem("led"), sc.sem("rested")
        self.summed, self.inverted, self.normed = sc.sem("summed"), sc.sem("inverted"), sc.sem("normed")
        self.sumsT, self.sumsT_copied = sc.sem("sumsT"), sc.sem("sumsT_copied")
        self.valued, self.valued_copied = sc.sem("valued"), sc.sem("valued_copied")

    def exp(self, a, pr, ready, it, j):
        e = it * STEPS + j
        a.wait_ge(ready, e + 1)
        a.activation(pr[:, :, :], pr[:, :, :], ACT.Exp).then_inc(self.exped, 1)
        need(a, self.summed, e - 1)
        a.wait_ge(self.exped, e + 1)
        a.activation(self.ph[j % 2][:, :, :], pr[:, :, :], ACT.Copy).then_inc(self.led, 1)

    def rest(self, engine, pr, it, j):
        engine.wait_ge(self.led, it * STEPS + j + 1)
        engine.tensor_tensor(self.pl[j % 2][:, :, :], pr[:, :, :], self.ph[j % 2][:, :, :].bitcast(F32),
                             ALU.subtract).then_inc(self.rested, 1)

    def sums(self, pe, it, j):
        e, u, ctx = it * STEPS + j, j // PAIRS % 2, self.ctx
        pe.wait_ge(self.rested, e + 1)
        need(pe, self.normed, e)
        if j % PAIRS == 0:
            pe.wait_ge(ctx.rows_lo, it * 2 + j // PAIRS + 1)
        for kt in range(ctx.tiles):
            last = three(pe, self.ups[:, 0:D + 2], (self.ph[j % 2][:, kt, :], self.pl[j % 2][:, kt, :]),
                         (ctx.hi[u][:, kt, :], ctx.lo[u][:, kt, :]), kt == 0, kt == ctx.tiles - 1)
        last.then_inc(self.summed, 1)

    def invert(self, v, it, j):
        e = it * STEPS + j
        v.wait_ge(self.summed, e + 1)
        need(v, self.normed, e - 1)
        v.reciprocal(self.inv[:, j % 2:j % 2 + 1], self.ups[:, D:D + 1]).then_inc(self.inverted, 1)

    def normalise(self, a, it, j):
        e = it * STEPS + j
        a.wait_ge(self.inverted, e + 1)
        need(a, self.sumsT, e - 1)
        a.activation(self.un[j % 2][:, :], self.ups[:, 0:D], ACT.Copy, scale=self.inv[:, j % 2:j % 2 + 1]).then_inc(self.normed, 1)

    def turn_sums(self, pe, it, first, count):
        e = it * STEPS + first
        pe.wait_ge(self.normed, e + count)
        need(pe, self.sumsT_copied, e)
        for c in range(count):
            for k in range(KD):
                last = pe.transpose(self.uTps[:, c, k, :], self.un[(first + c) % 2][:, k * P:(k + 1) * P], self.g.ident[:, :])
        last.then_inc(self.sumsT, count)

    def copy_sumsT(self, a, it, first, count):
        e = it * STEPS + first
        a.wait_ge(self.sumsT, e + count)
        need(a, self.valued, e - count * (len(self.uT) - 1))
        a.activation(self.uT[first // count % len(self.uT)][:, :, :, :], self.uTps, ACT.Copy).then_inc(self.sumsT_copied, count)

    def values(self, pe, it, first, count):
        e = it * STEPS + first
        pe.wait_ge(self.sumsT_copied, e + count)
        need(pe, self.valued_copied, e)
        for c in range(count):
            p = (first + c) % PAIRS
            for k in range(KD):
                last = pe.matmul(self.zps[:, c, :], self.wv[:, k, p * P:(p + 1) * P],
                                 self.uT[first // count % len(self.uT)][:, c, k, :], start=(k == 0), stop=(k == KD - 1))
        last.then_inc(self.valued, count)

    def copy_values(self, a, it, first, count):
        zTb, p = self.zT[:, :, :].rearrange("p h (b n) -> p h b n", n=N), first % PAIRS
        a.wait_ge(self.valued, it * STEPS + first + count)
        for half in range(2):
            part = slice(DH * half, DH * half + DH)
            last = a.activation(zTb[part, p:p + count, it * 2 + first // PAIRS, :],
                                self.zps[part, :, half * N:half * N + N], ACT.Copy)
        last.then_inc(self.valued_copied, count)


def phase_cross0(nc, g, i, ctx, wk, ahead, wv, cos, sin):
    CLIP, LAST = 11.0, 3
    with Scope(nc, "c0") as sc:
        kc, ks, kr = ([sc.sb(f"{k}{u}", [P, S]) for u in range(2)] for k in ("kc", "ks", "kr"))
        pr = sc.sb("pr", [P, KT, P])
        kps = sc.ps("kps", [P, S])
        sps = sc.ps("sps", [P, KT, P])
        uTb, zb = sc.ps("uTb", [P, 512]), sc.ps("zb", [P, 512])
        uT = [sc.sb(f"uT{u}", [P, 1, KD, P]) for u in range(2)]
        w = Weighted(g, sc, ctx, wv, uT, uTb[:, 0:KD * P].rearrange("p (c k q) -> p c k q", c=1, k=KD),
                     zb[:, 0:P].rearrange("p (c q) -> p c q", c=1))
        s = Names(**{name: sc.sem(name) for name in (
            "chain keys multiplied roped scored clipped").split()})
        swapped = [sc.sem(f"swapped{u}") for u in range(2)]
        block = sc.block()

        @block.sync
        def _(sp):
            def swap(it, j):
                sp.wait_ge(s.multiplied, it * STEPS + j + 1)
                for c in range(4):
                    to, of = 32 * c, 32 * (c ^ 1)
                    sp.dma_start(kr[j % 2][to:to + 32, :], ks[j % 2][of:of + 32, :]).then_inc(swapped[j % 2], 16)

            def step(it, j):
                batch, p = j // PAIRS, j % PAIRS
                if p == 1 and there(it, j + PAIRS):
                    ahead.load_blocks(sp, s.scored, settled(sp, it * 2 + batch + 1), (batch + 1) % 2)
                if p == 6 and there(it, j + 2 * PAIRS):
                    ctx.load(sp, settled(sp, it * 2 + batch + 2))
                if there(it, j + 2):
                    swap(it, j + 2)

            ctx.load(sp, 1)
            swap(0, 0)
            swap(0, 1)
            pipelined(sp, step, LAST, STEPS)
            ctx.load_output(sp, i.l0_wo)

        @block.gpsimd
        def _(pool):
            def prepare(nth, u):
                for r in range(KT // 2):
                    ctx.shifts(pool, nth, r)
                ctx.rest_rows(pool, nth, u)

            prepare(1, 1)
            with pool.Fori(0, ITERS - 1) as it:
                for u in range(2):
                    prepare(it * 2 + 2 + u, u)

        @block.vector
        def _(v):
            chain = Chain(v, s.chain)

            def multiply(it, j):
                v.wait_ge(s.keys, it * STEPS + j + 1)
                need(v, s.scored, it * STEPS + j - 1)
                v.tensor_tensor(kc[j % 2][:, :], kps[:, :], cos[:, :], ALU.mult)
                v.tensor_tensor(ks[j % 2][:, :], kps[:, :], sin[:, :], ALU.mult).then_inc(s.multiplied, 1)

            def rope(it, j):
                v.wait_ge(swapped[j % 2], (it * (STEPS // 2) + j // 2 + 1) * 64)
                v.tensor_tensor(kc[j % 2][:, :], kc[j % 2][:, :], kr[j % 2][:, :], ALU.add).then_inc(s.roped, 1)

            def clip(it, j):
                v.wait_ge(s.scored, it * STEPS + j + 1)
                need(v, w.rested, it * STEPS + j)
                v.tensor_scalar(pr[:, :, :], sps[:, :, :], CLIP, -CLIP, ALU.min, ALU.max).then_inc(s.clipped, 1)

            def step(it, j):
                nth, u, p = it * 2 + j // PAIRS + 1, (j // PAIRS + 1) % 2, j % PAIRS
                more = there(it, j + PAIRS)
                if there(it, j - 2):
                    w.invert(v, it, j - 2)
                if there(it, j):
                    clip(it, j)
                if there(it, j + 1):
                    rope(it, j + 1)
                if there(it, j + 2):
                    multiply(it, j + 2)
                if p == 0 and more:
                    ctx.scales(v, chain, nth)
                if there(it, j):
                    w.rest(v, pr, it, j)
                if p == PAIRS - 1 and there(it, j + PAIRS + 1):
                    ctx.statistics(v, chain, nth + 1)
                if 2 <= p <= 5 and more:
                    ctx.rest_turned(v, nth, u, p - 2)

            ahead.wait_loaded(v)
            for c in (1, 3):
                part = slice(32 * c, 32 * c + 32)
                last = v.tensor_scalar(sin[part, :], sin[part, :], -1.0, None, ALU.mult)
            chain(last)
            multiply(0, 0)
            multiply(0, 1)
            rope(0, 0)
            ctx.statistics(v, chain, 1)
            pipelined(v, step, LAST, STEPS, chain, 2 * 4)

        @block.scalar
        def _(a):
            def step(it, j):
                nth, u, p = it * 2 + j // PAIRS + 1, (j // PAIRS + 1) % 2, j % PAIRS
                more = there(it, j + PAIRS)
                if there(it, j - 2):
                    w.normalise(a, it, j - 2)
                if there(it, j):
                    w.exp(a, pr, s.clipped, it, j)
                if p == 0 and more:
                    norm_root(a, ctx.n, nth + 1)
                if p == 1 and more:
                    ctx.apply_scalar(a, nth)
                if there(it, j - 2):
                    w.copy_sumsT(a, it, j - 2, 1)
                if there(it, j - 3):
                    w.copy_values(a, it, j - 3, 1)
                if 2 <= p <= 5 and more:
                    ctx.leading_turned(a, nth, u, p - 2)
                if p == 4 and more:
                    ctx.leading_rows(a, nth, u)

            pipelined(a, step, LAST, STEPS)

        @block.tensor
        def _(pe):
            def keys(it, j):
                e, u, p = it * STEPS + j, j // PAIRS % 2, j % PAIRS
                if p == 0:
                    pe.wait_ge(ctx.turned_lo, (it * 2 + j // PAIRS + 1) * ctx.rounds)
                need(pe, s.multiplied, e)
                cols = slice(p * P, (p + 1) * P)
                for half in range(2):
                    part = slice(half * 512, half * 512 + 512)
                    for k in range(KD):
                        last = three(pe, kps[:, part], (wk.hi[:, k, cols], wk.lo[:, k, cols]),
                                     (ctx.hiT[u][:, k, part], ctx.loT[u][:, k, part]), k == 0, k == KD - 1)
                last.then_inc(s.keys, 1)

            def scores(it, j):
                e, u, p = it * STEPS + j, j // PAIRS % 2, j % PAIRS
                if p == 0:
                    pe.wait_ge(ahead.blocks_loaded[u], (it + j // STEPS + 1) * 32)
                pe.wait_ge(s.roped, e + 1)
                need(pe, s.clipped, e)
                for kt in range(KT):
                    last = pe.matmul(sps[:, kt, :], kc[j % 2][:, kt * P:kt * P + P], ahead.qd[u][:, p, :], start=True, stop=True)
                last.then_inc(s.scored, 1)

            def step(it, j):
                nth, p = it * 2 + j // PAIRS + 1, j % PAIRS
                if there(it, j):
                    scores(it, j)
                if there(it, j + 2):
                    keys(it, j + 2)
                if there(it, j - 2):
                    w.turn_sums(pe, it, j - 2, 1)
                if there(it, j - 3):
                    w.values(pe, it, j - 3, 1)
                if 2 <= p <= 5 and there(it, j + PAIRS):
                    ctx.turn(pe, nth, p - 2)
                if there(it, j - 1):
                    w.sums(pe, it, j - 1)

            keys(0, 0)
            keys(0, 1)
            ahead.wait_loaded(pe)
            pipelined(pe, step, LAST, STEPS)


def phase_out0(nc, g, ctx, bo):
    with Scope(nc, "o0") as sc:
        wo = ctx.raw
        ops = sc.ps("ops", [P, TT, 512])
        biased, out_done = sc.sem("biased"), sc.sem("out_done")
        block = sc.block()

        @block.vector
        def _(v):
            v.tensor_tensor(g.x_tok[:, :, :], g.x_tok[:, :, :], bo[:, None, :].to_broadcast([P, TT, D]),
                            ALU.add).then_inc(biased, 1)
            v.wait_ge(biased, 1)
            for t in range(TT):
                v.wait_ge(out_done, t + 1)
                v.tensor_tensor(g.x_tok[:, t, :], g.x_tok[:, t, :], ops[:, t, 0:D], ALU.add)

        @block.tensor
        def _(pe):
            pe.wait_ge(ctx.output_loaded, 16)
            for t in range(TT):
                for p in range(PAIRS):
                    last = pe.matmul(ops[:, t, 0:D], g.zT[:, p, t * P:(t + 1) * P], wo[:, p, :],
                                     start=(p == 0), stop=(p == PAIRS - 1))
                last.then_inc(out_done, 1)


def turned_norm(sc, name):
    m = Names(y=sc.sb(f"{name}_y", [P, TT, D]), yT=sc.sb(f"{name}_yT", [P, KD, T]))
    m.n = norm_tensors(sc, name, TT)
    m.tps = [sc.ps(f"{name}_tps{k}", [P, T]) for k in range(KD)]
    m.normed, m.turned, m.copied = (sc.sem(f"{name}_{k}") for k in ("normed", "turned", "copied"))
    return m


def turned_norm_vector(v, chain, m, x):
    norm_stats(v, chain, m.n, x, TT)
    norm_apply(v, chain, m.n, 1, x, m.y, TT, m.normed)


def turned_norm_scalar(a, m, between=None):
    norm_root(a, m.n, 1)
    if between:
        between()
    for k in range(KD):
        a.wait_ge(m.turned, k + 1)
        a.activation(m.yT[:, k, :], m.tps[k][:, :], ACT.Copy).then_inc(m.copied, 1)


def turned_norm_tensor(pe, g, m):
    for k in range(KD):
        for t in range(TT):
            if k == 0:
                pe.wait_ge(m.normed, t + 1)
            last = pe.transpose(m.tps[k][:, t * P:(t + 1) * P], m.y[:, t, k * P:(k + 1) * P], g.ident[:, :])
        last.then_inc(m.turned, 1)


def phase_attn0(nc, g, i):
    HS, HH = 16, 8
    UNITS = TT * 2
    LAG = 3
    C4 = 2 * D // P
    G4 = HH // 2
    with Scope(nc, "a0") as sc:
        wqk = sc.sb("wqk", [P, 4, KD, D])
        wv, wc = sc.sb("wv", [P, KD, 2 * D]), sc.sb("wc", [P, C4, D])
        causal, heads = sc.sb("causal", [P, N]), sc.sb("heads", [P, HH])
        masks, unit_matrix = sc.sb("masks", [P, HH, N], BF16), sc.sb("unit_matrix", [P, P], BF16)
        lqk, lamp, lams, lam = sc.sb("lqk", [P, 4, H]), sc.sb("lamp", [P, 2, H]), sc.sb("lams", [P, 2, H]), sc.sb("lam", [P, H])
        chan, ga, gb = sc.sb("chan", [P, 3]), sc.sb("ga", [P, 2]), sc.sb("gb", [P, 1])
        m = turned_norm(sc, "m")
        yT2 = sc.sb("yT2", [P, KD, B, 2, N])
        qkT = sc.sb("qkT", [P, 4, 2, T])
        vd = sc.sb("vd", [P, B, PAIRS, 2 * 32])
        kd = [sc.sb(f"kd{u}", [P, 2, HH, N]) for u in range(4)]
        sm = [sc.sb(f"sm{u}", [P, 2, HH, N]) for u in range(2)]
        mx = [sc.sb(f"mx{u}", [P, 2, HH]) for u in range(2)]
        su, rs = sc.sb("su", [P, 2, HH]), sc.sb("rs", [P, 2, HH])
        att = [sc.sb(f"att{u}", [P, HH, N]) for u in range(2)]
        attT = [sc.sb(f"attT{u}", [P, G4, P]) for u in range(2)]
        y4, yn = sc.sb("y4", [P, C4, T]), sc.sb("yn", [P, C4, T])
        gst = sc.sb("gst", [P, C4 * B, 6])
        gsum, gmean, gdif, gsq, gv, gs, gr, gmg, gshift = (sc.sb(k, [P, C4 * B]) for k in (
            "gsum", "gmean", "gdif", "gsq", "gv", "gs", "gr", "gmg", "gshift"))
        sps = [sc.ps(f"sps{u}", [P, 2, HH, N]) for u in range(2)]
        aps, yps = sc.ps("aps", [P, G4, P]), sc.ps("yps", [P, 512])
        pps = [sps[0][:, a, :, :].rearrange("p h n -> p (h n)") for a in range(2)]
        s = Names(**{name: sc.sem(name) for name in (
            "w_loaded wv_loaded c_loaded wc_loaded twice chain zeroed lam_in lam_out projected taken vprojected vtaken keyed masks_built "
            "scored shifted exped mixed attT attT_copied valued valued_copied gvar gstd gnormed out_done").split()})
        qkps = [aps[:, :, :].rearrange("p c q -> p (c q)"), yps[:, :]]
        vps = [m.tps[u][:, :] for u in range(2)]
        block = sc.block()

        @block.sync
        def _(sp):
            sp.dma_start(lqk[:, :, :], i.a0_lqk).then_inc(s.c_loaded, 16)
            sp.dma_start(chan[:, :], i.a0_chan).then_inc(s.c_loaded, 16)
            sp.dma_start(causal[:, :], i.causal).then_inc(s.c_loaded, 16)
            sp.dma_start(heads[:, :], i.heads).then_inc(s.c_loaded, 16)
            sp.dma_start(wqk[:, :, :, :], i.a0_wqk.rearrange("w (k p) n -> p w k n", p=P)).then_inc(s.w_loaded, 16)
            sp.dma_start(wv[:, :, :], rows(i.a0_wv)).then_inc(s.wv_loaded, 16)
            sp.dma_start(wc[:, :, :], rows(i.a0_wc)).then_inc(s.wc_loaded, 16)

        def build_keys(engine, unit, a):
            t, hh = unit // 2, unit % 2
            k = qkT[:, 2 + a, hh, t * P:(t + 1) * P].rearrange("p (b n) -> p b n", n=N)
            for b in range(2):
                last = engine.tensor_tensor(kd[unit % 2 * 2 + a][:, b, :, :], k[:, b, None, :].to_broadcast([P, HH, N]),
                                            heads[:, :, None].to_broadcast([P, HH, N]), ALU.mult)
            return last

        @block.gpsimd
        def _(pool):
            pool.memset(vd[:, :, :, :], 0.0).then_inc(s.zeroed, 1)
            pool.wait_ge(s.c_loaded, 64)
            pool.tensor_copy(unit_matrix[:, :], g.ident[:, :])
            pool.tensor_copy(masks[:, :, :], causal[:, None, :].to_broadcast([P, HH, N])).then_inc(s.masks_built, 1)
            for unit in range(UNITS):
                if unit < 2:
                    pool.wait_ge(s.taken, 4 * (unit + 1))
                if unit >= 2:
                    pool.wait_ge(s.scored, unit - 1)
                for a in range(2):
                    build_keys(pool, unit, a).then_inc(s.keyed, 1)

        @block.vector
        def _(v):
            chain = Chain(v, s.chain)
            turned_norm_vector(v, chain, m, g.x_tok)
            v.wait_ge(s.c_loaded, 64)
            v.tensor_tensor(lamp[:, :, :], lqk[:, 0:2, :], lqk[:, 2:4, :], ALU.mult).then_inc(s.lam_in, 1)
            v.tensor_scalar(ga[:, :], chan[:, 0:2], chan[:, 2:3], 1.0 - LAMBDA_INIT, ALU.mult, ALU.mult)
            v.wait_ge(s.lam_out, 1)
            chain(v.tensor_tensor(lam[:, :], lams[:, 0, :], lams[:, 1, :], ALU.subtract))
            chain(v.tensor_scalar(lam[:, :], lam[:, :], LAMBDA_INIT, None, ALU.add))
            def shift(unit):
                v.wait_ge(s.scored, unit + 1)
                chain(v.tensor_reduce(mx[unit % 2][:, :, :], sps[unit % 2][:, :, :, :], AX.X, ALU.max))
                if unit >= 2:
                    v.wait_ge(s.mixed, unit - 1)
                v.tensor_tensor(sm[unit % 2][:, :, :, :], sps[unit % 2][:, :, :, :],
                                mx[unit % 2][:, :, :, None].to_broadcast([P, 2, HH, N]), ALU.subtract).then_inc(s.shifted, 1)

            def mix(unit):
                hh = unit % 2
                v.wait_ge(s.exped, unit + 1)
                of = sm[unit % 2]
                chain(v.tensor_reduce(su[:, :, :], of[:, :, :, :], AX.X, ALU.add))
                chain(v.reciprocal(rs[:, :, :], su[:, :, :]))
                chain(v.tensor_tensor(rs[:, 1, :], rs[:, 1, :], lam[:, hh * HH:hh * HH + HH], ALU.mult))
                chain(v.tensor_tensor(of[:, :, :, :], of[:, :, :, :], rs[:, :, :, None].to_broadcast([P, 2, HH, N]), ALU.mult))
                if unit >= 2:
                    v.wait_ge(s.attT, unit - 1)
                v.tensor_tensor(att[unit % 2][:, :, :], of[:, 0, :, :], of[:, 1, :, :], ALU.subtract).then_inc(s.mixed, 1)

            def statistics(unit):
                t, hh = unit // 2, unit % 2
                v.wait_ge(s.valued_copied, unit + 1)
                for c in (2 * hh, 2 * hh + 1):
                    for b in (2 * t, 2 * t + 1):
                        last = v.bn_stats(gst[:, c * B + b, :], y4[:, c, b * N:b * N + N])
                return last

            for unit in range(UNITS + LAG):
                if unit < UNITS:
                    shift(unit)
                if 0 <= unit - 1 < UNITS:
                    mix(unit - 1)
                if unit >= LAG:
                    last = statistics(unit - LAG)
            chain(last)
            even, odd = gst[:, :, 1], gst[:, :, 4]
            v.tensor_tensor(gsum[:, :], even, odd, ALU.add)
            v.tensor_tensor(gdif[:, :], even, odd, ALU.subtract)
            chain(v.tensor_tensor(gsq[:, :], gst[:, :, 2], gst[:, :, 5], ALU.add))
            v.tensor_scalar(gmean[:, :], gsum[:, :], 0.5, None, ALU.mult)
            v.scalar_tensor_tensor(out=gdif[:, :], in0=gdif[:, :], scalar=0.25, in1=gdif[:, :], op0=ALU.mult, op1=ALU.mult)
            chain(v.tensor_scalar(gsq[:, :], gsq[:, :], 1.0 / N, EPS, ALU.mult, ALU.add))
            v.tensor_tensor(gv[:, :], gsq[:, :], gdif[:, :], ALU.add).then_inc(s.gvar, 1)
            v.wait_ge(s.gstd, 1)
            chain(v.reciprocal(gr[:, :], gs[:, :]))
            chain(v.tensor_scalar(gr[:, :], gr[:, :], ga[:, 0:1], None, ALU.mult))
            chain(v.tensor_tensor(gmg[:, :], gmean[:, :], gr[:, :], ALU.mult))
            chain(v.tensor_scalar(gshift[:, :], gmg[:, :], -1.0, ga[:, 1:2], ALU.mult, ALU.add))
            for t in range(TT):
                for c in range(C4):
                    for b in (2 * t, 2 * t + 1):
                        n = c * B + b
                        last = v.tensor_scalar(yn[:, c, b * N:b * N + N], y4[:, c, b * N:b * N + N], gr[:, n:n + 1],
                                               gshift[:, n:n + 1], ALU.mult, ALU.add)
                last.then_inc(s.gnormed, 1)
            for t in range(TT):
                v.wait_ge(s.out_done, t // 2 * 2 + 2)
                v.tensor_tensor(g.x_tok[:, t, :], g.x_tok[:, t, :], pps[t // 2][:, t % 2 * D:t % 2 * D + D], ALU.add)

        @block.scalar
        def _(a):
            turned_norm_scalar(a, m)
            a.wait_ge(s.lam_in, 1)
            a.activation(lams[:, :, :], lamp[:, :, :], ACT.Sigmoid).then_inc(s.lam_out, 1)
            for c in range(8):
                a.wait_ge(s.projected, c + 1)
                a.activation(qkT[:, c % 4, c // 4, :], qkps[c % 2], ACT.Copy).then_inc(s.taken, 1)
            for k in range(KD):
                a.activation(yT2[:, k, :, :, :], m.tps[k][:, :].rearrange("p (b n) -> p b n", n=N)[:, :, None, :]
                             .to_broadcast([P, B, 2, N]), ACT.Copy).then_inc(s.twice, 1)

            def take(b):
                a.wait_ge(s.vprojected, b + 1)
                src = vps[b % 2].rearrange("p (h c e) -> p h c e", c=2, e=32)
                for c in range(2):
                    part = slice(N * c, N * c + N)
                    last = a.activation(vd[part, b, :, 32 * c:32 * c + 32], src[part, :, c, :], ACT.Copy)
                last.then_inc(s.vtaken, 1)

            a.wait_ge(s.zeroed, 1)
            for b in range(2):
                take(b)
            for unit in range(UNITS + 3):
                if unit < UNITS:
                    a.wait_ge(s.shifted, unit + 1)
                    a.activation(sm[unit % 2][:, :, :, :], sm[unit % 2][:, :, :, :], ACT.Exp,
                                 scale=HS ** -0.5).then_inc(s.exped, 1)
                if unit + 2 < B:
                    take(unit + 2)
                if 0 <= unit - 1 < UNITS:
                    w = unit - 1
                    a.wait_ge(s.attT, w + 1)
                    if w >= 2:
                        a.wait_ge(s.valued, w - 1)
                    a.activation(attT[w % 2][:, :, :], aps[:, :, :], ACT.Copy).then_inc(s.attT_copied, 1)
                if 0 <= unit - 2 < UNITS:
                    w = unit - 2
                    t, hh = w // 2, w % 2
                    a.wait_ge(s.valued, w + 1)
                    a.activation(y4[:, 2 * hh:2 * hh + 2, t * P:(t + 1) * P],
                                 yps[:, 0:2 * P].rearrange("p (c q) -> p c q", c=2), ACT.Copy).then_inc(s.valued_copied, 1)
            a.wait_ge(s.gvar, 1)
            a.activation(gs[:, :], gv[:, :], ACT.Sqrt).then_inc(s.gstd, 1)

        @block.tensor
        def _(pe):
            turned_norm_tensor(pe, g, m)
            pe.wait_ge(m.copied, KD)
            pe.wait_ge(s.w_loaded, 16)
            for c in range(8):
                if c >= 2:
                    pe.wait_ge(s.taken, c - 1)
                for k in range(KD):
                    last = pe.matmul(qkps[c % 2], wqk[:, c % 4, k, c // 4 * P:c // 4 * P + P], m.yT[:, k, :],
                                     start=(k == 0), stop=(k == KD - 1))
                last.then_inc(s.projected, 1)
            pe.wait_ge(s.taken, 8)
            pe.wait_ge(s.masks_built, 1)

            def scores(unit):
                t, hh = unit // 2, unit % 2
                if unit >= 2:
                    pe.wait_ge(s.shifted, unit - 1)
                for a in range(2):
                    pe.wait_ge(s.keyed, 2 * unit + a + 1)
                    for b in range(2):
                        q = qkT[:, a, hh, t * P + b * N:t * P + b * N + N]
                        to = sps[unit % 2][b * N:b * N + N, a, :, :].rearrange("p h n -> p (h n)")
                        pe.matmul(to, unit_matrix[:, b * N:b * N + N], masks[:, :, :].rearrange("p h n -> p (h n)"),
                                  start=True, stop=False)
                        last = pe.matmul(to, q,
                                         kd[unit % 2 * 2 + a][:, b, :, :].rearrange("p h n -> p (h n)"),
                                         start=False, stop=True)
                last.then_inc(s.scored, 1)

            def project_values(b):
                if b >= 2:
                    pe.wait_ge(s.vtaken, b - 1)
                for k in range(KD):
                    last = pe.matmul(vps[b % 2], yT2[:, k, b, :, :].rearrange("p c n -> p (c n)"), wv[:, k, :],
                                     start=(k == 0), stop=(k == KD - 1))
                last.then_inc(s.vprojected, 1)

            scores(0)
            pe.wait_ge(s.twice, KD)
            pe.wait_ge(s.wv_loaded, 16)
            project_values(0)
            project_values(1)
            scores(1)
            project_values(2)
            scores(2)
            for unit in range(2, UNITS + 3):
                if unit + 1 < B:
                    project_values(unit + 1)
                if 0 <= unit - 2 < UNITS:
                    w = unit - 2
                    pe.wait_ge(s.mixed, w + 1)
                    if w >= 1:
                        pe.wait_ge(s.attT_copied, w)
                    for c in range(G4):
                        last = pe.transpose(aps[:, c, :], att[w % 2][:, 2 * c:2 * c + 2, :].rearrange("p h n -> p (h n)"),
                                            g.ident[:, :])
                    last.then_inc(s.attT, 1)
                if unit + 1 < UNITS:
                    scores(unit + 1)
                if 0 <= unit - 3 < UNITS:
                    w = unit - 3
                    t, hh = w // 2, w % 2
                    pe.wait_ge(s.attT_copied, w + 1)
                    if hh == 0:
                        pe.wait_ge(s.vtaken, 2 * t + 2)
                    if w >= 1:
                        pe.wait_ge(s.valued_copied, w)
                    for c in range(G4):
                        for b in range(2):
                            to = c // 2 * P + b * N
                            last = pe.matmul(yps[c % 2 * N:c % 2 * N + N, to:to + N], vd[:, 2 * t + b, hh * G4 + c, :],
                                             attT[w % 2][:, c, b * N:b * N + N], start=True, stop=True)
                    last.then_inc(s.valued, 1)
            pe.wait_ge(s.wc_loaded, 16)
            for t in range(TT):
                pe.wait_ge(s.gnormed, t + 1)
                for c in range(C4):
                    last = pe.matmul(pps[t // 2][:, t % 2 * D:t % 2 * D + D], yn[:, c, t * P:(t + 1) * P], wc[:, c, :],
                                     start=(c == 0), stop=(c == C4 - 1))
                last.then_inc(s.out_done, 1)


def phase_ffn0(nc, g, i):
    F = 1024
    M = F // P
    HALF = F // 2
    STAGED, RING = 3, 6
    GATES, SQUARES, TILES = 4, 2 * M, 4 + 2 * M + 2
    with Scope(nc, "f0") as sc:
        staged = [sc.sb(f"staged{u}", [P, F]) for u in range(STAGED)]
        wh, wl = ([sc.sb(f"w{k}{u}", [P, F], F32R) for u in range(RING)] for k in "hl")
        w3s, sca = sc.sb("w3s", [P, D]), sc.sb("sca", [P, 4, M])
        m = turned_norm(sc, "m")
        yh, yl = sc.sb("yh", [P, KD, T], F32R), sc.sb("yl", [P, KD, T], F32R)
        gate, hid = ([sc.sb(f"{k}{u}", [P, T]) for u in range(2)] for k in ("gate", "hid"))
        hh, hl = ([sc.sb(f"h{k}{u}", [P, M, T], F32R) for u in range(2)] for k in "hl")
        t3 = [sc.sb(f"t3{u}", [P, D]) for u in range(2)]
        gp = [sc.ps(f"gp{u}", [P, T]) for u in range(3)]
        up = [sc.ps(f"up{u}", [P, T]) for u in range(3)]
        s = Names(**{name: sc.sem(name) for name in (
            "scales_loaded chain y_hi y_lo w_hi w_lo gated upped silued hidden hidden_hi hidden_lo square gelued "
            "out_done added").split()})
        loaded = [sc.sem(f"loaded{u}") for u in range(STAGED)]
        block = sc.block()

        def tile(n):
            if n < GATES:
                half = n // 2 * HALF
                return rows((i.f0_w1, i.f0_w2)[n % 2])[:, :, half:half + HALF], KD
            if n < GATES + SQUARES:
                layer, c = (n - GATES) // M, (n - GATES) % M
                return rows((i.f0_h1, i.f0_h2)[layer])[:, :, c * P:(c + 1) * P], M
            half = (n - GATES - SQUARES) * (M // 2)
            return rows(i.f0_w3)[:, half:half + M // 2, :], M // 2

        def parts(n, k, cols):
            width = F // tile(n)[1]
            at = slice(k * width + cols.start, k * width + cols.stop)
            return wh[n % RING][:, at], wl[n % RING][:, at]

        @block.sync
        def _(sp):
            for n in range(TILES):
                if n >= STAGED:
                    sp.wait_ge(s.w_lo, n - STAGED + 1)
                source, slices = tile(n)
                sp.dma_start(staged[n % STAGED][:, :].rearrange("p (k n) -> p k n", k=slices), source).then_inc(
                    loaded[n % STAGED], 16)
                if n == 0:
                    sp.dma_start(sca[:, :, :], i.f0_scales).then_inc(s.scales_loaded, 16)
                    sp.dma_start(w3s[:, :], i.f0_w3s).then_inc(s.scales_loaded, 16)

        @block.gpsimd
        def _(pool):
            for n in range(TILES):
                pool.wait_ge(s.w_hi, n + 1)
                pool.tensor_tensor(wl[n % RING][:, :], staged[n % STAGED][:, :], wh[n % RING][:, :].bitcast(F32),
                                   ALU.subtract).then_inc(s.w_lo, 1)

        @block.vector
        def _(v):
            chain = Chain(v, s.chain)
            turned_norm_vector(v, chain, m, g.x_tok)
            for k in range(KD):
                v.wait_ge(s.y_hi, k + 1)
                v.tensor_tensor(yl[:, k, :], m.yT[:, k, :], yh[:, k, :].bitcast(F32), ALU.subtract).then_inc(s.y_lo, 1)

            def rest(nth):
                layer, c = nth // M % 2, nth % M
                v.wait_ge(s.hidden_hi, nth + 1)
                v.tensor_tensor(hl[layer][:, c, :], hid[nth % 2][:, :], hh[layer][:, c, :].bitcast(F32),
                                ALU.subtract).then_inc(s.hidden_lo, 1)

            v.wait_ge(s.scales_loaded, 32)
            for c in range(M):
                v.wait_ge(s.upped, c + 1)
                v.wait_ge(s.silued, c + 1)
                v.scalar_tensor_tensor(out=hid[c % 2][:, :], in0=up[c % 3][:, :], scalar=sca[:, 1, c:c + 1],
                                       in1=gate[c % 2][:, :], op0=ALU.mult, op1=ALU.mult).then_inc(s.hidden, 1)
                rest(c)
            for nth in range(M, 3 * M):
                rest(nth)
            for t in range(TT):
                v.wait_ge(s.out_done, t + 1)
                chain(v.tensor_tensor(t3[t % 2][:, :], up[t % 2][:, 0:D], w3s[:, :], ALU.mult))
                v.tensor_tensor(g.x_tok[:, t, :], g.x_tok[:, t, :], t3[t % 2][:, :], ALU.add).then_inc(s.added, 1)

        @block.scalar
        def _(a):
            def lead(n):
                a.wait_ge(loaded[n % STAGED], 16 * (n // STAGED + 1))
                before = n - RING
                if 0 <= before < GATES:
                    a.wait_ge(s.upped, (before // 2 + 1) * (M // 2))
                elif before >= GATES:
                    a.wait_ge(s.square, before - GATES + 1)
                a.activation(wh[n % RING][:, :], staged[n % STAGED][:, :], ACT.Copy).then_inc(s.w_hi, 1)

            def lead_hidden(nth):
                a.activation(hh[nth // M % 2][:, nth % M, :], hid[nth % 2][:, :], ACT.Copy).then_inc(s.hidden_hi, 1)

            turned_norm_scalar(a, m, lambda: lead(0))
            a.wait_ge(m.copied, KD)
            for k in range(KD):
                a.activation(yh[:, k, :], m.yT[:, k, :], ACT.Copy).then_inc(s.y_hi, 1)
            for n in range(1, GATES):
                lead(n)
            a.wait_ge(s.scales_loaded, 32)
            for c in range(M):
                a.wait_ge(s.gated, c + 1)
                if c >= 2:
                    a.wait_ge(s.hidden, c - 1)
                a.activation(gate[c % 2][:, :], gp[c % 3][:, :], ACT.Silu, scale=sca[:, 0, c:c + 1]).then_inc(s.silued, 1)
                a.wait_ge(s.hidden, c + 1)
                lead_hidden(c)
                if c % 4 < 2:
                    lead(GATES + c // 4 * 2 + c % 4)
            lead(GATES + 4)
            for nth in range(2 * M):
                a.wait_ge(s.square, nth + 1)
                a.wait_ge(s.hidden_lo, M + nth - 1)
                a.activation(hid[nth % 2][:, :], gp[nth % 3][:, :], ACT.Gelu,
                             scale=sca[:, 2 + nth // M, nth % M:nth % M + 1]).then_inc(s.gelued, 1)
                a.wait_ge(s.gelued, nth + 1)
                lead_hidden(M + nth)
                if GATES + 5 + nth < TILES:
                    lead(GATES + 5 + nth)

        @block.tensor
        def _(pe):
            turned_norm_tensor(pe, g, m)
            pe.wait_ge(s.y_lo, KD)
            for c in range(M):
                half = c // (M // 2)
                cols = slice(c % (M // 2) * P, c % (M // 2) * P + P)
                for w, (ps, done, free) in enumerate(((gp, s.gated, s.silued), (up, s.upped, s.hidden))):
                    if cols.start == 0:
                        pe.wait_ge(s.w_lo, 2 * half + w + 1)
                    if c >= 3:
                        pe.wait_ge(free, c - 2)
                    for k in range(KD):
                        last = three(pe, ps[c % 3][:, :], parts(2 * half + w, k, cols), (yh[:, k, :], yl[:, k, :]),
                                     k == 0, k == KD - 1)
                    last.then_inc(done, 1)
            pe.wait_ge(s.silued, M)
            for nth in range(2 * M):
                layer, n = nth // M, GATES + nth
                pe.wait_ge(s.w_lo, n + 1)
                if nth >= 3:
                    pe.wait_ge(s.gelued, nth - 2)
                for k in range(M):
                    if nth % M == 0:
                        pe.wait_ge(s.hidden_lo, layer * M + k + 1)
                    last = three(pe, gp[nth % 3][:, :], parts(n, k, slice(0, P)), (hh[layer][:, k, :], hl[layer][:, k, :]),
                                 k == 0, k == M - 1)
                last.then_inc(s.square, 1)
            pe.wait_ge(s.w_lo, TILES)
            for t in range(TT):
                if t >= 2:
                    pe.wait_ge(s.added, t - 1)
                cols = slice(t * P, (t + 1) * P)
                for k in range(M):
                    if t == 0:
                        pe.wait_ge(s.hidden_lo, 2 * M + k + 1)
                    last = three(pe, up[t % 2][:, 0:D], (hh[0][:, k, cols], hl[0][:, k, cols]),
                                 parts(GATES + SQUARES + k // (M // 2), k % (M // 2), slice(0, D)), k == 0, k == M - 1)
                last.then_inc(s.out_done, 1)


def phase_cross1(nc, g, i, ctx, ahead, wk, wv, mask8):
    K9 = KT + 1
    QQ = 2 * P
    CHUNKS = (K9 + 1) // 2
    BANKS = 3
    PER_BATCH = PAIRS // 2
    PER_ITER = 2 * PER_BATCH
    LAST = 2
    with Scope(nc, "c1") as sc:
        maskb = sc.sb("maskb", [P, B, K9])
        qh, ql = ([sc.sb(f"q{k}{u}", [P, KD, QQ], F32R) for u in range(2)] for k in "hl")
        pr = [sc.sb(f"pr{u}", [P, K9, QQ]) for u in range(2)]
        top, peak = sc.sb("top", [P, QQ]), sc.sb("peak", [P, 2])
        peak_parts, peaks = sc.sb("peak_parts", [P, 2, 2], F32R), sc.sb("peaks", [P, 2, 2, P], F32R)
        ones = sc.sb("ones", [P, P], F32R)
        sps = sc.ps("sps", [P, BANKS, 2, QQ])
        qb, mb, uTb = (sc.ps(k, [P, 512]) for k in ("qb", "mb", "uTb"))
        qaps = qb[:, :].rearrange("p (k q) -> p k q", k=KD)
        topT, peakb = mb[:, 0:QQ].rearrange("p (c q) -> p c q", c=2), mb[:, QQ:2 * QQ].rearrange("p (c q) -> p c q", c=2)
        w = Weighted(g, sc, ctx, wv, [sc.sb("uT", [P, 2, KD, P])],
                     uTb[:, :].rearrange("p (c k q) -> p c k q", c=2, k=KD), topT)
        s = Names(**{name: sc.sem(name) for name in (
            "chain absorbed absorbed_hi absorbed_lo scored masked topped topT peaked "
            "spread shifted").split()})
        block = sc.block()

        def when(j):
            return j // PER_BATCH + 1, (j // PER_BATCH + 1) % 2, j % PER_BATCH

        def part(j, c):
            return pr[j % 2][:, :, c * P:(c + 1) * P]

        @block.sync
        def _(sp):
            def load(nth, u):
                ctx.load(sp, nth)
                ahead.load_blocks(sp, s.absorbed, nth, u)

            load(1, 1)
            with sp.Fori(0, ITERS - 1) as it:
                for u in range(2):
                    load(sp.snap(it * 2 + 2 + u), u)
            ctx.load_output(sp, i.l1_wo)

        @block.gpsimd
        def _(pool):
            def step(it, j):
                nth, u, q = when(j)
                more = there(it, 2 * j + PAIRS)
                for c in range(2):
                    if there(it, 2 * j - 2):
                        w.rest(pool, part(j - 1, c), it, 2 * j - 2 + c)
                    if 1 <= q <= 2 and more:
                        ctx.shifts(pool, it * 2 + nth, 2 * (q - 1) + c)
                if q == 3 and more:
                    ctx.rest_rows(pool, it * 2 + nth, u)

            pipelined(pool, step, LAST, PER_ITER)

        @block.vector
        def _(v):
            chain = Chain(v, s.chain)

            def rest_absorbed(it, j):
                v.wait_ge(s.absorbed_hi, it * PER_ITER + j + 1)
                v.tensor_tensor(ql[j % 2][:, :, :], qaps, qh[j % 2][:, :, :].bitcast(F32),
                                ALU.subtract).then_inc(s.absorbed_lo, 1)

            def masked(it, j):
                e = it * PER_ITER + j
                need(v, w.rested, (e - 1) * 2)
                for c in range(CHUNKS):
                    tiles = slice(2 * c, min(2 * c + 2, K9))
                    count = tiles.stop - tiles.start
                    v.wait_ge(s.scored, e * CHUNKS + c + 1)
                    v.tensor_tensor(pr[j % 2][:, tiles, :], sps[:, c % BANKS, 0:count, :],
                                    maskb[:, it * 2 + j // PER_BATCH, tiles, None].to_broadcast([P, count, QQ]),
                                    ALU.add).then_inc(s.masked, 1)

            def top_of(it, j):
                e = it * PER_ITER + j
                v.wait_ge(s.masked, (e + 1) * CHUNKS)
                need(v, s.topT, e)
                v.tensor_reduce(top[:, :], pr[j % 2][:, :, :].rearrange("p k q -> p q k"), AX.X,
                                ALU.max).then_inc(s.topped, 1)

            def peak_of(it, j):
                e = it * PER_ITER + j
                v.wait_ge(s.topT, e + 1)
                chain(v.tensor_reduce(peak[:, :], topT, AX.X, ALU.max))
                chain(v.tensor_copy(peak_parts[:, 0, :], peak[:, :]))
                chain(v.tensor_tensor(peak_parts[:, 1, :], peak[:, :], peak_parts[:, 0, :].bitcast(F32), ALU.subtract))
                need(v, s.spread, e)
                v.tensor_tensor(peaks[:, :, :, :].rearrange("p a c q -> p (a c) q"), g.ident[:, None, :].to_broadcast([P, 4, P]),
                                peak_parts[:, :, :].bitcast(F32).rearrange("p a c -> p (a c)")[:, :, None]
                                .to_broadcast([P, 4, P]), ALU.mult).then_inc(s.peaked, 1)

            def shift_by_peak(it, j):
                v.wait_ge(s.spread, it * PER_ITER + j + 1)
                for c in range(2):
                    v.tensor_tensor(part(j, c), part(j, c), peakb[:, None, c, :].to_broadcast([P, K9, P]),
                                    ALU.subtract).then_inc(s.shifted, 1)

            def step(it, j):
                nth, u, q = when(j)
                more = there(it, 2 * j + PAIRS)
                if there(it, 2 * j):
                    masked(it, j)
                if q == 3 and more:
                    ctx.rest_turned(v, it * 2 + nth, u, 3)
                if there(it, 2 * j):
                    top_of(it, j)
                if there(it, 2 * j - 2):
                    w.invert(v, it, 2 * j - 2)
                if there(it, 2 * j):
                    peak_of(it, j)
                if 1 <= q and more:
                    ctx.rest_turned(v, it * 2 + nth, u, (0, 1, 4)[q - 1])
                if there(it, 2 * j + 2):
                    rest_absorbed(it, j + 1)
                if there(it, 2 * j - 2):
                    w.invert(v, it, 2 * j - 1)
                if there(it, 2 * j):
                    shift_by_peak(it, j)
                if q == 2 and more:
                    ctx.rest_turned(v, it * 2 + nth, u, 2)
                if q == 0 and more:
                    ctx.apply_vector(v, it * 2 + nth)

            v.memset(maskb[0:N, :, 0], 0.0)
            v.memset(maskb[N:P, :, 0], MASKED)
            ahead.wait_loaded(v)
            chain(v.tensor_scalar(maskb[:, :, 1:K9], mask8[:, :, :], -1.0, -MASKED, ALU.add, ALU.mult))
            v.tensor_copy(ones[:, :], g.ones[:, :])
            rest_absorbed(0, 0)
            pipelined(v, step, LAST, PER_ITER, chain, 3 * PER_ITER)

        @block.scalar
        def _(a):
            def lead_absorbed(it, j):
                e = it * PER_ITER + j
                a.wait_ge(s.absorbed, 2 * (e + 1))
                need(a, s.scored, (e - 1) * CHUNKS)
                a.activation(qh[j % 2][:, :, :], qaps, ACT.Copy).then_inc(s.absorbed_hi, 1)

            def step(it, j):
                nth, u, q = when(j)
                more = there(it, 2 * j + PAIRS)
                if there(it, 2 * j - 2):
                    w.exp(a, part(j - 1, 0), s.shifted, it, 2 * j - 2)
                if there(it, 2 * j - 4):
                    w.copy_sumsT(a, it, 2 * j - 4, 2)
                if q == 3 and more:
                    ctx.leading_turned(a, it * 2 + nth, u, 3)
                if there(it, 2 * j - 2):
                    w.exp(a, part(j - 1, 1), s.shifted, it, 2 * j - 1)
                if there(it, 2 * j - 4):
                    w.copy_values(a, it, 2 * j - 4, 2)
                if q == 3 and more:
                    ctx.leading_rows(a, it * 2 + nth, u)
                if there(it, 2 * j - 2):
                    w.normalise(a, it, 2 * j - 2)
                if 1 <= q and more:
                    ctx.leading_turned(a, it * 2 + nth, u, (0, 1, 4)[q - 1])
                if there(it, 2 * j + 2):
                    lead_absorbed(it, j + 1)
                if there(it, 2 * j - 2):
                    w.normalise(a, it, 2 * j - 1)
                if q == 2 and more:
                    ctx.leading_turned(a, it * 2 + nth, u, 2)

            lead_absorbed(0, 0)
            pipelined(a, step, LAST, PER_ITER)

        @block.tensor
        def _(pe):
            def absorb(it, j):
                e, u = it * PER_ITER + j, j // PER_BATCH % 2
                if j % PER_BATCH == 0:
                    pe.wait_ge(ahead.blocks_loaded[u], (it + j // PER_ITER + 1) * 32)
                need(pe, s.absorbed_lo, e)
                for c in range(2):
                    p = (2 * j + c) % PAIRS
                    for k in range(KD):
                        last = pe.matmul(qaps[:, k, c * P:(c + 1) * P], wk[:, p, k * P:(k + 1) * P], ahead.qd[u][:, p, :],
                                         start=True, stop=True)
                last.then_inc(s.absorbed, 2)

            def scores(it, j, chunks):
                e, u = it * PER_ITER + j, j // PER_BATCH % 2
                if j % PER_BATCH == 0 and chunks[0] == 0:
                    pe.wait_ge(ctx.turned_lo, (it * 2 + j // PER_BATCH + 1) * ctx.rounds)
                if chunks[0] == 0:
                    pe.wait_ge(s.absorbed_lo, e + 1)
                for c in chunks:
                    need(pe, s.masked, e * CHUNKS + (c - BANKS + 1 if c >= BANKS else (-1, 0, -2)[c]))
                    for t in range(2 * c, min(2 * c + 2, K9)):
                        cols = slice(t * P, (t + 1) * P)
                        for k in range(KD):
                            last = three(pe, sps[:, c % BANKS, t % 2, :], (ctx.hiT[u][:, k, cols], ctx.loT[u][:, k, cols]),
                                         (qh[j % 2][:, k, :], ql[j % 2][:, k, :]), k == 0, k == KD - 1)
                    last.then_inc(s.scored, 1)

            def turn_top(it, j):
                e = it * PER_ITER + j
                pe.wait_ge(s.topped, e + 1)
                need(pe, s.shifted, 2 * e)
                need(pe, w.valued_copied, 2 * (e - 1))
                for c in range(2):
                    last = pe.transpose(topT[:, c, :], top[:, c * P:(c + 1) * P], g.ident[:, :])
                last.then_inc(s.topT, 1)

            def spread(it, j):
                pe.wait_ge(s.peaked, it * PER_ITER + j + 1)
                for part_of in range(2):
                    last = pe.matmul(peakb, ones[:, :], peaks[:, part_of, :, :], start=(part_of == 0), stop=(part_of == 1))
                last.then_inc(s.spread, 1)

            def step(it, j):
                nth, u, q = when(j)
                more = there(it, 2 * j + PAIRS)
                if there(it, 2 * j):
                    scores(it, j, range(2))
                if there(it, 2 * j - 4):
                    w.turn_sums(pe, it, 2 * j - 4, 2)
                if q == 3 and more:
                    ctx.turn(pe, it * 2 + nth, 3)
                if there(it, 2 * j):
                    scores(it, j, range(2, CHUNKS))
                if there(it, 2 * j - 4):
                    if there(it, 2 * j - 2):
                        pe.wait_ge(s.shifted, 2 * (it * PER_ITER + j))
                    w.values(pe, it, 2 * j - 4, 2)
                if there(it, 2 * j - 2):
                    w.sums(pe, it, 2 * j - 2)
                if there(it, 2 * j + 2):
                    absorb(it, j + 1)
                if there(it, 2 * j):
                    turn_top(it, j)
                if 1 <= q and more:
                    ctx.turn(pe, it * 2 + nth, (0, 1, 4)[q - 1])
                if there(it, 2 * j - 2):
                    w.sums(pe, it, 2 * j - 1)
                if there(it, 2 * j):
                    spread(it, j)
                if q == 2 and more:
                    ctx.turn(pe, it * 2 + nth, 2)

            ahead.wait_loaded(pe)
            absorb(0, 0)
            pipelined(pe, step, LAST, PER_ITER)


def phase_out1(nc, g, ctx, og, ob):
    with Scope(nc, "o1") as sc:
        wo = ctx.raw
        gained = sc.sb("gained", [P, TT, D])
        norms = [norm_tensors(sc, f"n{t}", 1) for t in range(TT)]
        ops = sc.ps("ops", [P, TT, 512])
        chain_sem, out_done = sc.sem("chain"), sc.sem("out_done")
        block = sc.block()

        @block.vector
        def _(v):
            chain = Chain(v, chain_sem)
            chain(v.tensor_tensor(g.x_tok[:, :, :], g.x_tok[:, :, :], ob[:, None, :].to_broadcast([P, TT, D]), ALU.add))
            for t in range(TT):
                v.wait_ge(out_done, t + 1)
                n = norms[t]
                norm_stats(v, chain, n, ops[:, t:t + 1, :], 1)
                chain(v.scalar_tensor_tensor(out=gained[:, t, :], in0=ops[:, t, 0:D], scalar=n.mean[:, 0:1], in1=og[:, :],
                                             op0=ALU.subtract, op1=ALU.mult))
                v.wait_ge(n.std_ready, 1)
                chain(v.reciprocal(n.rstd[:, :], n.std[:, :]))
                v.scalar_tensor_tensor(out=g.x_tok[:, t, :], in0=gained[:, t, :], scalar=n.rstd[:, 0:1],
                                       in1=g.x_tok[:, t, :], op0=ALU.mult, op1=ALU.add)

        @block.scalar
        def _(a):
            for n in norms:
                norm_root(a, n, 1)

        @block.tensor
        def _(pe):
            pe.wait_ge(ctx.output_loaded, 16)
            for t in range(TT):
                for p in range(PAIRS):
                    last = pe.matmul(ops[:, t, 0:D], g.zT[:, p, t * P:(t + 1) * P], wo[:, p, :],
                                     start=(p == 0), stop=(p == PAIRS - 1))
                last.then_inc(out_done, 1)


def phase_attn1(nc, g, i):
    HN, HD = 8, P
    UNITS = TT
    HP = HN // 2
    with Scope(nc, "a1") as sc:
        wq, wkv, wo = sc.sb("wq", [P, KD, HN * HD]), sc.sb("wkv", [P, KD, 2 * HD]), sc.sb("wo", [P, HN, D])
        bqk, bv, pos = sc.sb("bqk", [P, HN + 1]), sc.sb("bv", [P, HD]), sc.sb("pos", [P, N])
        causal = sc.sb("causal", [P, N])
        m = turned_norm(sc, "m")
        qT = sc.sb("qT", [P, B, HN, N])
        kT = sc.sb("kT", [P, B, N])
        vr = sc.sb("vr", [N, B, HD])
        sm = [sc.sb(f"sm{u}", [P, 2, HP, N]) for u in range(UNITS)]
        mx, su, rs = sc.sb("mx", [P, 2, HP]), sc.sb("su", [P, 2, HP]), sc.sb("rs", [P, 2, HP])
        pT = [sc.sb(f"pT{u}", [N, HN * N]) for u in range(2)]
        oT = sc.sb("oT", [P, HN, T])
        pps = [sc.ps(f"pps{u}", [P, T]) for u in range(2)]
        sps = [sc.ps(f"sps{u}", [P, 2, HP, N]) for u in range(2)]
        ptps, ops = sc.ps("ptps", [N, HN * N]), sc.ps("ops", [P, HN, N])
        s = Names(**{name: sc.sem(name) for name in (
            "w_loaded t_loaded wo_loaded chain projected taken scored shifted exped probs turned turned_copied summed "
            "summed_copied out_done added").split()})
        block = sc.block()

        @block.sync
        def _(sp):
            for to, of in ((bqk, i.a1_bqk), (bv, i.a1_bv), (pos, i.a1_pos), (causal, i.causal)):
                sp.dma_start(to[:, :], of).then_inc(s.t_loaded, 16)
            sp.dma_start(wq[:, :, :], rows(i.a1_wq)).then_inc(s.w_loaded, 16)
            sp.dma_start(wkv[:, :, :], rows(i.a1_wkv)).then_inc(s.w_loaded, 16)
            sp.dma_start(wo[:, :, :], rows(i.a1_wo)).then_inc(s.wo_loaded, 16)

        @block.vector
        def _(v):
            chain = Chain(v, s.chain)
            turned_norm_vector(v, chain, m, g.x_tok)
            v.wait_ge(s.t_loaded, 64)
            by_batch = lambda t: t.rearrange("p (b n) -> p b n", n=N)
            for c in range(HN + 1):
                v.wait_ge(s.projected, c + 1)
                v.scalar_tensor_tensor(out=kT[:, :, :] if c == 0 else qT[:, :, c - 1, :], in0=by_batch(pps[c % 2][:, :]),
                                       scalar=bqk[:, c:c + 1], in1=pos[:, None, :].to_broadcast([P, B, N]),
                                       op0=ALU.add, op1=ALU.add).then_inc(s.taken, 1)
            for c in range(2):
                v.wait_ge(s.projected, HN + 1 + c + 1)
                v.tensor_tensor(vr[:, 4 * c:4 * c + 4, :], pps[(HN + 1 + c) % 2][0:N, :].rearrange("p (b e) -> p b e", b=4),
                                bv[0:N, None, :].to_broadcast([N, 4, HD]), ALU.add).then_inc(s.taken, 1)

            def shift(unit):
                v.wait_ge(s.scored, unit + 1)
                to = sm[unit]
                for b in range(2):
                    last = v.scalar_tensor_tensor(out=to[:, b, :, :], in0=sps[unit % 2][:, b, :, :], scalar=HD ** -0.5,
                                                  in1=causal[:, None, :].to_broadcast([P, HP, N]), op0=ALU.mult, op1=ALU.add)
                chain(last)
                chain(v.tensor_reduce(mx[:, :, :], to[:, :, :, :], AX.X, ALU.max))
                v.tensor_tensor(to[:, :, :, :], to[:, :, :, :], mx[:, :, :, None].to_broadcast([P, 2, HP, N]),
                                ALU.subtract).then_inc(s.shifted, 1)

            def normalise(unit):
                v.wait_ge(s.exped, unit + 1)
                of = sm[unit]
                chain(v.tensor_reduce(su[:, :, :], of[:, :, :, :], AX.X, ALU.add))
                chain(v.reciprocal(rs[:, :, :], su[:, :, :]))
                v.tensor_tensor(of[:, :, :, :], of[:, :, :, :], rs[:, :, :, None].to_broadcast([P, 2, HP, N]),
                                ALU.mult).then_inc(s.probs, 1)

            for unit in range(UNITS + 1):
                if unit < UNITS:
                    shift(unit)
                if unit >= 1:
                    normalise(unit - 1)
            for t in range(TT):
                v.wait_ge(s.out_done, t + 1)
                v.tensor_tensor(g.x_tok[:, t, :], g.x_tok[:, t, :], pps[t % 2][:, 0:D], ALU.add).then_inc(s.added, 1)

        @block.scalar
        def _(a):
            turned_norm_scalar(a, m)

            def exp(unit):
                a.wait_ge(s.shifted, unit + 1)
                a.activation(sm[unit][:, :, :, :], sm[unit][:, :, :, :], ACT.Exp).then_inc(s.exped, 1)

            exp(0)
            exp(1)
            for b in range(B + 1):
                if b < B:
                    a.wait_ge(s.turned, b + 1)
                    if b >= 2:
                        a.wait_ge(s.summed, b - 1)
                    a.activation(pT[b % 2][:, :], ptps[:, :], ACT.Copy).then_inc(s.turned_copied, 1)
                if b < 2:
                    exp(b + 2)
                if b >= 1:
                    w = b - 1
                    a.wait_ge(s.summed, w + 1)
                    a.activation(oT[:, :, w * N:w * N + N], ops[:, :, :], ACT.Copy).then_inc(s.summed_copied, 1)

        @block.tensor
        def _(pe):
            turned_norm_tensor(pe, g, m)
            pe.wait_ge(m.copied, KD)
            pe.wait_ge(s.w_loaded, 32)
            for c in range(HN + 1):
                if c >= 2:
                    pe.wait_ge(s.taken, c - 1)
                for k in range(KD):
                    w = wkv[:, k, 0:HD] if c == 0 else wq[:, k, (c - 1) * HD:c * HD]
                    last = pe.matmul(pps[c % 2][:, :], w, m.yT[:, k, :], start=(k == 0), stop=(k == KD - 1))
                last.then_inc(s.projected, 1)
            for c in range(2):
                nth = HN + 1 + c
                pe.wait_ge(s.taken, nth - 1)
                for b in range(4):
                    at = (4 * c + b) * N
                    for k in range(KD):
                        last = pe.matmul(pps[nth % 2][0:N, b * HD:(b + 1) * HD], m.yT[:, k, at:at + N],
                                         wkv[:, k, HD:2 * HD], start=(k == 0), stop=(k == KD - 1))
                last.then_inc(s.projected, 1)
            pe.wait_ge(s.taken, HN + 3)

            def scores(unit):
                if unit >= 2:
                    pe.wait_ge(s.shifted, unit - 1)
                for b in range(2):
                    for h in range(HP):
                        q = qT[:, 2 * unit + b, 2 * h:2 * h + 2, :].rearrange("p h n -> p (h n)")
                        last = pe.matmul(sps[unit % 2][:, b, h, :], q, kT[:, 2 * unit + b, :], start=True, stop=True)
                last.then_inc(s.scored, 1)

            for unit in range(3):
                scores(unit)
            pe.wait_ge(s.wo_loaded, 16)

            def out(t):
                if t >= 2:
                    pe.wait_ge(s.added, t - 1)
                pe.wait_ge(s.summed_copied, 2 * t + 2)
                for h in range(HN):
                    last = pe.matmul(pps[t % 2][:, 0:D], oT[:, h, t * P:(t + 1) * P], wo[:, h, :],
                                     start=(h == 0), stop=(h == HN - 1))
                last.then_inc(s.out_done, 1)

            for b in range(B + 1):
                unit = b // 2
                if b < B:
                    if b % 2 == 0:
                        pe.wait_ge(s.probs, unit + 1)
                    if b >= 1:
                        pe.wait_ge(s.turned_copied, b)
                    for h in range(HP):
                        last = pe.transpose(ptps[:, h * P:(h + 1) * P], sm[unit][:, b % 2, h, :], g.ident[:, :])
                    last.then_inc(s.turned, 1)
                if b >= 1:
                    w = b - 1
                    pe.wait_ge(s.turned_copied, w + 1)
                    if w >= 1:
                        pe.wait_ge(s.summed_copied, w)
                    pe.matmul(ops[:, :, :].rearrange("p h n -> p (h n)"), vr[:, w, :], pT[w % 2][:, :],
                              start=True, stop=True).then_inc(s.summed, 1)
                if b == 0:
                    scores(3)
                if b >= 3 and b % 2 == 1:
                    out((b - 3) // 2)
            out(TT - 1)


def phase_experts(nc, g, i):
    E, GROUPS, PER, TOP_GROUPS = EXPERTS, 4, EXPERTS // 4, 2
    ALL = E + 2
    RING, AHEAD = 4, 3
    with Scope(nc, "e1") as sc:
        we = [sc.sb(f"we{u}", [P, 3 * D]) for u in range(RING)]
        wh, wl = ([sc.sb(f"w{k}{u}", [P, 3 * D], F32R) for u in range(RING)] for k in "hl")
        yh, yl = sc.sb("yh", [P, KD, T], F32R), sc.sb("yl", [P, KD, T], F32R)
        hh, hl = ([sc.sb(f"h{k}{u}", [P, T], F32R) for u in range(2)] for k in "hl")
        gw, gbias, below = sc.sb("gw", [P, KD, E]), sc.sb("gbias", [P, E]), sc.sb("below", [P, GROUPS, GROUPS])
        m = turned_norm(sc, "m")
        score, choice, masked, left = (sc.sb(k, [P, TT, E]) for k in ("score", "choice", "masked", "left"))
        best = sc.sb("best", [P, TT, GROUPS, 8])
        gsum, rank, gmask = (sc.sb(k, [P, TT, GROUPS]) for k in ("gsum", "rank", "gmask"))
        more, same = sc.sb("more", [P, TT, GROUPS, GROUPS]), sc.sb("same", [P, TT, GROUPS, GROUPS])
        best8 = sc.sb("best8", [P, TT, 8])
        wsum = sc.sb("wsum", [P, TT])
        weight = sc.sb("weight", [P, TT, ALL])
        act = [sc.sb(f"act{u}", [P, T]) for u in range(2)]
        hid = [sc.sb(f"hid{u}", [P, T]) for u in range(2)]
        gps, ups = m.tps, [sc.ps(f"ups{u}", [P, T]) for u in range(2)]
        dps = [sc.ps(f"dps{u}", [P, TT, D]) for u in range(2)]
        s = Names(**{name: sc.sem(name) for name in (
            "t_loaded chain gated scored y_hi y_lo w_hi w_lo gate_done up_done silued hidden hidden_hi hidden_lo "
            "down_done added").split()})
        loaded = [sc.sem(f"loaded{u}") for u in range(RING)]
        block = sc.block()

        @block.sync
        def _(sp):
            def load(e, u):
                sp.dma_start(we[u][:, :], i.e1_w[e]).then_inc(loaded[u], 16)

            sp.dma_start(gw[:, :, :], rows(i.e1_gw)).then_inc(s.t_loaded, 16)
            sp.dma_start(gbias[:, :], i.e1_bias).then_inc(s.t_loaded, 16)
            sp.dma_start(below[:, :, :], i.e1_below).then_inc(s.t_loaded, 16)
            for u in range(RING):
                load(u, u)
            with sp.Fori(0, E // RING - 1) as it:
                for u in range(RING):
                    e = sp.snap(it * RING + u + RING)
                    sp.wait_ge(s.w_lo, it * RING + u + 1)
                    load(e, u)
            for u in range(2):
                sp.wait_ge(s.w_lo, E - RING + u + 1)
                load(E + u, u)

        @block.gpsimd
        def _(pool):
            def rest(e, u):
                pool.wait_ge(s.w_hi, e + 1)
                pool.tensor_tensor(wl[u % RING][:, :], we[u % RING][:, :], wh[u % RING][:, :].bitcast(F32),
                                   ALU.subtract).then_inc(s.w_lo, 1)

            with pool.Fori(0, E // RING) as it:
                for u in range(RING):
                    rest(it * RING + u, u)
            rest(E, E)
            rest(E + 1, E + 1)

        @block.vector
        def _(v):
            chain = Chain(v, s.chain)
            turned_norm_vector(v, chain, m, g.x_tok)
            for k in range(KD):
                v.wait_ge(s.y_hi, k + 1)
                v.tensor_tensor(yl[:, k, :], m.yT[:, k, :], yh[:, k, :].bitcast(F32), ALU.subtract).then_inc(s.y_lo, 1)
            v.memset(weight[:, :, E:ALL], 1.0)
            v.wait_ge(s.scored, 1)
            v.wait_ge(s.t_loaded, 48)
            chain(v.tensor_tensor(choice[:, :, :], score[:, :, :], gbias[:, None, :].to_broadcast([P, TT, E]), ALU.add))
            for t in range(TT):
                for q in range(GROUPS):
                    last = v.max(best[:, t, q, :], choice[:, t, q * PER:(q + 1) * PER])
            chain(last)
            chain(v.tensor_tensor(gsum[:, :, :], best[:, :, :, 0], best[:, :, :, 1], ALU.add))
            wide = [P, TT, GROUPS, GROUPS]
            other, own = gsum[:, :, None, :].to_broadcast(wide), gsum[:, :, :, None].to_broadcast(wide)
            v.tensor_tensor(more[:, :, :, :], other, own, ALU.is_gt)
            chain(v.tensor_tensor(same[:, :, :, :], other, own, ALU.is_equal))
            flat = lambda t: t[:, :, :, :].rearrange("p t a b -> p t (a b)")
            chain(v.tensor_tensor(flat(same), flat(same), below[:, :, :].rearrange("p a b -> p (a b)")[:, None, :]
                                  .to_broadcast([P, TT, GROUPS * GROUPS]), ALU.mult))
            chain(v.tensor_tensor(more[:, :, :, :], more[:, :, :, :], same[:, :, :, :], ALU.add))
            chain(v.tensor_reduce(rank[:, :, :], more[:, :, :, :], AX.X, ALU.add))
            chain(v.tensor_scalar(gmask[:, :, :], rank[:, :, :], TOP_GROUPS - 0.5, None, ALU.is_lt))
            grouped = lambda t: t[:, :, :].rearrange("p t (a b) -> p t a b", b=PER)
            chain(v.tensor_tensor(grouped(masked), grouped(choice), gmask[:, :, :, None].to_broadcast([P, TT, GROUPS, PER]),
                                  ALU.mult))
            chain(v.tensor_scalar(masked[:, :, :], masked[:, :, :], 0.0, None, ALU.add))
            for t in range(TT):
                last = v.max(best8[:, t, :], masked[:, t, :])
            chain(last)
            for t in range(TT):
                last = v.match_replace(out=left[:, t, :], in_to_replace=best8[:, t, :], in_values=masked[:, t, :],
                                       imm_value=MASKED)
            chain(last)
            chain(v.tensor_scalar(left[:, :, :], left[:, :, :], MASKED / 2, None, ALU.is_lt))
            chain(v.tensor_tensor(masked[:, :, :], left[:, :, :], score[:, :, :], ALU.mult))
            chain(v.tensor_reduce(wsum[:, :], masked[:, :, :], AX.X, ALU.add))
            chain(v.tensor_scalar(wsum[:, :], wsum[:, :], 1e-20, None, ALU.add))
            chain(v.reciprocal(wsum[:, :], wsum[:, :]))
            chain(v.tensor_scalar(wsum[:, :], wsum[:, :], ROUTED_SCALING, None, ALU.mult))
            chain(v.tensor_tensor(weight[:, :, 0:E], masked[:, :, :], wsum[:, :, None].to_broadcast([P, TT, E]), ALU.mult))

            def hide(e, u):
                v.wait_ge(s.silued, e + 1)
                v.wait_ge(s.up_done, e + 1)
                v.tensor_tensor(hid[u % 2][:, :], ups[u % 2][:, :], act[u % 2][:, :], ALU.mult).then_inc(s.hidden, 1)

            def rest(e, u):
                v.wait_ge(s.hidden_hi, e + 1)
                v.tensor_tensor(hl[u % 2][:, :], hid[u % 2][:, :], hh[u % 2][:, :].bitcast(F32),
                                ALU.subtract).then_inc(s.hidden_lo, 1)

            def add(e, u):
                v.wait_ge(s.down_done, e + 1)
                for t in range(TT):
                    last = v.scalar_tensor_tensor(out=g.x_tok[:, t, :], in0=dps[u % 2][:, t, :], scalar=weight[:, t, e:e + 1]
                                                  if isinstance(e, int) else weight[:, t, bass.ds(e, 1)],
                                                  in1=g.x_tok[:, t, :], op0=ALU.mult, op1=ALU.add)
                last.then_inc(s.added, 1)

            hide(0, 0)
            rest(0, 0)
            with v.Fori(0, E // RING) as it:
                for u in range(RING):
                    e = it * RING + u
                    hide(e + 1, u + 1)
                    add(e, u)
                    rest(e + 1, u + 1)
                    v.wait_ge(s.added, e + 1)
            hide(E + 1, E + 1)
            add(E, E)
            rest(E + 1, E + 1)
            v.wait_ge(s.added, E + 1)
            add(E + 1, E + 1)

        @block.scalar
        def _(a):
            def lead(e, u, turn=0):
                a.wait_ge(loaded[u % RING], (turn + 1 + u // RING) * 16)
                if not isinstance(e, int) or e >= RING:
                    a.wait_ge(s.down_done, e - RING + 1)
                a.activation(wh[u % RING][:, :], we[u % RING][:, :], ACT.Copy).then_inc(s.w_hi, 1)

            turned_norm_scalar(a, m, lambda: lead(0, 0))
            a.wait_ge(m.copied, KD)
            for k in range(KD):
                a.activation(yh[:, k, :], m.yT[:, k, :], ACT.Copy).then_inc(s.y_hi, 1)
            for e in range(1, AHEAD):
                lead(e, e)
            a.wait_ge(s.gated, 1)
            a.activation(score[:, :, :], ups[1][:, 0:TT * E].rearrange("p (t e) -> p t e", t=TT), ACT.Sigmoid).then_inc(s.scored, 1)

            def silu(e, u, free):
                a.wait_ge(s.gate_done, e + 1)
                if free is not None:
                    a.wait_ge(s.hidden, free)
                a.activation(act[u % 2][:, :], gps[u % 2][:, :], ACT.Silu).then_inc(s.silued, 1)

            def lead_hidden(e, u):
                a.wait_ge(s.hidden, e + 1)
                if not isinstance(e, int) or e >= 2:
                    a.wait_ge(s.down_done, e - 1)
                a.activation(hh[u % 2][:, :], hid[u % 2][:, :], ACT.Copy).then_inc(s.hidden_hi, 1)

            def step(e, u, turn=0):
                if not isinstance(e, int) or e + AHEAD < ALL:
                    lead(e + AHEAD, u + AHEAD, turn)
                if not isinstance(e, int) or e + 2 < ALL:
                    silu(e + 2, u + 2, e + 1)
                if not isinstance(e, int) or e + 1 < ALL:
                    lead_hidden(e + 1, u + 1)

            silu(0, 0, None)
            lead_hidden(0, 0)
            silu(1, 1, None)
            step(0, 0)
            with a.Fori(0, (ALL - AHEAD) // RING) as it:
                for u in range(1, RING + 1):
                    step(it * RING + u, u, it)
            for e in range(((ALL - AHEAD) // RING) * RING + 1, ALL):
                step(e, e)

        @block.tensor
        def _(pe):
            turned_norm_tensor(pe, g, m)
            pe.wait_ge(m.copied, KD)
            pe.wait_ge(s.t_loaded, 48)
            for t in range(TT):
                for k in range(KD):
                    last = pe.matmul(ups[1][:, t * E:(t + 1) * E], m.yT[:, k, t * P:(t + 1) * P], gw[:, k, :],
                                     start=(k == 0), stop=(k == KD - 1))
            last.then_inc(s.gated, 1)

            def gate_up(e, u, free):
                pe.wait_ge(s.w_lo, e + 1)
                for o, ps, done, used in ((0, gps, s.gate_done, s.silued), (D, ups, s.up_done, s.hidden)):
                    if free is not None:
                        pe.wait_ge(used, free)
                    for k in range(KD):
                        cols = slice(o + k * P, o + (k + 1) * P)
                        last = three(pe, ps[u % 2][:, :], (wh[u % RING][:, cols], wl[u % RING][:, cols]),
                                     (yh[:, k, :], yl[:, k, :]), k == 0, k == KD - 1)
                    last.then_inc(done, 1)

            def down(e, u, free):
                pe.wait_ge(s.hidden_lo, e + 1)
                if free is not None:
                    pe.wait_ge(s.added, free)
                for t in range(TT):
                    cols = slice(t * P, (t + 1) * P)
                    last = three(pe, dps[u % 2][:, t, :], (hh[u % 2][:, cols], hl[u % 2][:, cols]),
                                 (wh[u % RING][:, 2 * D:3 * D], wl[u % RING][:, 2 * D:3 * D]), True, True)
                last.then_inc(s.down_done, 1)

            pe.wait_ge(s.y_lo, KD)
            gate_up(0, 0, None)
            pe.wait_ge(s.scored, 1)
            gate_up(1, 1, None)
            with pe.Fori(0, E // RING) as it:
                for u in range(RING):
                    e = it * RING + u
                    gate_up(e + 2, u + 2, e + 1)
                    down(e, u, None)
            down(E, E, E - 1)
            down(E + 1, E + 1, E)


def phase_store(nc, g, o):
    with Scope(nc, "store") as sc:
        stored = sc.sem("stored")
        block = sc.block()

        @block.sync
        def _(sp):
            sp.dma_start(o.rearrange("(t p) d -> p t d", p=P), g.x_tok[:, :, :]).then_inc(stored, 16)
            sp.wait_ge(stored, 16)


def build(nc, i, o, only=range(6)):
    with Scope(nc, "g") as sc:
        g = Names(
            x_tok=sc.sb("x_tok", [P, TT, D]), ident=sc.sb("ident", [P, P]), ones=sc.sb("ones", [P, P]),
            ctx_mean=sc.sb("ctx_mean", [P, B, KT]), ctx_rstd=sc.sb("ctx_rstd", [P, B, KT]))
        g.x_loaded = sc.sem("x_loaded")
        phase_setup(nc, g, i, 0 not in only)
        g.q = nc.dram_tensor("q", (P, PAIRS, T), F32, kind="Internal").ap()
        g.lat = nc.dram_tensor("lat", (B, N, D), F32, kind="Internal").ap()
        if 0 in only:
            with Scope(nc, "x0") as sx:
                g.zT = sx.sb("zT", [P, PAIRS, T])
                ctx = Context(g, i, 0, sx)
                wk = Names(source=i.l0_wk, staged=g.zT[:, 0:4, :].rearrange("p (k a) t -> p k (a t)", k=KD),
                           hi=sx.sb("wk_hi", [P, KD, H * DH], F32R), lo=sx.sb("wk_lo", [P, KD, H * DH], F32R))
                wv, cos, sin = sx.sb("wv", [P, KD, H * DH]), sx.sb("cos", [P, S]), sx.sb("sin", [P, S])
                bo = sx.sb("bo", [P, D])
                ahead = Ahead(g, sx, [(cos[:, :], i.l0_cos), (sin[:, :], i.l0_sin), (wv[:, :, :], rows(i.l0_wv)),
                                       (bo[:, :], i.l0_bo)])
                phase_queries(nc, g, i, 0, i.l0_wq, i.l0_lat_g, i.l0_lat_b, ctx, wk, ahead)
                phase_cross0(nc, g, i, ctx, wk, ahead, wv, cos, sin)
                phase_out0(nc, g, ctx, bo)
        if 1 in only:
            phase_attn0(nc, g, i)
        if 2 in only:
            phase_ffn0(nc, g, i)
        if 3 in only:
            with Scope(nc, "x1") as sx:
                g.zT = sx.sb("zT", [P, PAIRS, T])
                ctx = Context(g, i, 1, sx)
                wk, wv = sx.sb("wk", [P, PAIRS, D]), sx.sb("wv", [P, KD, H * DH])
                mask8, og, ob = sx.sb("mask8", [P, B, KT], U8), sx.sb("og", [P, D]), sx.sb("ob", [P, D])
                ahead = Ahead(g, sx, [(wk[:, :, :], rows(i.l1_wkT)), (wv[:, :, :], rows(i.l1_wv)), (mask8[:, :, :], i.mask),
                                       (og[:, :], i.l1_out_g), (ob[:, :], i.l1_out_b)])
                phase_queries(nc, g, i, 1, i.l1_wq, i.l1_lat_g, i.l1_lat_b, ctx, None, ahead)
                phase_cross1(nc, g, i, ctx, ahead, wk, wv, mask8)
                phase_out1(nc, g, ctx, og, ob)
        if 4 in only:
            phase_attn1(nc, g, i)
        if 5 in only:
            phase_experts(nc, g, i)
        phase_store(nc, g, o)


def laid_out(a):
    wide = lambda v: np.ascontiguousarray(np.broadcast_to(v, (P, v.shape[-1])))
    keyed = lambda c: np.ascontiguousarray(
        np.tile(c.reshape(P, KT, -1).transpose(2, 1, 0).reshape(-1, S), (4, 1)))
    c = np.ascontiguousarray
    per = lambda v: c(v.reshape(-1, P).T)
    tiled = lambda v, n: np.tile(v, P // n)
    head = np.arange(P)[:, None] // 16 == np.arange(8)
    query, key = np.arange(P)[:, None] % N, np.arange(N)[None, :]
    w1, b1 = a["L1_attn_Wkv"], a["L1_attn_bkv"]
    pos = np.arange(N, dtype=np.float32)[:, None]
    ang = pos * np.exp(-np.log(np.float32(10000.0)) * np.arange(0, P, 2, dtype=np.float32) / np.float32(P))[None, :]
    pe = np.zeros((N, P), np.float32)
    pe[:, 0::2], pe[:, 1::2] = np.sin(ang), np.cos(ang)
    gates = lambda w: w.transpose(0, 2, 1).reshape(-1, KD, P, P).transpose(0, 2, 1, 3).reshape(-1, P, D)
    both = lambda k: np.concatenate([a[f"L1_ffn_expert_{k}"], a[f"L1_ffn_shared_{k}"].reshape(2, P, D)])
    down = np.concatenate([a["L1_ffn_expert_down"].transpose(0, 2, 1), a["L1_ffn_shared_down"].T.reshape(2, P, D)])
    below = np.arange(4)[None, :] < np.arange(4)[:, None]
    return {
        "e1_w": c(np.concatenate([gates(both("gate")), gates(both("up")), down], axis=2)),
        "e1_gw": c(a["L1_ffn_gate_w"].T), "e1_bias": wide(a["L1_ffn_gate_bias"]),
        "e1_below": c(np.broadcast_to(below.astype(np.float32), (P, 4, 4))),
        "a1_wq": a["L1_attn_Wq"], "a1_wkv": w1, "a1_wo": a["L1_attn_Wo"],
        "a1_bqk": c(np.concatenate([b1[None, :P], a["L1_attn_bq"].reshape(8, P)]).T), "a1_bv": wide(b1[P:]),
        "a1_pos": c(pe.T),
        "mask": c(a["mask_BxS2_bf1"].view(np.uint8).reshape(B, P, KT).transpose(1, 0, 2)),
        "l1_lat_g": wide(a["L1_xattn_g_l"]), "l1_lat_b": wide(a["L1_xattn_b_l"]),
        "l1_ctx_g": wide(a["L1_xattn_g_x"]), "l1_ctx_b": wide(a["L1_xattn_b_x"]),
        "l1_out_g": wide(a["L1_xattn_g_o"]), "l1_out_b": wide(a["L1_xattn_b_o"]),
        "l1_wq": a["L1_xattn_Wq"], "l1_wkT": c(a["L1_xattn_Wkv"][:, :H * DH].T),
        "l1_wv": c(a["L1_xattn_Wkv"][:, H * DH:]), "l1_wo": a["L1_xattn_Wout"],
        "causal": np.where(key <= query, 0.0, MASKED).astype(np.float32),
        "heads": head.astype(np.float32),
        "a0_lqk": c(np.broadcast_to(np.stack([a[f"L0_attn_{k}"].reshape(H) for k in ("lq1", "lq2", "lk1", "lk2")]), (P, 4, H))),
        "a0_chan": c(np.stack([np.tile(a[f"L0_attn_{k}"], P // 32) for k in ("gn_w", "gn_b", "gamma")], axis=1)),
        "a0_wqk": c(np.stack([a[f"L0_attn_{k}"].T for k in ("Wq1", "Wq2", "Wk1", "Wk2")])),
        "a0_wv": c(a["L0_attn_Wv"].T), "a0_wc": c(a["L0_attn_Wc"].T),
        "f0_w1": c(a["L0_ffn_w1_w"].T), "f0_w2": c(a["L0_ffn_w2_w"].T),
        "f0_h1": c(a["L0_ffn_h1_w"].T), "f0_h2": c(a["L0_ffn_h2_w"].T), "f0_w3": c(a["L0_ffn_w3_w"].T),
        "f0_scales": c(np.stack([per(a[f"L0_ffn_{k}_s"]) for k in ("w1", "w2", "h1", "h2")], axis=1)),
        "f0_w3s": wide(a["L0_ffn_w3_s"]),
        "x": a["x"].reshape(T, D),
        "ctx": a["ctx_1024"],
        "l0_lat_g": wide(a["L0_xattn_ln_lat_g"]), "l0_lat_b": wide(a["L0_xattn_ln_lat_b"]),
        "l0_ctx_g": wide(a["L0_xattn_ln_ctx_g"]), "l0_ctx_b": wide(a["L0_xattn_ln_ctx_b"]),
        "l0_cos": keyed(a["L0_xattn_cos"]), "l0_sin": keyed(a["L0_xattn_sin"]),
        "l0_wq": a["L0_xattn_Wq"],
        "l0_wk": np.ascontiguousarray(a["L0_xattn_Wkv"][:, :H * DH]),
        "l0_wv": np.ascontiguousarray(a["L0_xattn_Wkv"][:, H * DH:]),
        "l0_wo": a["L0_xattn_Wo"], "l0_bo": wide(a["L0_xattn_bo"]),
    }


def kernel(**inputs):
    import concourse.bacc as bacc
    from concourse.bass_utils import run_bass_kernel_spmd

    arrays = {f"in_{k}": np.ascontiguousarray(v) for k, v in
              laid_out({k: np.asarray(v) for k, v in inputs.items()}).items()}
    nc = bacc.Bacc("TRN2", target_bir_lowering=False, num_devices=1)
    i = Names(**{k[3:]: nc.dram_tensor(k, v.shape, mybir.dt.from_np(v.dtype), kind="ExternalInput").ap()
                           for k, v in arrays.items()})
    o = nc.dram_tensor("out_0", (T, D), F32, kind="ExternalOutput").ap()
    build(nc, i, o)
    r = run_bass_kernel_spmd(nc, [arrays], core_ids=[0])
    return r.results[0]["out_0"].reshape(B, N, D)
```
